# Optimizing a Trainium2 kernel written in Bass

```python
import numpy as np
import jax
import jax.numpy as jnp

def _softmax(x, axis=-1):
    return jax.nn.softmax(x, axis=axis)

def _gelu(x):
    return jax.nn.gelu(x, approximate=True)

def _silu(x):
    return jax.nn.silu(x)

def _sigmoid(x):
    return jax.nn.sigmoid(x)

def _layernorm(x, axis=-1, eps=1e-05):
    m = jnp.mean(x, axis=axis, keepdims=True)
    v = jnp.var(x, axis=axis, keepdims=True)
    return (x - m) / jnp.sqrt(v + eps)

def _scatter_add(tgt, idx, src, axis=0):
    return tgt.at[idx].add(src)

def _segment_sum(src, seg, n):
    return jax.ops.segment_sum(src, seg, n)
kernel_name = 'mk_gnn_resnorm_d4_gnn_r8_1ff638'

def setup_inputs(seed: int=0):
    np.random.seed(seed)
    _w = jnp.asarray

    def _rec_inputs():
        import jax
        import jax.numpy as jnp
        _gk = jax.random.key(seed)
        x = -0.0003713 + 1 * jax.random.normal(jax.random.fold_in(_gk, 1), (6250, 256), jnp.float32)
        src = jax.random.randint(jax.random.fold_in(_gk, 2), (100000,), 0, 6250, jnp.int32)
        dst = jnp.minimum((6250 * jax.random.uniform(jax.random.fold_in(_gk, 3), (100000,)) ** 2.0).astype(jnp.int32), 49999)
        _o = jnp.argsort(dst, stable=True)
        src = src[_o]
        dst = dst[_o]
        return (x, src, dst)
    x, src, dst = _rec_inputs()

    def _L0_gnn_setup():
        import jax, jax.numpy as jnp
        import numpy as np
        N = 6250
        E = 100000
        F_IN = 256
        HID = 64
        HEADS = 4

        def _segment_softmax(logits, seg, num_segments):
            m = jax.ops.segment_max(logits, seg, num_segments=num_segments)
            e = jnp.exp(logits - m[seg])
            z = jax.ops.segment_sum(e, seg, num_segments=num_segments)
            return e / z[seg]

        def _gat_layer(x, src, dst, W, a_src, a_dst, b, num_nodes):
            H, C = a_src.shape
            h = (x @ W).reshape(num_nodes, H, C)
            al_s = jnp.einsum('nhc,hc->nh', h, a_src)
            al_d = jnp.einsum('nhc,hc->nh', h, a_dst)
            logits = jax.nn.leaky_relu(al_s[src] + al_d[dst], 0.2)
            alpha = _segment_softmax(logits, dst, num_nodes)
            msg = h[src] * alpha[:, :, None]
            out = jax.ops.segment_sum(msg, dst, num_segments=num_nodes)
            return out.reshape(num_nodes, H * C) + b
        key = jax.random.key(seed)
        ks = jax.random.split(key, 12)
        s = 0.05
        x = jax.random.normal(ks[0], (N, F_IN), dtype=jnp.float32)
        edge_index = jax.random.randint(ks[1], (2, E), 0, N, dtype=jnp.int64)
        W1 = jax.random.normal(ks[2], (F_IN, HEADS * HID), dtype=jnp.float32) * s
        att_src1 = jax.random.normal(ks[3], (HEADS, HID), dtype=jnp.float32) * s
        att_dst1 = jax.random.normal(ks[4], (HEADS, HID), dtype=jnp.float32) * s
        b1 = jnp.zeros((HEADS * HID,), dtype=jnp.float32)
        W2 = jax.random.normal(ks[5], (HEADS * HID, HID), dtype=jnp.float32) * s
        att_src2 = jax.random.normal(ks[6], (1, HID), dtype=jnp.float32) * s
        att_dst2 = jax.random.normal(ks[7], (1, HID), dtype=jnp.float32) * s
        b2 = jnp.zeros((HID,), dtype=jnp.float32)
        Wf = jax.random.normal(ks[8], (HID, F_IN), dtype=jnp.float32) * s
        bf = jnp.zeros((F_IN,), dtype=jnp.float32)
        return {'x': x, 'edge_index': edge_index, 'W1': W1, 'att_src1': att_src1, 'att_dst1': att_dst1, 'b1': b1, 'W2': W2, 'att_src2': att_src2, 'att_dst2': att_dst2, 'b2': b2, 'Wf': Wf, 'bf': bf}
    _L0_gnn_all = _L0_gnn_setup()
    _L0_gnn_in = {k: v for k, v in _L0_gnn_all.items() if k in ('W1', 'att_src1', 'att_dst1', 'b1', 'W2', 'att_src2', 'att_dst2', 'b2', 'Wf', 'bf')}
    del _L0_gnn_all

    def _L1_gnn_setup():
        import jax, jax.numpy as jnp
        import numpy as np
        ALPHA = 0.2

        def _gat_head(node_feats, W, a, src, dst, N):
            h = node_feats @ W
            C = W.shape[1]
            a_l, a_r = (a[0, :C], a[0, C:])
            s_l = h @ a_l
            s_r = h @ a_r
            logits = s_l[src] + s_r[dst]
            e = jnp.exp(-jax.nn.leaky_relu(logits, negative_slope=ALPHA))
            row_sum = jax.ops.segment_sum(e, src, num_segments=N)
            h_prime = jax.ops.segment_sum(e[:, None] * h[dst], src, num_segments=N)
            return jax.nn.elu(h_prime / row_sum[:, None])
        key = jax.random.key(seed)
        k1, k2, k3, k4, k5, k6 = jax.random.split(key, 6)
        N, E, c_in, c_head = (6250, 100000, 256, 128)
        node_feats = jax.random.normal(k1, (N, c_in), dtype=jnp.float32)
        edge_index = jax.random.randint(k2, (2, E), 0, N, dtype=jnp.int64)
        std_W = 1.414 * np.sqrt(2.0 / (c_in + c_head))
        std_a = 1.414 * np.sqrt(2.0 / (1 + 2 * c_head))
        W1 = jax.random.normal(k3, (c_in, c_head), dtype=jnp.float32) * std_W
        a1 = jax.random.normal(k4, (1, 2 * c_head), dtype=jnp.float32) * std_a
        W2 = jax.random.normal(k5, (c_in, c_head), dtype=jnp.float32) * std_W
        a2 = jax.random.normal(k6, (1, 2 * c_head), dtype=jnp.float32) * std_a
        return {'node_feats': node_feats, 'W1': W1, 'a1': a1, 'W2': W2, 'a2': a2, 'edge_index': edge_index, 'N': N}
    _L1_gnn_all = _L1_gnn_setup()
    _L1_gnn_in = {k: v for k, v in _L1_gnn_all.items() if k in ('W1', 'a1', 'W2', 'a2')}
    del _L1_gnn_all

    def _L2_gnn_setup():
        import jax, jax.numpy as jnp
        import numpy as np
        N = 6250
        E = 100000
        HIDDEN = 256
        HEADS = 8
        HEAD_DIM = HIDDEN // HEADS

        def _linear_params(key, fan_in, fan_out):
            k1, k2 = jax.random.split(key)
            s = 1.0 / np.sqrt(fan_in)
            W = jax.random.uniform(k1, (fan_in, fan_out), jnp.float32, -s, s)
            b = jax.random.uniform(k2, (fan_out,), jnp.float32, -s, s)
            return (W, b)
        key = jax.random.key(seed)
        ks = jax.random.split(key, 7)
        h = jax.random.normal(ks[0], (N, HIDDEN), jnp.float32)
        row = jnp.sort(jax.random.randint(ks[1], (E,), 0, N))
        col = jax.random.randint(ks[2], (E,), 0, N)
        Wq, bq = _linear_params(ks[3], HIDDEN, HIDDEN)
        Wk, bk = _linear_params(ks[4], HIDDEN, HIDDEN)
        Wv, bv = _linear_params(ks[5], HIDDEN, HIDDEN)
        Wo, bo = _linear_params(ks[6], HIDDEN, HIDDEN)
        return dict(h=h, row=row, col=col, Wq=Wq, bq=bq, Wk=Wk, bk=bk, Wv=Wv, bv=bv, Wo=Wo, bo=bo)
    _L2_gnn_all = _L2_gnn_setup()
    _L2_gnn_in = {k: v for k, v in _L2_gnn_all.items() if k in ('Wq', 'bq', 'Wk', 'bk', 'Wv', 'bv', 'Wo', 'bo')}
    del _L2_gnn_all

    def _L3_gnn_setup():
        import jax, jax.numpy as jnp
        import numpy as np
        N_NODES = 12500
        BN_EPS = 1e-05

        def gcn_conv(x, src, dst, W, b, n):
            h = x @ W
            loop = jnp.arange(n, dtype=src.dtype)
            s = jnp.concatenate([src, loop])
            d = jnp.concatenate([dst, loop])
            deg = jax.ops.segment_sum(jnp.ones(s.shape, h.dtype), d, num_segments=n)
            dinv = jnp.where(deg > 0, jax.lax.rsqrt(jnp.maximum(deg, 1.0)), 0.0)
            norm = dinv[s] * dinv[d]
            msg = h[s] * norm[:, None]
            out = jax.ops.segment_sum(msg, d, num_segments=n)
            return out + b

        def batch_norm(x, gamma, beta):
            mean = jnp.mean(x, axis=0)
            var = jnp.mean(jnp.square(x - mean), axis=0)
            return (x - mean) * jax.lax.rsqrt(var + BN_EPS) * gamma + beta
        key = jax.random.key(seed)
        ks = jax.random.split(key, 10)
        d0, d1, d2 = (256, 128, 64)
        d_cat = d0 + d1 + d2
        inp = {'node_features': jax.random.normal(ks[0], (N_NODES, d0), jnp.float32), 'edge_idx': jax.random.randint(ks[1], (2, 200000), 0, N_NODES, jnp.int64), 'W1': jax.random.normal(ks[2], (d0, d1), jnp.float32) * (1.0 / np.sqrt(d0)), 'b1': jnp.zeros((d1,), jnp.float32), 'g1': jnp.ones((d1,), jnp.float32), 'be1': jnp.zeros((d1,), jnp.float32), 'W2': jax.random.normal(ks[3], (d1, d2), jnp.float32) * (1.0 / np.sqrt(d1)), 'b2': jnp.zeros((d2,), jnp.float32), 'g2': jnp.ones((d2,), jnp.float32), 'be2': jnp.zeros((d2,), jnp.float32), 'Wfc': jax.random.normal(ks[4], (d_cat, d0), jnp.float32) * (1.0 / np.sqrt(d_cat)), 'bfc': jnp.zeros((d0,), jnp.float32)}
        return inp
    _L3_gnn_all = _L3_gnn_setup()
    _L3_gnn_in = {k: v for k, v in _L3_gnn_all.items() if k in ('W1', 'b1', 'g1', 'be1', 'W2', 'b2', 'g2', 'be2', 'Wfc', 'bfc')}
    del _L3_gnn_all
    return {'x': x, 'src': src, 'dst': dst, 'L0_gnn_W1': _L0_gnn_in['W1'], 'L0_gnn_att_src1': _L0_gnn_in['att_src1'], 'L0_gnn_att_dst1': _L0_gnn_in['att_dst1'], 'L0_gnn_b1': _L0_gnn_in['b1'], 'L0_gnn_W2': _L0_gnn_in['W2'], 'L0_gnn_att_src2': _L0_gnn_in['att_src2'], 'L0_gnn_att_dst2': _L0_gnn_in['att_dst2'], 'L0_gnn_b2': _L0_gnn_in['b2'], 'L0_gnn_Wf': _L0_gnn_in['Wf'], 'L0_gnn_bf': _L0_gnn_in['bf'], 'L1_gnn_W1': _L1_gnn_in['W1'], 'L1_gnn_a1': _L1_gnn_in['a1'], 'L1_gnn_W2': _L1_gnn_in['W2'], 'L1_gnn_a2': _L1_gnn_in['a2'], 'L2_gnn_Wq': _L2_gnn_in['Wq'], 'L2_gnn_bq': _L2_gnn_in['bq'], 'L2_gnn_Wk': _L2_gnn_in['Wk'], 'L2_gnn_bk': _L2_gnn_in['bk'], 'L2_gnn_Wv': _L2_gnn_in['Wv'], 'L2_gnn_bv': _L2_gnn_in['bv'], 'L2_gnn_Wo': _L2_gnn_in['Wo'], 'L2_gnn_bo': _L2_gnn_in['bo'], 'L3_gnn_W1': _L3_gnn_in['W1'], 'L3_gnn_b1': _L3_gnn_in['b1'], 'L3_gnn_g1': _L3_gnn_in['g1'], 'L3_gnn_be1': _L3_gnn_in['be1'], 'L3_gnn_W2': _L3_gnn_in['W2'], 'L3_gnn_b2': _L3_gnn_in['b2'], 'L3_gnn_g2': _L3_gnn_in['g2'], 'L3_gnn_be2': _L3_gnn_in['be2'], 'L3_gnn_Wfc': _L3_gnn_in['Wfc'], 'L3_gnn_bfc': _L3_gnn_in['bfc']}

def reference(x, src, dst, L0_gnn_W1, L0_gnn_att_src1, L0_gnn_att_dst1, L0_gnn_b1, L0_gnn_W2, L0_gnn_att_src2, L0_gnn_att_dst2, L0_gnn_b2, L0_gnn_Wf, L0_gnn_bf, L1_gnn_W1, L1_gnn_a1, L1_gnn_W2, L1_gnn_a2, L2_gnn_Wq, L2_gnn_bq, L2_gnn_Wk, L2_gnn_bk, L2_gnn_Wv, L2_gnn_bv, L2_gnn_Wo, L2_gnn_bo, L3_gnn_W1, L3_gnn_b1, L3_gnn_g1, L3_gnn_be1, L3_gnn_W2, L3_gnn_b2, L3_gnn_g2, L3_gnn_be2, L3_gnn_Wfc, L3_gnn_bfc):
    import jax
    import jax.numpy as jnp

    def _L0_gnn_ref(x, edge_index, W1, att_src1, att_dst1, b1, W2, att_src2, att_dst2, b2, Wf, bf):
        import jax, jax.numpy as jnp
        import numpy as np
        N = 6250
        E = 100000
        F_IN = 256
        HID = 64
        HEADS = 4

        def _segment_softmax(logits, seg, num_segments):
            m = jax.ops.segment_max(logits, seg, num_segments=num_segments)
            e = jnp.exp(logits - m[seg])
            z = jax.ops.segment_sum(e, seg, num_segments=num_segments)
            return e / z[seg]

        def _gat_layer(x, src, dst, W, a_src, a_dst, b, num_nodes):
            H, C = a_src.shape
            h = (x @ W).reshape(num_nodes, H, C)
            al_s = jnp.einsum('nhc,hc->nh', h, a_src)
            al_d = jnp.einsum('nhc,hc->nh', h, a_dst)
            logits = jax.nn.leaky_relu(al_s[src] + al_d[dst], 0.2)
            alpha = _segment_softmax(logits, dst, num_nodes)
            msg = h[src] * alpha[:, :, None]
            out = jax.ops.segment_sum(msg, dst, num_segments=num_nodes)
            return out.reshape(num_nodes, H * C) + b
        num_nodes = x.shape[0]
        loop = jnp.arange(num_nodes, dtype=edge_index.dtype)
        src = jnp.concatenate([edge_index[0], loop])
        dst = jnp.concatenate([edge_index[1], loop])
        h = jax.nn.relu(_gat_layer(x, src, dst, W1, att_src1, att_dst1, b1, num_nodes))
        h = _gat_layer(h, src, dst, W2, att_src2, att_dst2, b2, num_nodes)
        return h @ Wf + bf

    def _L1_gnn_ref(node_feats, W1, a1, W2, a2, edge_index, N):
        import jax, jax.numpy as jnp
        import numpy as np
        ALPHA = 0.2

        def _gat_head(node_feats, W, a, src, dst, N):
            h = node_feats @ W
            C = W.shape[1]
            a_l, a_r = (a[0, :C], a[0, C:])
            s_l = h @ a_l
            s_r = h @ a_r
            logits = s_l[src] + s_r[dst]
            e = jnp.exp(-jax.nn.leaky_relu(logits, negative_slope=ALPHA))
            row_sum = jax.ops.segment_sum(e, src, num_segments=N)
            h_prime = jax.ops.segment_sum(e[:, None] * h[dst], src, num_segments=N)
            return jax.nn.elu(h_prime / row_sum[:, None])
        src, dst = (edge_index[0], edge_index[1])
        out1 = _gat_head(node_feats, W1, a1, src, dst, N)
        out2 = _gat_head(node_feats, W2, a2, src, dst, N)
        return jnp.concatenate([out1, out2], axis=1)

    def _L2_gnn_ref(h, row, col, Wq, bq, Wk, bk, Wv, bv, Wo, bo):
        import jax, jax.numpy as jnp
        import numpy as np
        N = 6250
        E = 100000
        HIDDEN = 256
        HEADS = 8
        HEAD_DIM = HIDDEN // HEADS

        def _linear_params(key, fan_in, fan_out):
            k1, k2 = jax.random.split(key)
            s = 1.0 / np.sqrt(fan_in)
            W = jax.random.uniform(k1, (fan_in, fan_out), jnp.float32, -s, s)
            b = jax.random.uniform(k2, (fan_out,), jnp.float32, -s, s)
            return (W, b)
        n = h.shape[0]
        scaling = HEAD_DIM ** (-0.5)
        q = (h @ Wq + bq).reshape(n, HEADS, HEAD_DIM) * scaling
        k = (h @ Wk + bk).reshape(n, HEADS, HEAD_DIM)
        v = (h @ Wv + bv).reshape(n, HEADS, HEAD_DIM)
        s = jnp.einsum('ehd,ehd->eh', q[row], k[col])
        m = jax.ops.segment_max(s, row, num_segments=n)
        p = jnp.exp(s - m[row])
        denom = jax.ops.segment_sum(p, row, num_segments=n)
        attn = p / denom[row]
        out = jax.ops.segment_sum(attn[:, :, None] * v[col], row, num_segments=n)
        return out.reshape(n, HIDDEN) @ Wo + bo

    def _L3_gnn_ref(node_features, edge_idx, W1, b1, g1, be1, W2, b2, g2, be2, Wfc, bfc):
        import jax, jax.numpy as jnp
        import numpy as np
        N_NODES = 12500
        BN_EPS = 1e-05

        def gcn_conv(x, src, dst, W, b, n):
            h = x @ W
            loop = jnp.arange(n, dtype=src.dtype)
            s = jnp.concatenate([src, loop])
            d = jnp.concatenate([dst, loop])
            deg = jax.ops.segment_sum(jnp.ones(s.shape, h.dtype), d, num_segments=n)
            dinv = jnp.where(deg > 0, jax.lax.rsqrt(jnp.maximum(deg, 1.0)), 0.0)
            norm = dinv[s] * dinv[d]
            msg = h[s] * norm[:, None]
            out = jax.ops.segment_sum(msg, d, num_segments=n)
            return out + b

        def batch_norm(x, gamma, beta):
            mean = jnp.mean(x, axis=0)
            var = jnp.mean(jnp.square(x - mean), axis=0)
            return (x - mean) * jax.lax.rsqrt(var + BN_EPS) * gamma + beta
        n = node_features.shape[0]
        src, dst = (edge_idx[0], edge_idx[1])
        feats = [node_features]
        x = node_features
        x = gcn_conv(x, src, dst, W1, b1, n)
        x = jax.nn.relu(batch_norm(x, g1, be1))
        feats.append(x)
        x = gcn_conv(x, src, dst, W2, b2, n)
        x = jax.nn.relu(batch_norm(x, g2, be2))
        feats.append(x)
        cat = jnp.concatenate(feats, axis=1)
        return jax.nn.relu(cat @ Wfc + bfc)
    edge_index = jnp.stack([src, dst])
    x = _layernorm(x + _L0_gnn_ref(x, edge_index, L0_gnn_W1, L0_gnn_att_src1, L0_gnn_att_dst1, L0_gnn_b1, L0_gnn_W2, L0_gnn_att_src2, L0_gnn_att_dst2, L0_gnn_b2, L0_gnn_Wf, L0_gnn_bf), axis=-1)
    x = _layernorm(x + _L1_gnn_ref(x, L1_gnn_W1, L1_gnn_a1, L1_gnn_W2, L1_gnn_a2, edge_index, 6250), axis=-1)
    x = _layernorm(x + _L2_gnn_ref(x, src, dst, L2_gnn_Wq, L2_gnn_bq, L2_gnn_Wk, L2_gnn_bk, L2_gnn_Wv, L2_gnn_bv, L2_gnn_Wo, L2_gnn_bo), axis=-1)
    x = _layernorm(x + _L3_gnn_ref(x, edge_index, L3_gnn_W1, L3_gnn_b1, L3_gnn_g1, L3_gnn_be1, L3_gnn_W2, L3_gnn_b2, L3_gnn_g2, L3_gnn_be2, L3_gnn_Wfc, L3_gnn_bfc), axis=-1)
    return x

_drawn_inputs = setup_inputs


def setup_inputs(seed=0):
    import zlib

    import numpy as np

    out = dict(_drawn_inputs(seed))
    spreads = {'L0_gnn_b1': (0.0, 0.1),
     'L0_gnn_b2': (0.0, 0.1),
     'L0_gnn_bf': (0.0, 0.1),
     'L3_gnn_b1': (0.0, 2.0),
     'L3_gnn_g1': (1.0, 0.2),
     'L3_gnn_be1': (0.0, 0.1),
     'L3_gnn_b2': (0.0, 2.0),
     'L3_gnn_g2': (1.0, 0.2),
     'L3_gnn_be2': (0.0, 0.558),
     'L3_gnn_bfc': (0.0, 0.1)}
    factors = {'L0_gnn_W1': 3.309,
     'L0_gnn_att_src1': 8.0,
     'L0_gnn_att_dst1': 8.0,
     'L0_gnn_att_src2': 8.0,
     'L0_gnn_att_dst2': 8.0,
     'L2_gnn_bq': 35.657,
     'L2_gnn_bk': 64.0,
     'L2_gnn_bv': 2.839}
    for name, (base, spread) in spreads.items():
        noise = np.random.default_rng([zlib.crc32(name.encode()), seed]).standard_normal(out[name].shape)
        drawn = base * np.exp(spread * noise) if base else spread * noise
        out[name] = jnp.asarray(drawn.astype(out[name].dtype))
    for name, factor in factors.items():
        out[name] = (out[name] * factor).astype(out[name].dtype)
    return out
```

```python
import concourse.bass as bass
from concourse import mybir
from concourse.alu_op_type import AluOpType as ALU
from contextlib import ExitStack

F32 = mybir.dt.float32
BF16 = mybir.dt.bfloat16
I32 = mybir.dt.int32
ACT = mybir.ActivationFunctionType
AX = mybir.AxisListType

P = 128
N = 6250
E = 100000
D = 256
WIN = -(-N // P)
NW = WIN + 1
NPAD = NW * P
PAD_ROW = NPAD - 1
GE = 2 * P
UN = 8
NG = -(-((E + WIN * (GE - 1)) // GE) // UN) * UN
NSLOT = 2 * NG
EP, EC = 125, 800
SB = 8
BIG = 65536.0
CLIP = 30000.0
EPS = 1e-5
LAST = WIN - 1
VALID = N - LAST * P


class Group:

    def __init__(self, i, k):
        self.i, self.k = i, k

    def plus(self, n):
        return self.i * UN + (self.k + n)

    def slot(self, n):
        return self.k % n

    def turn(self, n):
        return self.i * (UN // n) + self.k // n

    def exists(self):
        return not isinstance(self.i, int) or 0 <= self.i * UN + self.k < NG


def wait(eng, sem, count):
    if isinstance(count, int) and count <= 0:
        return
    eng.wait_ge(sem, count)


class Link:

    def __init__(self, eng, sem):
        self.eng, self.sem, self.n = eng, sem, 0

    def __call__(self, ins):
        self.n += 1
        ins.then_inc(self.sem, 1)
        self.eng.wait_ge(self.sem, self.n)


def apart(eng, sem, count, passed):
    wait(eng, sem, count)
    eng.sem_inc(passed, 1)


def bc(ap, shape):
    return ap.to_broadcast(shape)


class Memory:

    def __init__(self, nc, stack, stage):
        self.nc, self.stack, self.stage = nc, stack, stage
        self.sems = []
        stack.callback(self.clear)

    def clear(self):
        if self.sems:
            self.nc.clear_and_free_semaphores(self.sems)
            self.nc.all_engine_barrier()

    def sb(self, name, shape, dt=F32):
        return self.stack.enter_context(self.nc.sbuf_tensor(f"{self.stage}_{name}", shape, dt))

    def ps(self, name, shape, dt=F32):
        return self.stack.enter_context(self.nc.psum_tensor(f"{self.stage}_{name}", shape, dt))

    def sem(self, name):
        sem = self.nc.alloc_semaphore(f"{self.stage}_{name}")
        self.sems.append(sem)
        return sem



def constants(nc, m, c):
    c.ident = m.sb("ident", [P, P])
    c.ident16 = m.sb("ident16", [P, P], BF16)
    c.big16 = m.sb("big16", [P, 4, P], BF16)
    c.lane = m.sb("lane", [P, P])
    c.lanei = m.sb("lanei", [P, P], I32)
    c.tri = m.sb("tri", [P, P])
    c.ones = m.sb("ones", [P, P])
    c.zero = m.sb("zero", [P, 1])
    c.minus_half = m.sb("minus_half", [P, 1])
    c.valid = m.sb("valid", [P, 2])
    s_made = m.sem("made")
    with nc.Block() as block:
        @block.gpsimd
        def _(pool):
            link = Link(pool, s_made)
            link(pool.memset(c.ident[:, :], 0.0))
            link(pool.affine_select(out=c.ident[:, :], in_=c.ident[:, :], compare_op=ALU.not_equal, fill=1.0,
                                    base=0, pattern=[[-1, P]], channel_multiplier=1))
            link(pool.tensor_copy(c.ident16[:, :], c.ident[:, :]))
            for h in range(4):
                link(pool.tensor_scalar(c.big16[:, h, :], c.ident[:, :], BIG, None, ALU.mult))
            link(pool.memset(c.ones[:, :], 1.0))
            link(pool.memset(c.zero[:, :], 0.0))
            link(pool.memset(c.minus_half[:, :], -0.5))
            link(pool.affine_select(out=c.tri[:, :], in_=c.ones[:, :], compare_op=ALU.is_gt, fill=0.0,
                                    base=0, pattern=[[1, P]], channel_multiplier=-1))
            link(pool.iota(c.lanei[:, :], pattern=[[1, P]], base=0, channel_multiplier=0))
            link(pool.tensor_copy(c.lane[:, :], c.lanei[:, :]))
            link(pool.memset(c.valid[:, :], 0.0))
            link(pool.affine_select(out=c.valid[:, 0:1], in_=c.ones[:, 0:1], compare_op=ALU.is_gt, fill=0.0,
                                    base=VALID, pattern=[[0, 1]], channel_multiplier=-1))



def sort_edges(nc, c, stage, key_d, other_d, records_d, keep):
    with ExitStack() as stack:
        m = Memory(nc, stack, stage)
        key = m.sb("key", [EP, EC], I32)
        other = m.sb("other", [EP, EC], I32)
        winf = m.sb("winf", [EP, EC])
        hit = m.sb("hit", [EP, EC])
        run = m.sb("run", [EP, EC])
        rank = m.sb("rank", [EP, EC])
        post = m.sb("post", [EP, EC, 3], I32)
        staged = m.sb("staged", [EP, 2, SB, 3], I32)
        empty = m.sb("empty", [P, NSLOT, 2], I32)
        back = m.sb("back", [P, NSLOT, 2], I32)
        total = m.sb("total", [P, WIN])
        offset = m.sb("offset", [P, WIN])
        groups = m.sb("groups", [P, WIN])
        groupsi = m.sb("groupsi", [P, WIN], I32)
        ends = m.sb("ends", [P, WIN])
        numberi = m.sb("numberi", [P, NG], I32)
        number = m.sb("number", [P, NG])
        windowf = m.sb("windowf", [P, NG])
        ps = m.ps("sums", [P, 2, 256])
        s_in, s_fill, s_back = m.sem("in"), m.sem("fill"), m.sem("back")
        s_pool, s_dve, s_total, s_summed = m.sem("pool"), m.sem("dve"), m.sem("total"), m.sem("summed")
        s_staged, s_scattered = m.sem("staged"), [m.sem(f"scattered{h}") for h in range(2)]
        s_loop, s_base, s_passed = m.sem("loop"), m.sem("base"), m.sem("passed")
        TURNS = EC // (2 * SB)
        A, B = 5, 2

        with nc.Block() as block:
            @block.sync
            def _(sp):
                sp.dma_start(key[:, :], key_d.rearrange("(p c) -> p c", p=EP)).then_inc(s_in, 16)
                sp.dma_start(other[:, :], other_d.rearrange("(p c) -> p c", p=EP)).then_inc(s_in, 16)
                sp.wait_ge(s_pool, 3)
                sp.dma_start(records_d, empty[:, :, :]).then_inc(s_fill, 16)
                for h in range(2):
                    sp.wait_ge(s_scattered[h], 16 * SB * TURNS)
                sp.dma_start(back[:, :, :], records_d).then_inc(s_back, 16)

            @block.gpsimd
            def _(pool):
                pool.memset(empty[:, :, 0:1], PAD_ROW).then_inc(s_pool, 1)
                pool.memset(empty[:, :, 1:2], -1).then_inc(s_pool, 1)
                pool.iota(numberi[:, :], pattern=[[1, NG]], base=0, channel_multiplier=0).then_inc(s_pool, 1)
                pool.wait_ge(s_fill, 16)
                with pool.Fori(0, TURNS) as i:
                    for h in range(2):
                        apart(pool, s_staged, i * 2 + (h + 1), s_passed)
                        for j in range(SB):
                            pool.indirect_dma_start(
                                out=records_d.rearrange("p s r -> (p s) r"),
                                out_offset=bass.IndirectOffsetOnAxis(ap=staged[:, h, j, 0:1], axis=0),
                                in_=staged[:, h, j, 1:3], in_offset=None).then_inc(s_scattered[h], 16)

            @block.tensor
            def _(pe):
                pe.wait_ge(s_total, 1)
                pe.matmul(ps[0:EP, 0, 0:WIN], c.tri[0:EP, 0:EP], total[0:EP, :], start=True, stop=True)
                pe.matmul(ps[:, 1, 0:WIN], c.ones[0:EP, :], total[0:EP, :], start=True, stop=True).then_inc(s_summed, 1)

            @block.vector
            def _(dve):
                link = Link(dve, s_dve)
                dve.wait_ge(s_in, 32)
                link(dve.tensor_single_scalar(post[:, :, 0], key[:, :], 7, ALU.arith_shift_right))
                link(dve.tensor_copy(winf[:, :], post[:, :, 0]))
                link(dve.memset(rank[:, :], 0.0))
                with dve.Fori(0, WIN) as w:
                    wcol = c.lane[0:EP, bass.ds(w, 1)]
                    dve.tensor_scalar(hit[:, :], winf[:, :], wcol, None, ALU.is_equal).then_inc(s_loop, 1)
                    dve.wait_ge(s_loop, w * A + 1)
                    dve.tensor_tensor_scan(run[:, :], hit[:, :], bc(c.zero[0:EP, :], [EP, EC]), 0.0, ALU.add, ALU.add).then_inc(s_loop, 1)
                    dve.wait_ge(s_loop, w * A + 2)
                    dve.tensor_copy(total[0:EP, bass.ds(w, 1)], run[:, EC - 1:EC]).then_inc(s_loop, 1)
                    dve.tensor_tensor(hit[:, :], hit[:, :], run[:, :], ALU.mult).then_inc(s_loop, 1)
                    dve.wait_ge(s_loop, w * A + 4)
                    dve.tensor_tensor(rank[:, :], rank[:, :], hit[:, :], ALU.add).then_inc(s_loop, 1)
                    dve.wait_ge(s_loop, w * A + 5)
                dve.memset(windowf[:, :], 0.0).then_inc(s_total, 1)
                dve.wait_ge(s_summed, 1)
                link(dve.tensor_scalar(groups[:, :], ps[:, 1, 0:WIN], float(GE - 1), None, ALU.add))
                link(dve.tensor_copy(groupsi[:, :], groups[:, :]))
                link(dve.tensor_single_scalar(groupsi[:, :], groupsi[:, :], GE.bit_length() - 1, ALU.arith_shift_right))
                link(dve.tensor_copy(groups[:, :], groupsi[:, :]))
                link(dve.tensor_tensor_scan(ends[:, :], groups[:, :], bc(c.zero[:, :], [P, WIN]), 0.0, ALU.add, ALU.add))
                link(dve.tensor_tensor(offset[:, :], ends[:, :], groups[:, :], ALU.subtract))
                link(dve.tensor_scalar(offset[:, :], offset[:, :], float(GE), -1.0, ALU.mult, ALU.add))
                link(dve.tensor_tensor(offset[0:EP, :], offset[0:EP, :], ps[0:EP, 0, 0:WIN], ALU.add))
                with dve.Fori(0, WIN) as w:
                    dve.tensor_scalar(hit[:, :], winf[:, :], c.lane[0:EP, bass.ds(w, 1)], offset[0:EP, bass.ds(w, 1)],
                                      ALU.is_equal, ALU.mult).then_inc(s_base, 1)
                    dve.wait_ge(s_base, w * B + 1)
                    dve.tensor_tensor(rank[:, :], rank[:, :], hit[:, :], ALU.add).then_inc(s_base, 1)
                    dve.wait_ge(s_base, w * B + 2)
                link(dve.tensor_copy(post[:, :, 1], rank[:, :]))
                link(dve.tensor_single_scalar(post[:, :, 2], post[:, :, 1], 7, ALU.arith_shift_right))
                link(dve.tensor_copy(run[:, :], post[:, :, 2]))
                link(dve.scalar_tensor_tensor(hit[:, :], run[:, :], -float(P), rank[:, :], ALU.mult, ALU.add))
                link(dve.scalar_tensor_tensor(hit[:, :], hit[:, :], float(NSLOT), run[:, :], ALU.mult, ALU.add))
                link(dve.tensor_copy(post[:, :, 0], hit[:, :]))
                link(dve.tensor_copy(post[:, :, 1], other[:, :]))
                link(dve.tensor_copy(post[:, :, 2], key[:, :]))

                def stage(h, col, count):
                    dve.tensor_copy(staged[:, h, :, :], post[:, col, :]).then_inc(s_staged, 1)

                for h in range(2):
                    dve.tensor_copy(staged[:, h, :, :], post[:, h * SB:(h + 1) * SB, :]).then_inc(s_staged, 1)
                dve.wait_ge(s_pool, 3)
                link(dve.tensor_copy(number[:, :], numberi[:, :]))
                for w in range(WIN):
                    link(dve.scalar_tensor_tensor(windowf[:, :], number[:, :], ends[:, w:w + 1], windowf[:, :], ALU.is_ge, ALU.add))
                link(dve.tensor_copy(keep.window[:, :], windowf[:, :]))
                with dve.Fori(1, TURNS) as i:
                    for h in range(2):
                        dve.wait_ge(s_scattered[h], i * (16 * SB))
                        dve.tensor_copy(staged[:, h, :, :], post[:, bass.ds(i * (2 * SB) + h * SB, SB), :]).then_inc(s_staged, 1)
                dve.wait_ge(s_back, 16)
                link(dve.memset(keep.row[:, NSLOT:], PAD_ROW))
                link(dve.tensor_copy(keep.row[:, 0:NSLOT], back[:, :, 0]))
                link(dve.tensor_copy(keep.place[:, :], back[:, :, 1]))
                link(dve.scalar_tensor_tensor(
                    keep.place[:, :].rearrange("p (g j) -> p g j", j=2), bc(windowf[:, :].rearrange("p (g j) -> p g j", j=1), [P, NG, 2]),
                    -float(P), keep.place[:, :].rearrange("p (g j) -> p g j", j=2), ALU.mult, ALU.add))



def linear(nc, c, stage, sources, weights, bias, width, drain_v, drain_a, table=None, table_width=0, table_by=""):
    with ExitStack() as stack:
        m = Memory(nc, stack, stage)
        K = len(sources)
        turned = m.sb("turned", [P, 2, K, P])
        fetched = m.sb("fetched", [P, 2, K, P])
        tile = m.sb("tile", [P, 2, max(table_width, 1)])
        ps_t = [m.ps(f"ps_t{b}", [P, 512]) for b in range(2)]
        banks = -(-width // 512)
        ps_o = [m.ps(f"ps_o{b}", [P, banks * 512]) for b in range(2)]
        s_fetched, s_t, s_turned, s_product, s_v, s_a, s_passed = (m.sem(x) for x in ("fetched", "t", "turned", "product", "v", "a", "passed"))
        s_stored = [m.sem(f"stored{b}") for b in range(2)]
        cuts = [(a, min(a + 512, width)) for a in range(0, width, 512)]

        with nc.Block() as block:
            @block.tensor
            def _(pe):
                def turn(w, b):
                    wait(pe, s_turned, w - 1)
                    apart(pe, s_fetched, w + 1, s_passed)
                    for k, (x, c0, n) in enumerate(sources):
                        last = pe.transpose(ps_t[b][0:n, k * P:(k + 1) * P], fetched[:, b, k, 0:n], c.ident[:, :])
                    last.then_inc(s_t, 1)

                def product(w, b):
                    pe.wait_ge(s_turned, w + 1)
                    wait(pe, s_v, w - 1)
                    if drain_a is not None:
                        wait(pe, s_a, w - 1)
                    for a0, a1 in cuts:
                        for k, (x, c0, n) in enumerate(sources):
                            last = pe.matmul(ps_o[b][:, a0:a1], turned[0:n, b, k, :], weights[k][0:n, a0:a1],
                                             start=k == 0, stop=k == K - 1 and bias is None)
                        if bias is not None:
                            last = pe.matmul(ps_o[b][:, a0:a1], c.ones[0:1, :], bias[0:1, a0:a1], start=False, stop=True)
                    last.then_inc(s_product, 1)

                turn(0, 0)
                turn(1, 1)
                product(0, 0)
                turn(2, 0)
                product(1, 1)
                with pe.Fori(1, NW // 2 - 1) as i:
                    turn(i * 2 + 1, 1)
                    product(i * 2, 0)
                    turn(i * 2 + 2, 0)
                    product(i * 2 + 1, 1)
                turn(NW - 1, 1)
                product(NW - 2, 0)
                product(NW - 1, 1)

            @block.scalar
            def _(act):
                def copy(w, b):
                    act.wait_ge(s_t, w + 1)
                    wait(act, s_product, w - 1)
                    for k, (x, c0, n) in enumerate(sources):
                        last = act.activation(turned[0:n, b, k, :], ps_t[b][0:n, k * P:(k + 1) * P], ACT.Copy)
                    last.then_inc(s_turned, 1)

                def drain(w, b):
                    if drain_a is None:
                        return
                    act.wait_ge(s_product, w + 1)
                    if "a" in table_by:
                        wait(act, s_stored[b], (w // 2) * 16 if isinstance(w, int) else (w - b) * 8)
                    drain_a(act, ps_o[b], w, tile[:, b, :]).then_inc(s_a, 1)

                copy(0, 0)
                copy(1, 1)
                drain(0, 0)
                copy(2, 0)
                drain(1, 1)
                with act.Fori(1, NW // 2 - 1) as i:
                    copy(i * 2 + 1, 1)
                    drain(i * 2, 0)
                    copy(i * 2 + 2, 0)
                    drain(i * 2 + 1, 1)
                copy(NW - 1, 1)
                drain(NW - 2, 0)
                drain(NW - 1, 1)

            @block.vector
            def _(dve):
                def drain(w, b):
                    dve.wait_ge(s_a if drain_a is not None else s_product, w + 1)
                    if "v" in table_by:
                        wait(dve, s_stored[b], (w // 2) * 16 if isinstance(w, int) else (w - b) * 8)
                    drain_v(dve, ps_o[b], w, tile[:, b, :]).then_inc(s_v, 1)

                def fetch(w, b):
                    wait(dve, s_t, w - 1)
                    for k, (x, c0, n) in enumerate(sources):
                        last = dve.tensor_copy(fetched[:, b, k, 0:n], x[:, bass.ds(w, 1), c0:c0 + n].rearrange("p a n -> p (a n)"))
                    last.then_inc(s_fetched, 1)

                fetch(0, 0)
                fetch(1, 1)
                fetch(2, 0)
                drain(0, 0)
                fetch(3, 1)
                drain(1, 1)
                with dve.Fori(1, NW // 2 - 1) as i:
                    fetch(i * 2 + 2, 0)
                    drain(i * 2, 0)
                    fetch(i * 2 + 3, 1)
                    drain(i * 2 + 1, 1)
                drain(NW - 2, 0)
                drain(NW - 1, 1)

            if table is not None:
                rows = table.rearrange("(w p) n -> w p n", p=P)

                @block.sync
                def _(sp):
                    def store(w, b):
                        if "v" in table_by:
                            sp.wait_ge(s_v, w + 1)
                        if "a" in table_by:
                            sp.wait_ge(s_a, w + 1)
                        sp.dma_start(rows[bass.ds(w, 1), :, :].rearrange("w p n -> (w p) n"), tile[:, b, 0:table_width]).then_inc(s_stored[b], 16)

                    with sp.Fori(0, NW // 2) as i:
                        store(i * 2, 0)
                        store(i * 2 + 1, 1)
                    for b in range(2):
                        sp.wait_ge(s_stored[b], 16 * (NW // 2))



class EdgeSemaphores:

    def __init__(self, m):
        self.index = m.sem("index")
        self.onehot = m.sem("onehot")
        self.t = m.sem("t")
        self.turned = m.sem("turned")
        self.n = m.sem("n")
        self.first = m.sem("first")
        self.logit = m.sem("logit")
        self.logit16 = m.sem("logit16")
        self.onehot16 = m.sem("onehot16")
        self.m = m.sem("m")
        self.top = m.sem("top")
        self.peak = m.sem("peak")
        self.drop = m.sem("drop")
        self.kept = m.sem("kept")
        self.fade = m.sem("fade")
        self.e = m.sem("e")
        self.arg = m.sem("arg")
        self.weight = m.sem("weight")
        self.summand = m.sem("summand")
        self.u = m.sem("u")
        self.faded = m.sem("faded")
        self.acc = m.sem("acc")
        self.ones = m.sem("ones")
        self.passed = m.sem("passed")


def edge_pass(nc, c, stage, order, table, width, acc, R, kind, H=1, C=0, node=None, node_c0=0, value_c0=0, count=False, biggest=None, slots=8):
    with ExitStack() as stack:
        m = Memory(nc, stack, stage)
        GS = slots
        guarded = kind in ("gat", "dot")
        weighted = kind != "sum"
        HC = H * C
        NV = HC if kind == "dot" else H
        index = m.sb("index", [P, GS, 2], I32)
        rows = m.sb("rows", [P, GS, 2, width])
        onehot = m.sb("onehot", [P, 4, 2, P])
        if weighted:
            turned = m.sb("turned", [P, 4, 2, P])
            logit = m.sb("logit", [P, 4, 2, H])
            first = m.sb("first", [P, 2, NV])
            summand = m.sb("summand", [P, 2, 2, R])
            ps_t = m.ps("ps_t", [P, 2, 256])
            ps_n = m.ps("ps_n", [P, 2, 256])
        if guarded:
            onehot16 = m.sb("onehot16", [P, 4, 2, P], BF16)
            logit16 = m.sb("logit16", [P, 2, 2, H], BF16)
            top = m.sb("top", [P, 2, H])
            peak = m.sb("peak", [P, 4, H])
            drop = m.sb("drop", [P, 4, H])
            fade = m.sb("fade", [P, 4, H])
            arg = m.sb("arg", [P, 2, 2, H])
            ps_m = m.ps("ps_m", [P, 2, max(H, 2), P])
            ps_e = m.ps("ps_e", [P, 2, 256])
        ps_u = m.ps("ps_u", [P, 512])
        s = EdgeSemaphores(m)
        s_rows = [m.sem(f"rows{g}") for g in range(GS)]
        freed = s.summand if weighted else s.u

        def heads(ap):
            return ap.rearrange("p (h c) -> p h c", h=H)

        def arrived(eng, g):
            eng.wait_ge(s_rows[g.slot(GS)], g.turn(GS) * 32 + 32)

        def steps(eng, stages):
            most = max(lag for lag, _ in stages)

            def turn(i, k0=0, k1=UN):
                for k in range(k0, k1):
                    for lag, what in stages:
                        g = Group(i, k - lag)
                        if g.exists():
                            what(g)

            turn(0)
            with eng.Fori(1, NG // UN) as i:
                turn(i)
            turn(NG // UN, 0, most)

        with nc.Block() as block:
            @block.gpsimd
            def _(pool):
                def gather(g):
                    wait(pool, freed, g.plus(1 - GS))
                    apart(pool, s.index, g.plus(1), s.passed)
                    for j in range(2):
                        pool.indirect_dma_start(
                            out=rows[:, g.slot(GS), j, :], out_offset=None, in_=table,
                            in_offset=bass.IndirectOffsetOnAxis(ap=index[:, g.slot(GS), j:j + 1], axis=0),
                        ).then_inc(s_rows[g.slot(GS)], 16)

                steps(pool, [(0, gather)])

            @block.tensor
            def _(pe):
                def turn(g):
                    pe.wait_ge(s.onehot, g.plus(1))
                    wait(pe, s.turned, g.plus(0))
                    for j in range(2):
                        last = pe.transpose(ps_t[:, j, 0:P], onehot[:, g.slot(4), j, :], c.ident[:, :])
                    last.then_inc(s.t, 1)

                def of_node(g):
                    window = pe.value_load(order.window[0:1, bass.ds(g.plus(0), 1)], min_val=0, max_val=NW - 1)
                    pe.wait_ge(s.turned, g.plus(1))
                    wait(pe, s.first, g.plus(0))
                    for j in range(2):
                        last = pe.matmul(ps_n[:, j, 0:NV], turned[:, g.slot(4), j, :],
                                         node[:, bass.ds(window, 1), node_c0:node_c0 + NV].rearrange("p a n -> p (a n)"), start=True, stop=True)
                    last.then_inc(s.n, 1)

                def spread(g):
                    pe.wait_ge(s.onehot16, g.plus(1))
                    pe.wait_ge(s.logit16, g.plus(1))
                    wait(pe, s.top, g.plus(0))
                    for j in range(2):
                        for h0 in range(0, H, 4):
                            h1 = min(H, h0 + 4)
                            for h in range(h0, h1):
                                pe.matmul(ps_m[:, j, h, :], bc(logit16[:, g.slot(2), j, h:h + 1], [P, P]), c.ident16[:, :],
                                          start=h == h0, stop=False, skip_group_check=True)
                            last = pe.matmul(ps_m[:, j, h0:h1, :], onehot16[:, g.slot(4), j, :], c.big16[:, 0:h1 - h0, :],
                                             start=False, stop=True, skip_group_check=True)
                    last.then_inc(s.m, 1)

                def of_peak(g):
                    pe.wait_ge(s.peak, g.plus(1))
                    wait(pe, s.arg, g.plus(0))
                    for j in range(2):
                        last = pe.matmul(ps_e[:, j, 0:H], turned[:, g.slot(4), j, :], peak[:, g.slot(4), :], start=True, stop=True)
                    last.then_inc(s.e, 1)

                def gather_in(g):
                    if weighted:
                        pe.wait_ge(s.summand, g.plus(1))
                    else:
                        pe.wait_ge(s.onehot, g.plus(1))
                        arrived(pe, g)
                    wait(pe, s.acc, g.plus(0))
                    for j in range(2):
                        rhs = summand[:, g.slot(2), j, :] if weighted else rows[:, g.slot(GS), j, 0:R]
                        last = pe.matmul(ps_u[:, 0:R], onehot[:, g.slot(4), j, :], rhs, start=j == 0, stop=j == 1)
                    last.then_inc(s.u, 1)

                if guarded:
                    steps(pe, [(2, of_peak), (1, spread), (0, turn), (0, of_node), (3, gather_in)])
                elif weighted:
                    steps(pe, [(0, turn), (0, of_node), (2, gather_in)])
                else:
                    steps(pe, [(0, gather_in)])

            @block.scalar
            def _(act):
                def weight(g):
                    w = summand[:, g.slot(2), :, 0:H * (C + 1)].rearrange("p j (h c) -> p j h c", h=H)[:, :, :, C]
                    wait(act, s.u, g.plus(-1))
                    if guarded:
                        act.wait_ge(s.arg, g.plus(1))
                        act.activation(w, arg[:, g.slot(2), :, :], ACT.Exp).then_inc(s.weight, 1)
                    else:
                        act.wait_ge(s.logit, g.plus(1))
                        act.activation(w, logit[:, g.slot(4), :, :], ACT.Exp, scale=-1.0).then_inc(s.weight, 1)

                def fading(g):
                    act.wait_ge(s.drop, g.plus(1))
                    wait(act, s.faded, g.plus(-3))
                    act.activation(fade[:, g.slot(4), :], drop[:, g.slot(4), :], ACT.Exp).then_inc(s.fade, 1)

                def narrow(g):
                    act.wait_ge(s.onehot, g.plus(1))
                    wait(act, s.m, g.plus(-3))
                    act.activation(onehot16[:, g.slot(4), :, :], onehot[:, g.slot(4), :, :], ACT.Copy).then_inc(s.onehot16, 1)

                def copy(g):
                    act.wait_ge(s.t, g.plus(1))
                    wait(act, s.e if guarded else s.n, g.plus(-3))
                    act.activation(turned[:, g.slot(4), :, :], ps_t[:, :, 0:P], ACT.Copy).then_inc(s.turned, 1)

                if guarded:
                    steps(act, [(3, weight), (2, fading), (0, narrow), (0, copy)])
                elif weighted:
                    steps(act, [(1, weight), (0, copy)])

            @block.vector
            def _(dve):
                def stage_index(g):
                    at = g.plus(GS) if g is not None else None
                    dve.tensor_copy(index[:, g.slot(GS), :], order.row[:, bass.ds(at * 2, 2)]).then_inc(s.index, 1)

                def mark(g):
                    wait(dve, s.u, g.plus(-3))
                    if guarded:
                        wait(dve, s.onehot16, g.plus(-3))
                    dve.tensor_tensor(onehot[:, g.slot(4), :, :], bc(c.lane[:, :].rearrange("p (j n) -> p j n", j=1), [P, 2, P]),
                                      bc(order.place[:, bass.ds(g.plus(0) * 2, 2)].rearrange("p (j n) -> p j n", n=1), [P, 2, P]),
                                      ALU.is_equal).then_inc(s.onehot, 1)

                def logits(g):
                    dve.wait_ge(s.n, g.plus(1))
                    arrived(dve, g)
                    stage_index(g)
                    r = rows[:, g.slot(GS), :, :]
                    if kind == "dot":
                        dve.tensor_tensor(first[:, :, :], ps_n[:, :, 0:NV], r[:, :, 0:HC], ALU.mult).then_inc(s.first, 1)
                        dve.wait_ge(s.first, g.plus(1))
                        dve.tensor_reduce(logit[:, g.slot(4), :, :], first[:, :, :].rearrange("p j (h c) -> p j h c", h=H), AX.X, ALU.add).then_inc(s.logit, 1)
                    else:
                        dve.tensor_tensor(first[:, :, :], ps_n[:, :, 0:NV], r[:, :, HC:HC + H], ALU.add).then_inc(s.first, 1)
                        dve.wait_ge(s.first, g.plus(1))
                        dve.scalar_tensor_tensor(logit[:, g.slot(4), :, :], first[:, :, :], 0.2, first[:, :, :], ALU.mult, ALU.max).then_inc(s.logit, 1)
                    if guarded:
                        dve.wait_ge(s.logit, g.plus(1))
                        wait(dve, s.m, g.plus(-1))
                        dve.tensor_scalar(logit16[:, g.slot(2), :, :], logit[:, g.slot(4), :, :], CLIP, -CLIP, ALU.min, ALU.max).then_inc(s.logit16, 1)

                def maximum(g):
                    window = dve.value_load(order.window[0:1, bass.ds(g.plus(0), 1)], min_val=0, max_val=NW - 1)
                    dve.wait_ge(s.m, g.plus(1))
                    dve.tensor_reduce(top[:, g.slot(2), :], ps_m[:, :, 0:H, :].rearrange("p j h e -> p h j e"), AX.XY, ALU.max).then_inc(s.top, 1)
                    dve.wait_ge(s.top, g.plus(1))
                    wait(dve, s.kept, g.plus(0))
                    wait(dve, s.e, g.plus(-3))
                    now = biggest[:, bass.ds(window, 1), 0:H].rearrange("p a h -> p (a h)")
                    dve.scalar_tensor_tensor(peak[:, g.slot(4), :], top[:, g.slot(2), :], -BIG, now, ALU.add, ALU.max).then_inc(s.peak, 1)
                    dve.wait_ge(s.peak, g.plus(1))
                    wait(dve, s.fade, g.plus(-3))
                    dve.tensor_tensor(drop[:, g.slot(4), :], now, peak[:, g.slot(4), :], ALU.subtract).then_inc(s.drop, 1)
                    dve.wait_ge(s.drop, g.plus(1))
                    dve.tensor_scalar(now, peak[:, g.slot(4), :], 1.0, None, ALU.mult).then_inc(s.kept, 1)

                def argument(g):
                    dve.wait_ge(s.e, g.plus(1))
                    wait(dve, s.weight, g.plus(-1))
                    dve.tensor_tensor(arg[:, g.slot(2), :, :], logit[:, g.slot(4), :, :], ps_e[:, :, 0:H], ALU.subtract).then_inc(s.arg, 1)

                def weigh(g):
                    dve.wait_ge(s.weight, g.plus(1))
                    out = summand[:, g.slot(2), :, 0:H * (C + 1)].rearrange("p j (h c) -> p j h c", h=H)
                    dve.tensor_tensor(out[:, :, :, 0:C], rows[:, g.slot(GS), :, value_c0:value_c0 + HC].rearrange("p j (h c) -> p j h c", h=H),
                                      bc(out[:, :, :, C:C + 1], [P, 2, H, C]), ALU.mult).then_inc(s.summand, 1)

                def add(g):
                    window = dve.value_load(order.window[0:1, bass.ds(g.plus(0), 1)], min_val=0, max_val=NW - 1)
                    wait(dve, s.acc, g.plus(0))
                    mine = acc[:, bass.ds(window * R, R)]
                    if guarded:
                        dve.wait_ge(s.fade, g.plus(1))
                        part = acc[:, bass.ds(window * R, H * (C + 1))].rearrange("p (h c) -> p h c", h=H)
                        dve.tensor_tensor(part, part, bc(fade[:, g.slot(4), :].rearrange("p (h c) -> p h c", c=1), [P, H, C + 1]), ALU.mult).then_inc(s.faded, 1)
                        dve.wait_ge(s.faded, g.plus(1))
                    dve.wait_ge(s.u, g.plus(1))
                    dve.tensor_tensor(mine, mine, ps_u[:, 0:R], ALU.add).then_inc(s.acc, 1)
                    if not weighted:
                        stage_index(g)

                for k in range(GS):
                    dve.tensor_copy(index[:, k, :], order.row[:, 2 * k:2 * k + 2]).then_inc(s.index, 1)
                if count:
                    dve.memset(summand[:, :, :, R - 1:R], 1.0).then_inc(s.ones, 1)
                else:
                    dve.memset(onehot[:, :, :, :], 0.0).then_inc(s.ones, 1)
                dve.wait_ge(s.ones, 1)
                if guarded:
                    steps(dve, [(3, argument), (4, add), (2, maximum), (1, logits), (0, mark), (3, weigh)])
                elif weighted:
                    steps(dve, [(3, add), (1, logits), (0, mark), (2, weigh)])
                else:
                    steps(dve, [(0, mark), (2, add)])



def all_windows(x, n=D):
    return x[:, 0:NW * n].rearrange("p (w n) -> p w n", n=n)


def keep_valid(link, dve, c, x):
    n = x.shape[2]
    link(dve.tensor_tensor(x[:, LAST:NW, :], x[:, LAST:NW, :], bc(c.valid[:, :].rearrange("p (w n) -> p w n", n=1), [P, 2, n]), ALU.mult))


def normalize(link, dve, c, x, scratch, small):
    mean, var = small[:, 0, :], small[:, 1, :]

    def wide(a):
        return bc(a.rearrange("p (w n) -> p w n", n=1), [P, NW, D])

    link(dve.tensor_reduce(mean, x, AX.X, ALU.add))
    link(dve.tensor_scalar(mean, mean, 1.0 / D, None, ALU.mult))
    link(dve.tensor_tensor(x, x, wide(mean), ALU.subtract))
    link(dve.tensor_tensor(scratch, x, x, ALU.mult))
    link(dve.tensor_reduce(var, scratch, AX.X, ALU.add))
    link.asked(dve.tensor_scalar(var, var, 1.0 / D, EPS, ALU.mult, ALU.add))
    link(dve.tensor_tensor(x, x, wide(var), ALU.mult))
    keep_valid(link, dve, c, x)


def inverse_root(pool, minus_half, x):
    return pool.tensor_tensor(x, x, bc(minus_half, [P, x.shape[1]]), ALU.pow)


def on_vector(nc, c, stage, loads, work, root=None):
    with ExitStack() as stack:
        m = Memory(nc, stack, stage)
        s_loaded, s_step, s_ask, s_root = (m.sem(x) for x in ("loaded", "step", "ask", "root"))
        with nc.Block() as block:
            if root is not None:
                @block.gpsimd
                def _(pool):
                    pool.wait_ge(s_ask, 1)
                    inverse_root(pool, c.minus_half[:, :], root).then_inc(s_root, 1)

            @block.sync
            def _(sp):
                for to, frm in loads:
                    sp.dma_start(to, frm).then_inc(s_loaded, 16)

            @block.vector
            def _(dve):
                if loads:
                    dve.wait_ge(s_loaded, 16 * len(loads))
                link = Link(dve, s_step)

                def asked(ins):
                    ins.then_inc(s_ask, 1)
                    dve.wait_ge(s_root, 1)

                link.asked = asked
                work(link, dve)


def row(v):
    return v.rearrange("(a n) -> a n", a=1)


def spread_row(v, n):
    return row(v).to_broadcast([P, n]) if len(v.shape) == 1 else v.to_broadcast([P, n])


def fold(link, dve, w, c0, a, H, C, to, scratch):
    n = H * C
    for k in range(2):
        link(dve.tensor_tensor(scratch[:, 0:n], w[:, k, c0:c0 + n], a, ALU.mult))
        link(dve.tensor_reduce(w[:, k, to:to + H], scratch[:, 0:n].rearrange("p (h c) -> p h c", h=H), AX.X, ALU.add))


def by_chunk(w):
    return w.rearrange("(k p) n -> p k n", p=P)


class Keep:
    pass


def gnn_kernel(nc, x, src, dst,
               a_w1, a_as1, a_ad1, a_b1, a_w2, a_as2, a_ad2, a_b2, a_wf, a_bf,
               b_w1, b_a1, b_w2, b_a2,
               t_wq, t_bq, t_wk, t_bk, t_wv, t_bv, t_wo, t_bo,
               g_w1, g_b1, g_g1, g_be1, g_w2, g_b2, g_g2, g_be2, g_wfc, g_bfc, out):
    records = [nc.dram_tensor(f"records_{n}", [P, NSLOT, 2], I32, kind="Internal").ap() for n in ("dst", "src")]
    tables = {n: nc.dram_tensor(f"table_{n}", [NPAD, n], F32, kind="Internal").ap() for n in (264, 66, 258, 512, 128, 64)}

    def drain(eng, to, frm, scale=1.0):
        if eng is nc.vector or not hasattr(eng, "activation"):
            return eng.tensor_copy(to, frm)
        return eng.activation(to, frm, ACT.Copy, scale=scale)

    with ExitStack() as stack:
        m = Memory(nc, stack, "all")
        c = Keep()
        constants(nc, m, c)
        order = Keep()
        order.row = m.sb("row", [P, NSLOT + 2 * UN], I32)
        order.place = m.sb("place", [P, NSLOT])
        order.window = m.sb("window", [P, NG], I32)
        kept = {n: (nc.dram_tensor(f"kept_row_{n}", [P, NSLOT + 2 * UN], I32, kind="Internal").ap(),
                    nc.dram_tensor(f"kept_place_{n}", [P, NSLOT], F32, kind="Internal").ap(),
                    nc.dram_tensor(f"kept_window_{n}", [P, NG], I32, kind="Internal").ap()) for n in ("dst", "src")}

        def move_order(name, load):
            s_moved = m.sem(f"moved_{name}_{load}")
            with nc.Block() as block:
                @block.sync
                def _(sp):
                    for d, t in zip(kept[name], (order.row, order.place, order.window)):
                        to, frm = (t[:, :], d) if load else (d, t[:, :])
                        sp.dma_start(to, frm).then_inc(s_moved, 16)
                    sp.wait_ge(s_moved, 48)

        sort_edges(nc, c, "by_src", src, dst, records[1], order)
        move_order("src", False)
        sort_edges(nc, c, "by_dst", dst, src, records[0], order)
        move_order("dst", False)

        X = m.sb("X", [P, NW * D])
        acc = m.sb("acc", [P, NW * 264])
        Y = m.sb("Y", [P, NW * D])
        nodes = m.sb("nodes", [P, NW, 8])
        biggest = m.sb("biggest", [P, NW, 8])
        small = m.sb("small", [P, 2, NW])
        degree = m.sb("degree", [P, NW])
        x3, y3 = all_windows(X), all_windows(Y)

        def wide(a, *shape):
            return bc(a, [P, NW, *shape])

        def at(t, w, n, c0=0, c1=None):
            return t[:, bass.ds(w * n + c0, (n if c1 is None else c1) - c0)]

        with ExitStack() as st:
            mm = Memory(nc, st, "a1")
            W = mm.sb("W", [P, 2, 264])
            avec = mm.sb("avec", [P, 2, 256])
            tmp = mm.sb("tmp", [P, 256])

            def work(link, dve):
                fold(link, dve, W, 0, avec[:, 0, :], 4, 64, 256, tmp)
                fold(link, dve, W, 0, avec[:, 1, :], 4, 64, 260, tmp)

            def zero(link, dve):
                link(dve.memset(x3[:, LAST:NW, :], 0.0))

            on_vector(nc, c, "a1z", [], zero)
            on_vector(nc, c, "a1w", [
                (x3[:, 0:LAST, :], x[0:LAST * P, :].rearrange("(w p) n -> p w n", p=P)),
                (X[0:VALID, LAST * D:(LAST + 1) * D], x[LAST * P:N, :]),
                (W[:, :, 0:256], by_chunk(a_w1)),
                (avec[:, 0, :], spread_row(a_as1.rearrange("h c -> (h c)"), 256)),
                (avec[:, 1, :], spread_row(a_ad1.rearrange("h c -> (h c)"), 256)),
            ], work)
            R = 4 * 65 + 1

            def drain_v(dve, ps, w, tile):
                dve.tensor_copy(at(acc, w, R, 0, 260).rearrange("p (h c) -> p h c", h=4)[:, :, 0:64], ps[:, 0:256].rearrange("p (h c) -> p h c", h=4))
                return dve.tensor_copy(nodes[:, bass.ds(w, 1), :].rearrange("p a n -> p (a n)"), ps[:, 256:264])

            def drain_a(act, ps, w, tile):
                return act.activation(tile[:, 0:264], ps[:, 0:264], ACT.Copy)

            linear(nc, c, "a1l", [(x3, 0, P), (x3, P, P)], [W[:, 0, :], W[:, 1, :]], None, 264, drain_v, drain_a, tables[264], 264, "a")

        def self_loops(H, C, R, ones):
            def work(link, dve):
                a = acc[:, 0:NW * R].rearrange("p (w r) -> p w r", r=R)
                link(dve.memset(a[:, :, 0:H * (C + 1)].rearrange("p w (h c) -> p w h c", h=H)[:, :, :, C], 1.0))
                if ones:
                    link(dve.memset(a[:, :, R - 1:R], 1.0))
                link(dve.tensor_tensor(biggest[:, :, 0:H], nodes[:, :, 0:H], nodes[:, :, H:2 * H], ALU.add))
                link(dve.scalar_tensor_tensor(biggest[:, :, 0:H], biggest[:, :, 0:H], 0.2, biggest[:, :, 0:H], ALU.mult, ALU.max))
            return work

        on_vector(nc, c, "a1s", [], self_loops(4, 64, R, True))
        edge_pass(nc, c, "a1e", order, tables[264], 264, acc, R, "gat", H=4, C=64, node=nodes, node_c0=4, count=True, biggest=biggest)

        with ExitStack() as st:
            mm = Memory(nc, st, "a2")
            W = mm.sb("W", [P, 2, 66])
            avec = mm.sb("avec", [P, 2, 64])
            tmp = mm.sb("tmp", [P, 256])
            bias = mm.sb("bias", [P, 256])

            def work(link, dve):
                a = acc[:, 0:NW * R].rearrange("p (w r) -> p w r", r=R)
                link(dve.tensor_copy(degree[:, :], a[:, :, R - 1]))
                for h in range(4):
                    z = a[:, :, h * 65 + 64:h * 65 + 65]
                    link(dve.reciprocal(z, z))
                    link(dve.tensor_tensor(y3[:, :, h * 64:(h + 1) * 64], a[:, :, h * 65:h * 65 + 64], wide(z, 64), ALU.mult))
                link(dve.tensor_tensor(y3, y3, bc(bias[:, :].rearrange("p (w n) -> p w n", w=1), [P, NW, 256]), ALU.add))
                link(dve.tensor_scalar(y3, y3, 0.0, None, ALU.max))
                keep_valid(link, dve, c, y3)
                fold(link, dve, W, 0, avec[:, 0, :], 1, 64, 64, tmp)
                fold(link, dve, W, 0, avec[:, 1, :], 1, 64, 65, tmp)

            on_vector(nc, c, "a2w", [
                (W[:, :, 0:64], by_chunk(a_w2)), (bias[:, :], spread_row(a_b1, 256)),
                (avec[:, 0, :], spread_row(a_as2, 64)), (avec[:, 1, :], spread_row(a_ad2, 64)),
            ], work)

            def drain_v2(dve, ps, w, tile):
                dve.tensor_copy(at(acc, w, 65, 0, 64), ps[:, 0:64])
                return dve.tensor_copy(nodes[:, bass.ds(w, 1), 0:2].rearrange("p a n -> p (a n)"), ps[:, 64:66])

            def drain_a2(act, ps, w, tile):
                return act.activation(tile[:, 0:66], ps[:, 0:66], ACT.Copy)

            linear(nc, c, "a2l", [(y3, 0, P), (y3, P, P)], [W[:, 0, :], W[:, 1, :]], None, 66, drain_v2, drain_a2, tables[66], 66, "a")
        on_vector(nc, c, "a2s", [], self_loops(1, 64, 65, False))
        edge_pass(nc, c, "a2e", order, tables[66], 66, acc, 65, "gat", H=1, C=64, node=nodes, node_c0=1, biggest=biggest)

        def add_to_x(dve, ps, w, tile):
            return dve.tensor_tensor(at(X, w, D), at(X, w, D), ps[:, 0:D], ALU.add)

        with ExitStack() as st:
            mm = Memory(nc, st, "af")
            W = mm.sb("W", [P, 256])
            brow = mm.sb("brow", [1, 256])
            bias = mm.sb("bias", [P, 64])
            h64 = all_windows(Y, 64)

            def work(link, dve):
                a = acc[:, 0:NW * 65].rearrange("p (w r) -> p w r", r=65)
                link(dve.reciprocal(a[:, :, 64:65], a[:, :, 64:65]))
                link(dve.tensor_tensor(h64, a[:, :, 0:64], wide(a[:, :, 64:65], 64), ALU.mult))
                link(dve.tensor_tensor(h64, h64, bc(bias[:, :].rearrange("p (w n) -> p w n", w=1), [P, NW, 64]), ALU.add))

            on_vector(nc, c, "afw", [(W[0:64, :], a_wf), (brow[:, :], row(a_bf)), (bias[:, :], spread_row(a_b2, 64))], work)
            linear(nc, c, "afl", [(h64, 0, 64)], [W], brow, 256, add_to_x, None)

        with ExitStack() as st:
            mm = Memory(nc, st, "b")
            W = mm.sb("W", [P, 2, 260])
            avec = mm.sb("avec", [P, 4, 128])
            tmp = mm.sb("tmp", [P, 256])
            R = 2 * 129

            def work(link, dve):
                normalize(link, dve, c, x3, y3, small)
                for h in range(2):
                    fold(link, dve, W, 128 * h, avec[:, 2 * h + 1, :], 1, 128, 256 + h, tmp)
                    fold(link, dve, W, 128 * h, avec[:, 2 * h, :], 1, 128, 258 + h, tmp)
                link(dve.memset(acc[:, 0:NW * R], 0.0))
                for h in range(2):
                    z = acc[:, 0:NW * R].rearrange("p (w r) -> p w r", r=R)[:, LAST:NW, h * 129 + 128]
                    link(dve.tensor_scalar(z, c.valid[:, :], -1.0, 1.0, ALU.mult, ALU.add))

            on_vector(nc, c, "bw", [
                (W[:, :, 0:128], by_chunk(b_w1)), (W[:, :, 128:256], by_chunk(b_w2)),
            ] + [(avec[:, 2 * h + k, :], spread_row(a[:, 128 * k:128 * (k + 1)], 128))
                 for h, a in enumerate((b_a1, b_a2)) for k in range(2)], work, small[:, 1, :])

            def drain_vb(dve, ps, w, tile):
                return dve.tensor_copy(nodes[:, bass.ds(w, 1), 0:2].rearrange("p a n -> p (a n)"), ps[:, 258:260])

            def drain_ab(act, ps, w, tile):
                return act.activation(tile[:, 0:258], ps[:, 0:258], ACT.Copy)

            linear(nc, c, "bl", [(x3, 0, P), (x3, P, P)], [W[:, 0, :], W[:, 1, :]], None, 260, drain_vb, drain_ab, tables[258], 258, "a")
        move_order("src", True)
        edge_pass(nc, c, "be", order, tables[258], 258, acc, R, "neg", H=2, C=128, node=nodes, node_c0=0)

        with ExitStack() as st:
            mm = Memory(nc, st, "t")
            W = mm.sb("W", [P, 2, 768])
            brow = mm.sb("brow", [1, 768])

            def work(link, dve):
                a = acc[:, 0:NW * R].rearrange("p (w r) -> p w r", r=R)
                for h in range(2):
                    z = a[:, :, h * 129 + 128:h * 129 + 129]
                    link(dve.reciprocal(z, z))
                    link(dve.tensor_tensor(y3[:, :, h * 128:(h + 1) * 128], a[:, :, h * 129:h * 129 + 128], wide(z, 128), ALU.mult))
                low = acc[:, 0:NW * D].rearrange("p (w n) -> p w n", n=D)
                link(dve.tensor_scalar(low, y3, 0.0, None, ALU.min))

            on_vector(nc, c, "tw", [
                (W[:, :, 0:256], by_chunk(t_wq)), (W[:, :, 256:512], by_chunk(t_wk)), (W[:, :, 512:768], by_chunk(t_wv)),
                (brow[:, 0:256], row(t_bq)), (brow[:, 256:512], row(t_bk)), (brow[:, 512:768], row(t_bv)),
            ], work)
            s_exp = mm.sem("exp")
            with nc.Block() as block:
                @block.scalar
                def _(act):
                    act.activation(acc[:, 0:NW * D], acc[:, 0:NW * D], ACT.Exp).then_inc(s_exp, 1)

            def work(link, dve):
                low = acc[:, 0:NW * D].rearrange("p (w n) -> p w n", n=D)
                link(dve.scalar_tensor_tensor(y3, y3, 0.0, low, ALU.max, ALU.add))
                link(dve.scalar_tensor_tensor(x3, y3, -1.0, x3, ALU.add, ALU.add))
                normalize(link, dve, c, x3, y3, small)
                link(dve.memset(acc[:, :], 0.0))
                link(dve.memset(biggest[:, :, :], -BIG))

            on_vector(nc, c, "tx", [], work, small[:, 1, :])

            def drain_vt(dve, ps, w, tile):
                return dve.tensor_scalar(at(Y, w, D), ps[:, 0:256], 32.0 ** -0.5, None, ALU.mult)

            def drain_at(act, ps, w, tile):
                return act.activation(tile[:, 0:512], ps[:, 256:768], ACT.Copy)

            linear(nc, c, "tl", [(x3, 0, P), (x3, P, P)], [W[:, 0, :], W[:, 1, :]], brow, 768, drain_vt, drain_at, tables[512], 512, "a")
        R = 8 * 33
        edge_pass(nc, c, "te", order, tables[512], 512, acc, R, "dot", H=8, C=32, node=y3, node_c0=0, value_c0=256, biggest=biggest, slots=4)

        with ExitStack() as st:
            mm = Memory(nc, st, "to")
            W = mm.sb("W", [P, 2, 256])
            brow = mm.sb("brow", [1, 256])

            def work(link, dve):
                a = acc[:, 0:NW * R].rearrange("p (w r) -> p w r", r=R)
                for h in range(8):
                    z = a[:, :, h * 33 + 32:h * 33 + 33]
                    link(dve.tensor_scalar(z, z, 1e-37, None, ALU.max))
                    link(dve.reciprocal(z, z))
                    link(dve.tensor_tensor(y3[:, :, h * 32:(h + 1) * 32], a[:, :, h * 33:h * 33 + 32], wide(z, 32), ALU.mult))

            on_vector(nc, c, "tow", [(W[:, :, :], by_chunk(t_wo)), (brow[:, :], row(t_bo))], work)
            linear(nc, c, "tol", [(y3, 0, P), (y3, P, P)], [W[:, 0, :], W[:, 1, :]], brow, 256, add_to_x, None)

        move_order("dst", True)

        f1, f2 = Y[:, 0:NW * 128], Y[:, NW * 128:NW * 192]
        f1w = f1.rearrange("p (w n) -> p w n", n=128)
        f2w = f2.rearrange("p (w n) -> p w n", n=64)

        def dinv(n):
            return bc(small[:, 1, :].rearrange("p (w n) -> p w n", n=1), [P, NW, n])

        def convolve(tag, sources, weights, n):
            def drain_v(dve, ps, w, tile):
                dve.tensor_tensor(tile[:, 0:n], ps[:, 0:n], bc(small[:, 1, bass.ds(w, 1)], [P, n]), ALU.mult)
                return dve.tensor_tensor(at(acc, w, n), ps[:, 0:n], bc(small[:, 1, bass.ds(w, 1)], [P, n]), ALU.mult)

            linear(nc, c, tag + "l", sources, weights, None, n, drain_v, None, tables[n], n, "v")
            edge_pass(nc, c, tag + "e", order, tables[n], n, acc, n, "sum")

        def batch_norm(tag, n, to, b, gamma, beta):
            with ExitStack() as st:
                mm = Memory(nc, st, tag)
                vecs = mm.sb("vecs", [P, 3, n])
                part = mm.sb("part", [P, n])
                mean = mm.sb("mean", [P, n])
                scale = mm.sb("scale", [P, n])
                ps = mm.ps("ps", [P, 2, 512])
                s_loaded, s_step, s_part, s_sum, s_ask, s_root = (mm.sem(x) for x in ("loaded", "step", "part", "sum", "ask", "root"))
                a = acc[:, 0:NW * n].rearrange("p (w n) -> p w n", n=n)
                down = acc[:, 0:NW * n].rearrange("p (w n) -> p n w", n=n)
                sq = acc[:, NW * n:2 * NW * n].rearrange("p (w n) -> p w n", n=n)

                def rows(v):
                    return bc(v.rearrange("p (w n) -> p w n", w=1), [P, NW, n])

                with nc.Block() as block:
                    @block.sync
                    def _(sp):
                        for k, v in enumerate((b, gamma, beta)):
                            sp.dma_start(vecs[:, k, :], spread_row(v, n)).then_inc(s_loaded, 16)

                    @block.gpsimd
                    def _(pool):
                        pool.wait_ge(s_ask, 1)
                        inverse_root(pool, c.minus_half[:, :], scale[:, :]).then_inc(s_root, 1)

                    @block.tensor
                    def _(pe):
                        for k in range(2):
                            pe.wait_ge(s_part, k + 1)
                            pe.matmul(ps[:, k, 0:n], c.ones[:, :], part[:, :], start=True, stop=True).then_inc(s_sum, 1)

                    @block.vector
                    def _(dve):
                        link = Link(dve, s_step)
                        dve.wait_ge(s_loaded, 48)
                        link(dve.tensor_tensor(a, a, dinv(n), ALU.mult))
                        link(dve.tensor_tensor(a, a, rows(vecs[:, 0, :]), ALU.add))
                        keep_valid(link, dve, c, a)
                        dve.tensor_reduce(part[:, :], down, AX.X, ALU.add).then_inc(s_part, 1)
                        dve.wait_ge(s_sum, 1)
                        link(dve.tensor_scalar(mean[:, :], ps[:, 0, 0:n], 1.0 / N, None, ALU.mult))
                        link(dve.tensor_tensor(a, a, rows(mean[:, :]), ALU.subtract))
                        keep_valid(link, dve, c, a)
                        link(dve.tensor_tensor(to, a, a, ALU.mult))
                        dve.tensor_reduce(part[:, :], to.rearrange("p w n -> p n w"), AX.X, ALU.add).then_inc(s_part, 1)
                        dve.wait_ge(s_sum, 2)
                        dve.tensor_scalar(scale[:, :], ps[:, 1, 0:n], 1.0 / N, EPS, ALU.mult, ALU.add).then_inc(s_ask, 1)
                        dve.wait_ge(s_root, 1)
                        link(dve.tensor_tensor(scale[:, :], scale[:, :], vecs[:, 1, :], ALU.mult))
                        link(dve.tensor_tensor(a, a, rows(scale[:, :]), ALU.mult))
                        link(dve.tensor_tensor(a, a, rows(vecs[:, 2, :]), ALU.add))
                        link(dve.tensor_scalar(to, a, 0.0, None, ALU.max))

        with ExitStack() as st:
            mm = Memory(nc, st, "g1")
            W = mm.sb("W", [P, 2, 128])

            def work(link, dve):
                normalize(link, dve, c, x3, y3, small)

            def degrees(link, dve):
                link.asked(dve.tensor_copy(small[:, 1, :], degree[:, :]))

            on_vector(nc, c, "g1w", [(W[:, :, :], by_chunk(g_w1))], work, small[:, 1, :])
            on_vector(nc, c, "g1d", [], degrees, small[:, 1, :])
            convolve("g1", [(x3, 0, P), (x3, P, P)], [W[:, 0, :], W[:, 1, :]], 128)
            batch_norm("n1", 128, f1w, g_b1, g_g1, g_be1)
        with ExitStack() as st:
            mm = Memory(nc, st, "g2")
            W = mm.sb("W", [P, 64])
            on_vector(nc, c, "g2w", [(W[:, :], g_w2)], lambda link, dve: None)
            convolve("g2", [(f1w, 0, P)], [W], 64)
            batch_norm("n2", 64, f2w, g_b2, g_g2, g_be2)
        with ExitStack() as st:
            mm = Memory(nc, st, "gf")
            W = mm.sb("W", [P, 4, 256])
            brow = mm.sb("brow", [1, 256])
            on_vector(nc, c, "gfw", [(W[:, 0:3, :], by_chunk(g_wfc[0:384, :])), (W[0:64, 3, :], g_wfc[384:448, :]),
                                  (brow[:, :], row(g_bfc))], lambda link, dve: None)

            def drain_vf(dve, ps, w, tile):
                return dve.scalar_tensor_tensor(at(X, w, D), ps[:, 0:D], 0.0, at(X, w, D), ALU.max, ALU.add)

            linear(nc, c, "gfl", [(x3, 0, P), (x3, P, P), (f1w, 0, P), (f2w, 0, 64)], [W[:, k, :] for k in range(4)], brow, 256, drain_vf, None)
            on_vector(nc, c, "last", [], lambda link, dve: normalize(link, dve, c, x3, y3, small), small[:, 1, :])
        s_out = m.sem("out")
        with nc.Block() as block:
            @block.sync
            def _(sp):
                sp.dma_start(out[0:LAST * P, :].rearrange("(w p) n -> p w n", p=P), x3[:, 0:LAST, :]).then_inc(s_out, 16)
                sp.dma_start(out[LAST * P:N, :], X[0:VALID, LAST * D:(LAST + 1) * D]).then_inc(s_out, 16)
                sp.wait_ge(s_out, 32)


_INS = ["x", "src", "dst", "L0_gnn_W1", "L0_gnn_att_src1", "L0_gnn_att_dst1", "L0_gnn_b1", "L0_gnn_W2",
        "L0_gnn_att_src2", "L0_gnn_att_dst2", "L0_gnn_b2", "L0_gnn_Wf", "L0_gnn_bf", "L1_gnn_W1", "L1_gnn_a1",
        "L1_gnn_W2", "L1_gnn_a2", "L2_gnn_Wq", "L2_gnn_bq", "L2_gnn_Wk", "L2_gnn_bk", "L2_gnn_Wv", "L2_gnn_bv",
        "L2_gnn_Wo", "L2_gnn_bo", "L3_gnn_W1", "L3_gnn_b1", "L3_gnn_g1", "L3_gnn_be1", "L3_gnn_W2", "L3_gnn_b2",
        "L3_gnn_g2", "L3_gnn_be2", "L3_gnn_Wfc", "L3_gnn_bfc"]


def kernel(**inputs):
    import numpy as np
    import concourse.bacc as bacc
    from concourse.bass_utils import run_bass_kernel_spmd

    nc = bacc.Bacc("TRN2", target_bir_lowering=False, num_devices=1)
    arrays, args = {}, []
    for name in _INS:
        a = np.ascontiguousarray(inputs[name])
        arrays[f"in_{name}"] = a
        args.append(nc.dram_tensor(f"in_{name}", a.shape, mybir.dt.from_np(a.dtype), kind="ExternalInput").ap())
    out = nc.dram_tensor("out", (N, D), F32, kind="ExternalOutput").ap()
    gnn_kernel(nc, *args, out)
    r = run_bass_kernel_spmd(nc, [arrays], core_ids=[0])
    return r.results[0]["out"]
```

```python
import concourse.bass as bass
from concourse import mybir
from concourse.alu_op_type import AluOpType as ALU
from contextlib import ExitStack

F32 = mybir.dt.float32
BF16 = mybir.dt.bfloat16
I32 = mybir.dt.int32
ACT = mybir.ActivationFunctionType
AX = mybir.AxisListType

P = 128
N = 6250
E = 100000
D = 256
WIN = -(-N // P)
NW = WIN + 1
NPAD = NW * P
PAD_ROW = NPAD - 1
GE = 2 * P
UN = 8
LEAD = 6
NG = -(-((E + WIN * (GE - 1)) // GE) // UN) * UN
NSLOT = 2 * NG
WT = NG + LEAD + UN
EP, EC = 125, 800
SB = 8
BIG = 65536.0
CLIP = 30000.0
EPS = 1e-5
LAST = WIN - 1
VALID = N - LAST * P


class Group:

    def __init__(self, i, k, windows=None):
        self.i, self.k = i, k
        self.window = None if windows is None else windows[k + LEAD]

    def plus(self, n):
        return self.i * UN + (self.k + n)

    def slot(self, n):
        return self.k % n

    def turn(self, n):
        return self.i * (UN // n) + self.k // n

    def exists(self):
        return not isinstance(self.i, int) or 0 <= self.i * UN + self.k < NG


def wait(eng, sem, count):
    if isinstance(count, int) and count <= 0:
        return
    eng.wait_ge(sem, count)


class Link:

    def __init__(self, eng, sem):
        self.eng, self.sem, self.n = eng, sem, 0

    def __call__(self, ins):
        self.n += 1
        ins.then_inc(self.sem, 1)
        self.eng.wait_ge(self.sem, self.n)


def apart(eng, sem, count, passed):
    wait(eng, sem, count)
    eng.sem_inc(passed, 1)


def bc(ap, shape):
    return ap.to_broadcast(shape)


class Memory:

    def __init__(self, nc, stack, stage):
        self.nc, self.stack, self.stage = nc, stack, stage
        self.sems = []
        stack.callback(self.clear)

    def clear(self):
        if self.sems:
            self.nc.clear_and_free_semaphores(self.sems)
            self.nc.all_engine_barrier()

    def sb(self, name, shape, dt=F32):
        return self.stack.enter_context(self.nc.sbuf_tensor(f"{self.stage}_{name}", shape, dt))

    def ps(self, name, shape, dt=F32):
        return self.stack.enter_context(self.nc.psum_tensor(f"{self.stage}_{name}", shape, dt))

    def sem(self, name):
        sem = self.nc.alloc_semaphore(f"{self.stage}_{name}")
        self.sems.append(sem)
        return sem



def constants(nc, m, c):
    c.ident = m.sb("ident", [P, P])
    c.ident16 = m.sb("ident16", [P, P], BF16)
    c.big16 = m.sb("big16", [P, 4, P], BF16)
    c.lane = m.sb("lane", [P, P])
    c.lanei = m.sb("lanei", [P, P], I32)
    c.tri = m.sb("tri", [P, P])
    c.ones = m.sb("ones", [P, P])
    c.zero = m.sb("zero", [P, 1])
    c.minus_half = m.sb("minus_half", [P, 1])
    c.valid = m.sb("valid", [P, 2])
    s_made = m.sem("made")
    with nc.Block() as block:
        @block.gpsimd
        def _(pool):
            link = Link(pool, s_made)
            link(pool.memset(c.ident[:, :], 0.0))
            link(pool.affine_select(out=c.ident[:, :], in_=c.ident[:, :], compare_op=ALU.not_equal, fill=1.0,
                                    base=0, pattern=[[-1, P]], channel_multiplier=1))
            link(pool.tensor_copy(c.ident16[:, :], c.ident[:, :]))
            for h in range(4):
                link(pool.tensor_scalar(c.big16[:, h, :], c.ident[:, :], BIG, None, ALU.mult))
            link(pool.memset(c.ones[:, :], 1.0))
            link(pool.memset(c.zero[:, :], 0.0))
            link(pool.memset(c.minus_half[:, :], -0.5))
            link(pool.affine_select(out=c.tri[:, :], in_=c.ones[:, :], compare_op=ALU.is_gt, fill=0.0,
                                    base=0, pattern=[[1, P]], channel_multiplier=-1))
            link(pool.iota(c.lanei[:, :], pattern=[[1, P]], base=0, channel_multiplier=0))
            link(pool.tensor_copy(c.lane[:, :], c.lanei[:, :]))
            link(pool.memset(c.valid[:, :], 0.0))
            link(pool.affine_select(out=c.valid[:, 0:1], in_=c.ones[:, 0:1], compare_op=ALU.is_gt, fill=0.0,
                                    base=VALID, pattern=[[0, 1]], channel_multiplier=-1))



def sort_edges(nc, c, stage, key_d, other_d, records_d, keep):
    with ExitStack() as stack:
        m = Memory(nc, stack, stage)
        key = m.sb("key", [EP, EC], I32)
        other = m.sb("other", [EP, EC], I32)
        winf = m.sb("winf", [EP, EC])
        hit = m.sb("hit", [EP, EC])
        run = m.sb("run", [EP, EC])
        rank = m.sb("rank", [EP, EC])
        post = m.sb("post", [EP, EC, 3], I32)
        staged = m.sb("staged", [EP, 2, SB, 3], I32)
        empty = m.sb("empty", [P, NSLOT, 2], I32)
        back = m.sb("back", [P, NSLOT, 2], I32)
        total = m.sb("total", [P, WIN])
        offset = m.sb("offset", [P, WIN])
        groups = m.sb("groups", [P, WIN])
        groupsi = m.sb("groupsi", [P, WIN], I32)
        ends = m.sb("ends", [P, WIN])
        numberi = m.sb("numberi", [P, NG], I32)
        number = m.sb("number", [P, NG])
        windowf = m.sb("windowf", [P, NG])
        ps = m.ps("sums", [P, 2, 256])
        s_in, s_fill, s_back = m.sem("in"), m.sem("fill"), m.sem("back")
        s_pool, s_dve, s_total, s_summed = m.sem("pool"), m.sem("dve"), m.sem("total"), m.sem("summed")
        s_staged, s_scattered = m.sem("staged"), [m.sem(f"scattered{h}") for h in range(2)]
        s_loop, s_base, s_passed = m.sem("loop"), m.sem("base"), m.sem("passed")
        TURNS = EC // (2 * SB)
        A, B = 5, 2

        with nc.Block() as block:
            @block.sync
            def _(sp):
                sp.dma_start(key[:, :], key_d.rearrange("(p c) -> p c", p=EP)).then_inc(s_in, 16)
                sp.dma_start(other[:, :], other_d.rearrange("(p c) -> p c", p=EP)).then_inc(s_in, 16)
                sp.wait_ge(s_pool, 3)
                sp.dma_start(records_d, empty[:, :, :]).then_inc(s_fill, 16)
                for h in range(2):
                    sp.wait_ge(s_scattered[h], 16 * SB * TURNS)
                sp.dma_start(back[:, :, :], records_d).then_inc(s_back, 16)

            @block.gpsimd
            def _(pool):
                pool.memset(empty[:, :, 0:1], PAD_ROW).then_inc(s_pool, 1)
                pool.memset(empty[:, :, 1:2], -1).then_inc(s_pool, 1)
                pool.iota(numberi[:, :], pattern=[[1, NG]], base=0, channel_multiplier=0).then_inc(s_pool, 1)
                pool.wait_ge(s_fill, 16)
                with pool.Fori(0, TURNS) as i:
                    for h in range(2):
                        apart(pool, s_staged, i * 2 + (h + 1), s_passed)
                        for j in range(SB):
                            pool.indirect_dma_start(
                                out=records_d.rearrange("p s r -> (p s) r"),
                                out_offset=bass.IndirectOffsetOnAxis(ap=staged[:, h, j, 0:1], axis=0),
                                in_=staged[:, h, j, 1:3], in_offset=None).then_inc(s_scattered[h], 16)

            @block.tensor
            def _(pe):
                pe.wait_ge(s_total, 1)
                pe.matmul(ps[0:EP, 0, 0:WIN], c.tri[0:EP, 0:EP], total[0:EP, :], start=True, stop=True)
                pe.matmul(ps[:, 1, 0:WIN], c.ones[0:EP, :], total[0:EP, :], start=True, stop=True).then_inc(s_summed, 1)

            @block.vector
            def _(dve):
                link = Link(dve, s_dve)
                dve.wait_ge(s_in, 32)
                link(dve.tensor_single_scalar(post[:, :, 0], key[:, :], 7, ALU.arith_shift_right))
                link(dve.tensor_copy(winf[:, :], post[:, :, 0]))
                link(dve.memset(rank[:, :], 0.0))
                with dve.Fori(0, WIN) as w:
                    wcol = c.lane[0:EP, bass.ds(w, 1)]
                    dve.tensor_scalar(hit[:, :], winf[:, :], wcol, None, ALU.is_equal).then_inc(s_loop, 1)
                    dve.wait_ge(s_loop, w * A + 1)
                    dve.tensor_tensor_scan(run[:, :], hit[:, :], bc(c.zero[0:EP, :], [EP, EC]), 0.0, ALU.add, ALU.add).then_inc(s_loop, 1)
                    dve.wait_ge(s_loop, w * A + 2)
                    dve.tensor_copy(total[0:EP, bass.ds(w, 1)], run[:, EC - 1:EC]).then_inc(s_loop, 1)
                    dve.tensor_tensor(hit[:, :], hit[:, :], run[:, :], ALU.mult).then_inc(s_loop, 1)
                    dve.wait_ge(s_loop, w * A + 4)
                    dve.tensor_tensor(rank[:, :], rank[:, :], hit[:, :], ALU.add).then_inc(s_loop, 1)
                    dve.wait_ge(s_loop, w * A + 5)
                dve.memset(windowf[:, :], 0.0).then_inc(s_total, 1)
                dve.wait_ge(s_summed, 1)
                link(dve.tensor_scalar(groups[:, :], ps[:, 1, 0:WIN], float(GE - 1), None, ALU.add))
                link(dve.tensor_copy(groupsi[:, :], groups[:, :]))
                link(dve.tensor_single_scalar(groupsi[:, :], groupsi[:, :], GE.bit_length() - 1, ALU.arith_shift_right))
                link(dve.tensor_copy(groups[:, :], groupsi[:, :]))
                link(dve.tensor_tensor_scan(ends[:, :], groups[:, :], bc(c.zero[:, :], [P, WIN]), 0.0, ALU.add, ALU.add))
                link(dve.tensor_tensor(offset[:, :], ends[:, :], groups[:, :], ALU.subtract))
                link(dve.tensor_scalar(offset[:, :], offset[:, :], float(GE), -1.0, ALU.mult, ALU.add))
                link(dve.tensor_tensor(offset[0:EP, :], offset[0:EP, :], ps[0:EP, 0, 0:WIN], ALU.add))
                with dve.Fori(0, WIN) as w:
                    dve.tensor_scalar(hit[:, :], winf[:, :], c.lane[0:EP, bass.ds(w, 1)], offset[0:EP, bass.ds(w, 1)],
                                      ALU.is_equal, ALU.mult).then_inc(s_base, 1)
                    dve.wait_ge(s_base, w * B + 1)
                    dve.tensor_tensor(rank[:, :], rank[:, :], hit[:, :], ALU.add).then_inc(s_base, 1)
                    dve.wait_ge(s_base, w * B + 2)
                link(dve.tensor_copy(post[:, :, 1], rank[:, :]))
                link(dve.tensor_single_scalar(post[:, :, 2], post[:, :, 1], 7, ALU.arith_shift_right))
                link(dve.tensor_copy(run[:, :], post[:, :, 2]))
                link(dve.scalar_tensor_tensor(hit[:, :], run[:, :], -float(P), rank[:, :], ALU.mult, ALU.add))
                link(dve.scalar_tensor_tensor(hit[:, :], hit[:, :], float(NSLOT), run[:, :], ALU.mult, ALU.add))
                link(dve.tensor_copy(post[:, :, 0], hit[:, :]))
                link(dve.tensor_copy(post[:, :, 1], other[:, :]))
                link(dve.tensor_copy(post[:, :, 2], key[:, :]))

                def stage(h, col, count):
                    dve.tensor_copy(staged[:, h, :, :], post[:, col, :]).then_inc(s_staged, 1)

                for h in range(2):
                    dve.tensor_copy(staged[:, h, :, :], post[:, h * SB:(h + 1) * SB, :]).then_inc(s_staged, 1)
                dve.wait_ge(s_pool, 3)
                link(dve.tensor_copy(number[:, :], numberi[:, :]))
                for w in range(WIN):
                    link(dve.scalar_tensor_tensor(windowf[:, :], number[:, :], ends[:, w:w + 1], windowf[:, :], ALU.is_ge, ALU.add))
                link(dve.memset(keep.window[:, :], WIN))
                link(dve.tensor_copy(keep.window[:, LEAD:LEAD + NG], windowf[:, :]))
                with dve.Fori(1, TURNS) as i:
                    for h in range(2):
                        dve.wait_ge(s_scattered[h], i * (16 * SB))
                        dve.tensor_copy(staged[:, h, :, :], post[:, bass.ds(i * (2 * SB) + h * SB, SB), :]).then_inc(s_staged, 1)
                dve.wait_ge(s_back, 16)
                link(dve.memset(keep.row[:, NSLOT:], PAD_ROW))
                link(dve.tensor_copy(keep.row[:, 0:NSLOT], back[:, :, 0]))
                link(dve.tensor_copy(keep.place[:, :], back[:, :, 1]))
                link(dve.scalar_tensor_tensor(
                    keep.place[:, :].rearrange("p (g j) -> p g j", j=2), bc(windowf[:, :].rearrange("p (g j) -> p g j", j=1), [P, NG, 2]),
                    -float(P), keep.place[:, :].rearrange("p (g j) -> p g j", j=2), ALU.mult, ALU.add))



def linear(nc, c, stage, sources, weights, bias, width, drain_v, drain_a, table=None, table_width=0, table_by=""):
    with ExitStack() as stack:
        m = Memory(nc, stack, stage)
        K = len(sources)
        turned = m.sb("turned", [P, 2, K, P])
        fetched = m.sb("fetched", [P, 2, K, P])
        tile = m.sb("tile", [P, 2, max(table_width, 1)])
        ps_t = [m.ps(f"ps_t{b}", [P, 512]) for b in range(2)]
        banks = -(-width // 512)
        ps_o = [m.ps(f"ps_o{b}", [P, banks * 512]) for b in range(2)]
        s_fetched, s_t, s_turned, s_product, s_v, s_a, s_passed = (m.sem(x) for x in ("fetched", "t", "turned", "product", "v", "a", "passed"))
        s_stored = [m.sem(f"stored{b}") for b in range(2)]
        cuts = [(a, min(a + 512, width)) for a in range(0, width, 512)]

        with nc.Block() as block:
            @block.tensor
            def _(pe):
                def turn(w, b):
                    wait(pe, s_turned, w - 1)
                    apart(pe, s_fetched, w + 1, s_passed)
                    for k, (x, c0, n) in enumerate(sources):
                        last = pe.transpose(ps_t[b][0:n, k * P:(k + 1) * P], fetched[:, b, k, 0:n], c.ident[:, :])
                    last.then_inc(s_t, 1)

                def product(w, b):
                    pe.wait_ge(s_turned, w + 1)
                    wait(pe, s_v, w - 1)
                    if drain_a is not None:
                        wait(pe, s_a, w - 1)
                    for a0, a1 in cuts:
                        for k, (x, c0, n) in enumerate(sources):
                            last = pe.matmul(ps_o[b][:, a0:a1], turned[0:n, b, k, :], weights[k][0:n, a0:a1],
                                             start=k == 0, stop=k == K - 1 and bias is None)
                        if bias is not None:
                            last = pe.matmul(ps_o[b][:, a0:a1], c.ones[0:1, :], bias[0:1, a0:a1], start=False, stop=True)
                    last.then_inc(s_product, 1)

                turn(0, 0)
                turn(1, 1)
                product(0, 0)
                turn(2, 0)
                product(1, 1)
                with pe.Fori(1, NW // 2 - 1) as i:
                    turn(i * 2 + 1, 1)
                    product(i * 2, 0)
                    turn(i * 2 + 2, 0)
                    product(i * 2 + 1, 1)
                turn(NW - 1, 1)
                product(NW - 2, 0)
                product(NW - 1, 1)

            @block.scalar
            def _(act):
                def copy(w, b):
                    act.wait_ge(s_t, w + 1)
                    wait(act, s_product, w - 1)
                    for k, (x, c0, n) in enumerate(sources):
                        last = act.activation(turned[0:n, b, k, :], ps_t[b][0:n, k * P:(k + 1) * P], ACT.Copy)
                    last.then_inc(s_turned, 1)

                def drain(w, b):
                    if drain_a is None:
                        return
                    act.wait_ge(s_product, w + 1)
                    if "a" in table_by:
                        wait(act, s_stored[b], (w // 2) * 16 if isinstance(w, int) else (w - b) * 8)
                    drain_a(act, ps_o[b], w, tile[:, b, :]).then_inc(s_a, 1)

                copy(0, 0)
                copy(1, 1)
                drain(0, 0)
                copy(2, 0)
                drain(1, 1)
                with act.Fori(1, NW // 2 - 1) as i:
                    copy(i * 2 + 1, 1)
                    drain(i * 2, 0)
                    copy(i * 2 + 2, 0)
                    drain(i * 2 + 1, 1)
                copy(NW - 1, 1)
                drain(NW - 2, 0)
                drain(NW - 1, 1)

            @block.vector
            def _(dve):
                def drain(w, b):
                    dve.wait_ge(s_a if drain_a is not None else s_product, w + 1)
                    if "v" in table_by:
                        wait(dve, s_stored[b], (w // 2) * 16 if isinstance(w, int) else (w - b) * 8)
                    drain_v(dve, ps_o[b], w, tile[:, b, :]).then_inc(s_v, 1)

                def fetch(w, b):
                    wait(dve, s_t, w - 1)
                    for k, (x, c0, n) in enumerate(sources):
                        last = dve.tensor_copy(fetched[:, b, k, 0:n], x[:, bass.ds(w, 1), c0:c0 + n].rearrange("p a n -> p (a n)"))
                    last.then_inc(s_fetched, 1)

                fetch(0, 0)
                fetch(1, 1)
                fetch(2, 0)
                drain(0, 0)
                fetch(3, 1)
                drain(1, 1)
                with dve.Fori(1, NW // 2 - 1) as i:
                    fetch(i * 2 + 2, 0)
                    drain(i * 2, 0)
                    fetch(i * 2 + 3, 1)
                    drain(i * 2 + 1, 1)
                drain(NW - 2, 0)
                drain(NW - 1, 1)

            if table is not None:
                rows = table.rearrange("(w p) n -> w p n", p=P)

                @block.sync
                def _(sp):
                    def store(w, b):
                        if "v" in table_by:
                            sp.wait_ge(s_v, w + 1)
                        if "a" in table_by:
                            sp.wait_ge(s_a, w + 1)
                        sp.dma_start(rows[bass.ds(w, 1), :, :].rearrange("w p n -> (w p) n"), tile[:, b, 0:table_width]).then_inc(s_stored[b], 16)

                    with sp.Fori(0, NW // 2) as i:
                        store(i * 2, 0)
                        store(i * 2 + 1, 1)
                    for b in range(2):
                        sp.wait_ge(s_stored[b], 16 * (NW // 2))



class EdgeSemaphores:

    def __init__(self, m):
        self.index = m.sem("index")
        self.onehot = m.sem("onehot")
        self.transposed = m.sem("transposed")
        self.turned = m.sem("turned")
        self.at_node = m.sem("at_node")
        self.product = m.sem("product")
        self.logit = m.sem("logit")
        self.logit16 = m.sem("logit16")
        self.spread = m.sem("spread")
        self.before = m.sem("before")
        self.peak = m.sem("peak")
        self.drop = m.sem("drop")
        self.kept = m.sem("kept")
        self.fade = m.sem("fade")
        self.at_peak = m.sem("at_peak")
        self.argument = m.sem("argument")
        self.weight = m.sem("weight")
        self.summand = m.sem("summand")
        self.summed = m.sem("summed")
        self.faded = m.sem("faded")
        self.added = m.sem("added")
        self.ready = m.sem("ready")
        self.passed = m.sem("passed")
        self.distance = m.sem("distance")
        self.passed_dve = m.sem("passed_dve")


def edge_pass(nc, c, stage, order, table, width, acc, R, kind, H=1, C=0, node=None, node_c0=0, value_c0=0, count=False, biggest=None, slots=8):
    with ExitStack() as stack:
        m = Memory(nc, stack, stage)
        GS = slots
        guarded = kind in ("gat", "dot")
        weighted = kind != "sum"
        dot = kind == "dot"
        HC = H * C
        OS = UN if weighted else 4
        index = m.sb("index", [P, GS, 2], I32)
        rows = m.sb("rows", [P, GS, 2, width])
        onehot = m.sb("onehot", [P, OS, 2, P])
        if weighted:
            turned = m.sb("turned", [P, 4, 2, P])
            logit = m.sb("logit", [P, 4, 2, H])
            summand = m.sb("summand", [P, 2, 2, R])
            product = m.sb("product", [P, 2, HC if dot else H])
            ps_t = m.ps("ps_t", [P, 2, 256])
            ps_n = m.ps("ps_n", [P, 2, 256])
        if guarded:
            distance = m.sb("distance", [P, 2, P])
            away = m.sb("away", [P, 4, 2, P], BF16)
            logit16 = m.sb("logit16", [P, 2, 2, H], BF16)
            before = m.sb("before", [P, 2, H])
            peak = m.sb("peak", [P, 4, H])
            drop = m.sb("drop", [P, 2, H])
            fade = m.sb("fade", [P, 4, H])
            argument = m.sb("argument", [P, 2, 2, H])
            ps_m = m.ps("ps_m", [P, max(H, 2), 2, P])
            ps_e = m.ps("ps_e", [P, 2, 256])
        if dot:
            turned16 = m.sb("turned16", [P, 2, 2, P], BF16)
        ps_u = m.ps("ps_u", [P, 512])
        s = EdgeSemaphores(m)
        s_rows = [m.sem(f"rows{g}") for g in range(GS)]
        freed = s.summand if weighted else s.summed

        def arrived(eng, g):
            eng.wait_ge(s_rows[g.slot(GS)], g.turn(GS) * 32 + 32)

        def steps(eng, stages, engine_type=None):
            most = max(lag for lag, _ in stages)

            def turn(i, k0=0, k1=UN):
                windows = None
                if engine_type is not None:
                    _, windows = nc.values_load_multi_w_load_instructions(
                        order.window[0:1, bass.ds(i * UN, UN + LEAD)], engines=(engine_type,), min_val=0, max_val=NW - 1,
                        skip_runtime_bounds_check_because="a window's number is a count of windows, at most WIN")
                for k in range(k0, k1):
                    for lag, what in stages:
                        g = Group(i, k - lag, windows)
                        if g.exists():
                            what(g)

            turn(0)
            with eng.Fori(1, NG // UN) as i:
                turn(i)
            turn(NG // UN, 0, most)

        with nc.Block() as block:
            @block.gpsimd
            def _(pool):
                def gather(g):
                    wait(pool, freed, g.plus(1 - GS))
                    apart(pool, s.index, g.plus(1), s.passed)
                    for j in range(2):
                        pool.indirect_dma_start(
                            out=rows[:, g.slot(GS), j, :], out_offset=None, in_=table,
                            in_offset=bass.IndirectOffsetOnAxis(ap=index[:, g.slot(GS), j:j + 1], axis=0),
                        ).then_inc(s_rows[g.slot(GS)], 16)

                steps(pool, [(0, gather)])

            @block.tensor
            def _(pe):
                def transpose(g):
                    pe.wait_ge(s.onehot, g.plus(1))
                    wait(pe, s.turned, g.plus(0))
                    for j in range(2):
                        last = pe.transpose(ps_t[:, j, 0:P], onehot[:, g.slot(OS), j, :], c.ident[:, :])
                    last.then_inc(s.transposed, 1)

                def of_node(g):
                    pe.wait_ge(s.turned, g.plus(1))
                    wait(pe, s.product, g.plus(0))
                    if not dot:
                        arrived(pe, g)
                    for j in range(2):
                        if dot:
                            for part in range(3):
                                last = pe.matmul(ps_n[:, j, 0:HC], turned16[:, g.slot(2), j, :],
                                                 node[:, bass.ds(g.window * 3 + part, 1), :].rearrange("p a n -> p (a n)"),
                                                 start=part == 0, stop=part == 2)
                        else:
                            pe.matmul(ps_n[:, j, 0:H], turned[:, g.slot(4), j, :],
                                      node[:, bass.ds(g.window, 1), node_c0:node_c0 + H].rearrange("p a n -> p (a n)"), start=True, stop=False)
                            last = pe.matmul(ps_n[:, j, 0:H], c.ident[:, :], rows[:, g.slot(GS), j, HC:HC + H], start=False, stop=True)
                    last.then_inc(s.at_node, 1)

                def spread(g):
                    pe.wait_ge(s.logit16, g.plus(1))
                    wait(pe, s.peak, g.plus(0))
                    for h in range(H):
                        for j in range(2):
                            last = pe.matmul(ps_m[:, h, j, :], bc(logit16[:, g.slot(2), j, h:h + 1], [P, P]), c.ident16[:, :],
                                             start=True, stop=True)
                    last.then_inc(s.spread, 1)

                def of_peak(g):
                    pe.wait_ge(s.peak, g.plus(1))
                    wait(pe, s.argument, g.plus(0))
                    for j in range(2):
                        last = pe.matmul(ps_e[:, j, 0:H], turned[:, g.slot(4), j, :], peak[:, g.slot(4), :], start=True, stop=True)
                    last.then_inc(s.at_peak, 1)

                def sum_edges(g):
                    if weighted:
                        pe.wait_ge(s.summand, g.plus(1))
                    else:
                        pe.wait_ge(s.onehot, g.plus(1))
                        arrived(pe, g)
                    wait(pe, s.added, g.plus(0))
                    for j in range(2):
                        rhs = summand[:, g.slot(2), j, :] if weighted else rows[:, g.slot(GS), j, 0:R]
                        last = pe.matmul(ps_u[:, 0:R], onehot[:, g.slot(OS), j, :], rhs, start=j == 0, stop=j == 1)
                    last.then_inc(s.summed, 1)

                if guarded:
                    steps(pe, [(1, transpose), (4, of_peak), (3, spread), (2, of_node), (5, sum_edges)], mybir.EngineType.PE)
                elif weighted:
                    steps(pe, [(1, transpose), (2, of_node), (4, sum_edges)], mybir.EngineType.PE)
                else:
                    steps(pe, [(0, sum_edges)])

            @block.scalar
            def _(act):
                def mark(g):
                    wait(act, s.onehot, g.plus(0))
                    for j in range(2):
                        act.activation(distance[:, j, :], c.lane[:, :], ACT.Abs, scale=-1.0,
                                       bias=order.place[:, bass.ds(g.plus(0) * 2 + j, 1)]).then_inc(s.distance, 1)
                    wait(act, s.summed, g.plus(1 - OS))
                    act.wait_ge(s.distance, g.plus(1) * 2)
                    act.activation(onehot[:, g.slot(OS), :, :], distance[:, :, :], ACT.Relu, scale=-1.0, bias=1.0).then_inc(s.onehot, 1)

                def weight(g):
                    w = summand[:, g.slot(2), :, 0:H * (C + 1)].rearrange("p j (h c) -> p j h c", h=H)[:, :, :, C]
                    wait(act, s.summed, g.plus(-1))
                    if guarded:
                        act.wait_ge(s.argument, g.plus(1))
                        act.activation(w, argument[:, g.slot(2), :, :], ACT.Exp).then_inc(s.weight, 1)
                    else:
                        act.wait_ge(s.logit, g.plus(1))
                        act.activation(w, logit[:, g.slot(4), :, :], ACT.Exp, scale=-1.0).then_inc(s.weight, 1)

                def fading(g):
                    act.wait_ge(s.drop, g.plus(1))
                    wait(act, s.faded, g.plus(-3))
                    act.activation(fade[:, g.slot(4), :], drop[:, g.slot(2), :], ACT.Exp).then_inc(s.fade, 1)

                def copy(g):
                    act.wait_ge(s.transposed, g.plus(1))
                    wait(act, s.at_peak if guarded else s.at_node, g.plus(-3))
                    if guarded:
                        wait(act, s.peak, g.plus(-3))
                        act.activation(away[:, g.slot(4), :, :], ps_t[:, :, 0:P], ACT.Copy, scale=BIG, bias=-BIG)
                    if dot:
                        wait(act, s.at_node, g.plus(-1))
                        act.activation(turned16[:, g.slot(2), :, :], ps_t[:, :, 0:P], ACT.Copy)
                    act.activation(turned[:, g.slot(4), :, :], ps_t[:, :, 0:P], ACT.Copy).then_inc(s.turned, 1)

                if guarded:
                    steps(act, [(1, copy), (0, mark), (4, fading), (4, weight)])
                elif weighted:
                    steps(act, [(1, copy), (3, weight)])

            @block.vector
            def _(dve):
                def stage_index(g):
                    dve.tensor_copy(index[:, g.slot(GS), :], order.row[:, bass.ds(g.plus(GS) * 2, 2)]).then_inc(s.index, 1)

                def mark(g):
                    wait(dve, s.summed, g.plus(1 - OS))
                    dve.tensor_tensor(onehot[:, g.slot(OS), :, :], bc(c.lane[:, :].rearrange("p (j n) -> p j n", j=1), [P, 2, P]),
                                      bc(order.place[:, bass.ds(g.plus(0) * 2, 2)].rearrange("p (j n) -> p j n", n=1), [P, 2, P]),
                                      ALU.is_equal).then_inc(s.onehot, 1)

                def logits(g):
                    dve.wait_ge(s.at_node, g.plus(1))
                    arrived(dve, g)
                    stage_index(g)
                    to = logit[:, g.slot(4), :, :]
                    if dot:
                        dve.tensor_tensor(product[:, :, :], ps_n[:, :, 0:HC], rows[:, g.slot(GS), :, 0:HC], ALU.mult).then_inc(s.product, 1)
                        dve.wait_ge(s.product, g.plus(1))
                        dve.tensor_reduce(to, product[:, :, :].rearrange("p j (h c) -> p j h c", h=H), AX.X, ALU.add).then_inc(s.logit, 1)
                    else:
                        wait(dve, s.logit, g.plus(0))
                        dve.tensor_scalar(product[:, :, :], ps_n[:, :, 0:H], 1.0, None, ALU.mult).then_inc(s.product, 1)
                        dve.wait_ge(s.product, g.plus(1))
                        dve.scalar_tensor_tensor(to, product[:, :, :], 0.2, product[:, :, :], ALU.mult, ALU.max).then_inc(s.logit, 1)
                    if guarded:
                        dve.wait_ge(s.logit, g.plus(1))
                        dve.tensor_scalar(logit16[:, g.slot(2), :, :], to, CLIP, -CLIP, ALU.min, ALU.max).then_inc(s.logit16, 1)

                def maximum(g):
                    now = biggest[:, bass.ds(g.window, 1), 0:H].rearrange("p a h -> p (a h)")
                    wait(dve, s.kept, g.plus(0))
                    dve.tensor_scalar(before[:, g.slot(2), :], now, 1.0, None, ALU.mult).then_inc(s.before, 1)
                    apart(dve, s.before, g.plus(1), s.passed_dve)
                    apart(dve, s.spread, g.plus(1), s.passed_dve)
                    for h in range(H):
                        last = dve.tensor_tensor_reduce(out=ps_m[:, h, :, :], in0=ps_m[:, h, :, :], in1=away[:, g.slot(4), :, :], scale=1.0,
                                                        scalar=before[:, g.slot(2), h:h + 1], op0=ALU.add, op1=ALU.max,
                                                        accum_out=peak[:, g.slot(4), h:h + 1])
                    last.then_inc(s.peak, 1)
                    dve.wait_ge(s.peak, g.plus(1))
                    dve.tensor_tensor(drop[:, g.slot(2), :], before[:, g.slot(2), :], peak[:, g.slot(4), :], ALU.subtract).then_inc(s.drop, 1)
                    dve.tensor_scalar(now, peak[:, g.slot(4), :], 1.0, None, ALU.mult).then_inc(s.kept, 1)

                def subtract(g):
                    dve.wait_ge(s.at_peak, g.plus(1))
                    dve.tensor_tensor(argument[:, g.slot(2), :, :], logit[:, g.slot(4), :, :], ps_e[:, :, 0:H], ALU.subtract).then_inc(s.argument, 1)

                def weigh(g):
                    dve.wait_ge(s.weight, g.plus(1))
                    out = summand[:, g.slot(2), :, 0:H * (C + 1)].rearrange("p j (h c) -> p j h c", h=H)
                    dve.tensor_tensor(out[:, :, :, 0:C], rows[:, g.slot(GS), :, value_c0:value_c0 + HC].rearrange("p j (h c) -> p j h c", h=H),
                                      bc(out[:, :, :, C:C + 1], [P, 2, H, C]), ALU.mult).then_inc(s.summand, 1)

                def add(g):
                    wait(dve, s.added, g.plus(0))
                    at = g.window * R
                    mine = acc[:, bass.ds(at, R)]
                    if guarded:
                        dve.wait_ge(s.fade, g.plus(1))
                        part = acc[:, bass.ds(at, H * (C + 1))].rearrange("p (h c) -> p h c", h=H)
                        dve.tensor_tensor(part, part, bc(fade[:, g.slot(4), :].rearrange("p (h c) -> p h c", c=1), [P, H, C + 1]), ALU.mult).then_inc(s.faded, 1)
                        dve.wait_ge(s.faded, g.plus(1))
                    dve.wait_ge(s.summed, g.plus(1))
                    dve.tensor_tensor(mine, mine, ps_u[:, 0:R], ALU.add).then_inc(s.added, 1)
                    if not weighted:
                        stage_index(g)

                for k in range(GS):
                    dve.tensor_copy(index[:, k, :], order.row[:, 2 * k:2 * k + 2]).then_inc(s.index, 1)
                if count:
                    dve.memset(summand[:, :, :, R - 1:R], 1.0).then_inc(s.ready, 1)
                    dve.wait_ge(s.ready, 1)
                if guarded:
                    steps(dve, [(4, maximum), (3, logits), (6, add), (4, subtract), (5, weigh)], mybir.EngineType.DVE)
                elif weighted:
                    steps(dve, [(0, mark), (3, logits), (5, add), (4, weigh)], mybir.EngineType.DVE)
                else:
                    steps(dve, [(0, mark), (2, add)], mybir.EngineType.DVE)



def all_windows(x, n=D):
    return x[:, 0:NW * n].rearrange("p (w n) -> p w n", n=n)


def keep_valid(link, dve, c, x):
    n = x.shape[2]
    link(dve.tensor_tensor(x[:, LAST:NW, :], x[:, LAST:NW, :], bc(c.valid[:, :].rearrange("p (w n) -> p w n", n=1), [P, 2, n]), ALU.mult))


def normalize(link, dve, c, x, scratch, small):
    mean, var = small[:, 0, :], small[:, 1, :]

    def wide(a):
        return bc(a.rearrange("p (w n) -> p w n", n=1), [P, NW, D])

    link(dve.tensor_reduce(mean, x, AX.X, ALU.add))
    link(dve.tensor_scalar(mean, mean, 1.0 / D, None, ALU.mult))
    link(dve.tensor_tensor(x, x, wide(mean), ALU.subtract))
    link(dve.tensor_tensor(scratch, x, x, ALU.mult))
    link(dve.tensor_reduce(var, scratch, AX.X, ALU.add))
    link.asked(dve.tensor_scalar(var, var, 1.0 / D, EPS, ALU.mult, ALU.add))
    link(dve.tensor_tensor(x, x, wide(var), ALU.mult))
    keep_valid(link, dve, c, x)


def inverse_root(pool, minus_half, x):
    return pool.tensor_tensor(x, x, bc(minus_half, [P, x.shape[1]]), ALU.pow)


def on_vector(nc, c, stage, loads, work, root=None):
    with ExitStack() as stack:
        m = Memory(nc, stack, stage)
        s_loaded, s_step, s_ask, s_root = (m.sem(x) for x in ("loaded", "step", "ask", "root"))
        with nc.Block() as block:
            if root is not None:
                @block.gpsimd
                def _(pool):
                    pool.wait_ge(s_ask, 1)
                    inverse_root(pool, c.minus_half[:, :], root).then_inc(s_root, 1)

            @block.sync
            def _(sp):
                for to, frm in loads:
                    sp.dma_start(to, frm).then_inc(s_loaded, 16)

            @block.vector
            def _(dve):
                if loads:
                    dve.wait_ge(s_loaded, 16 * len(loads))
                link = Link(dve, s_step)

                def asked(ins):
                    ins.then_inc(s_ask, 1)
                    dve.wait_ge(s_root, 1)

                link.asked = asked
                work(link, dve)


def row(v):
    return v.rearrange("(a n) -> a n", a=1)


def spread_row(v, n):
    return row(v).to_broadcast([P, n]) if len(v.shape) == 1 else v.to_broadcast([P, n])


def fold(link, dve, w, c0, a, H, C, to, scratch):
    n = H * C
    for k in range(2):
        link(dve.tensor_tensor(scratch[:, 0:n], w[:, k, c0:c0 + n], a, ALU.mult))
        link(dve.tensor_reduce(w[:, k, to:to + H], scratch[:, 0:n].rearrange("p (h c) -> p h c", h=H), AX.X, ALU.add))


def by_chunk(w):
    return w.rearrange("(k p) n -> p k n", p=P)


class Keep:
    pass


def gnn_kernel(nc, x, src, dst,
               a_w1, a_as1, a_ad1, a_b1, a_w2, a_as2, a_ad2, a_b2, a_wf, a_bf,
               b_w1, b_a1, b_w2, b_a2,
               t_wq, t_bq, t_wk, t_bk, t_wv, t_bv, t_wo, t_bo,
               g_w1, g_b1, g_g1, g_be1, g_w2, g_b2, g_g2, g_be2, g_wfc, g_bfc, out):
    records = [nc.dram_tensor(f"records_{n}", [P, NSLOT, 2], I32, kind="Internal").ap() for n in ("dst", "src")]
    tables = {n: nc.dram_tensor(f"table_{n}", [NPAD, n], F32, kind="Internal").ap() for n in (264, 66, 258, 512, 128, 64)}

    def drain(eng, to, frm, scale=1.0):
        if eng is nc.vector or not hasattr(eng, "activation"):
            return eng.tensor_copy(to, frm)
        return eng.activation(to, frm, ACT.Copy, scale=scale)

    with ExitStack() as stack:
        m = Memory(nc, stack, "all")
        c = Keep()
        constants(nc, m, c)
        order = Keep()
        order.row = m.sb("row", [P, NSLOT + 2 * UN], I32)
        order.place = m.sb("place", [P, NSLOT])
        order.window = m.sb("window", [P, WT], I32)
        kept = {n: (nc.dram_tensor(f"kept_row_{n}", [P, NSLOT + 2 * UN], I32, kind="Internal").ap(),
                    nc.dram_tensor(f"kept_place_{n}", [P, NSLOT], F32, kind="Internal").ap(),
                    nc.dram_tensor(f"kept_window_{n}", [P, WT], I32, kind="Internal").ap()) for n in ("dst", "src")}

        def move_order(name, load):
            s_moved = m.sem(f"moved_{name}_{load}")
            with nc.Block() as block:
                @block.sync
                def _(sp):
                    for d, t in zip(kept[name], (order.row, order.place, order.window)):
                        to, frm = (t[:, :], d) if load else (d, t[:, :])
                        sp.dma_start(to, frm).then_inc(s_moved, 16)
                    sp.wait_ge(s_moved, 48)

        sort_edges(nc, c, "by_src", src, dst, records[1], order)
        move_order("src", False)
        sort_edges(nc, c, "by_dst", dst, src, records[0], order)
        move_order("dst", False)

        acc = m.sb("acc", [P, NW * 264])
        both = m.sb("both", [P, 2 * NW * D])
        Y, X = both[:, 0:NW * D], both[:, NW * D:2 * NW * D]
        x_kept = nc.dram_tensor("x_kept", [P, NW * D], F32, kind="Internal").ap()
        nodes = m.sb("nodes", [P, NW, 8])
        biggest = m.sb("biggest", [P, NW, 8])
        small = m.sb("small", [P, 2, NW])
        degree = m.sb("degree", [P, NW])
        x3, y3 = all_windows(X), all_windows(Y)

        def wide(a, *shape):
            return bc(a, [P, NW, *shape])

        def at(t, w, n, c0=0, c1=None):
            return t[:, bass.ds(w * n + c0, (n if c1 is None else c1) - c0)]

        with ExitStack() as st:
            mm = Memory(nc, st, "a1")
            W = mm.sb("W", [P, 2, 264])
            avec = mm.sb("avec", [P, 2, 256])
            tmp = mm.sb("tmp", [P, 256])

            def work(link, dve):
                fold(link, dve, W, 0, avec[:, 0, :], 4, 64, 256, tmp)
                fold(link, dve, W, 0, avec[:, 1, :], 4, 64, 260, tmp)

            def zero(link, dve):
                link(dve.memset(x3[:, LAST:NW, :], 0.0))

            on_vector(nc, c, "a1z", [], zero)
            on_vector(nc, c, "a1w", [
                (x3[:, 0:LAST, :], x[0:LAST * P, :].rearrange("(w p) n -> p w n", p=P)),
                (X[0:VALID, LAST * D:(LAST + 1) * D], x[LAST * P:N, :]),
                (W[:, :, 0:256], by_chunk(a_w1)),
                (avec[:, 0, :], spread_row(a_as1.rearrange("h c -> (h c)"), 256)),
                (avec[:, 1, :], spread_row(a_ad1.rearrange("h c -> (h c)"), 256)),
            ], work)
            R = 4 * 65 + 1

            def drain_v(dve, ps, w, tile):
                dve.tensor_copy(at(acc, w, R, 0, 260).rearrange("p (h c) -> p h c", h=4)[:, :, 0:64], ps[:, 0:256].rearrange("p (h c) -> p h c", h=4))
                return dve.tensor_copy(nodes[:, bass.ds(w, 1), :].rearrange("p a n -> p (a n)"), ps[:, 256:264])

            def drain_a(act, ps, w, tile):
                return act.activation(tile[:, 0:264], ps[:, 0:264], ACT.Copy)

            linear(nc, c, "a1l", [(x3, 0, P), (x3, P, P)], [W[:, 0, :], W[:, 1, :]], None, 264, drain_v, drain_a, tables[264], 264, "a")

        def self_loops(H, C, R, ones):
            def work(link, dve):
                a = acc[:, 0:NW * R].rearrange("p (w r) -> p w r", r=R)
                link(dve.memset(a[:, :, 0:H * (C + 1)].rearrange("p w (h c) -> p w h c", h=H)[:, :, :, C], 1.0))
                if ones:
                    link(dve.memset(a[:, :, R - 1:R], 1.0))
                link(dve.tensor_tensor(biggest[:, :, 0:H], nodes[:, :, 0:H], nodes[:, :, H:2 * H], ALU.add))
                link(dve.scalar_tensor_tensor(biggest[:, :, 0:H], biggest[:, :, 0:H], 0.2, biggest[:, :, 0:H], ALU.mult, ALU.max))
            return work

        on_vector(nc, c, "a1s", [], self_loops(4, 64, R, True))
        edge_pass(nc, c, "a1e", order, tables[264], 264, acc, R, "gat", H=4, C=64, node=nodes, node_c0=4, count=True, biggest=biggest)

        with ExitStack() as st:
            mm = Memory(nc, st, "a2")
            W = mm.sb("W", [P, 2, 66])
            avec = mm.sb("avec", [P, 2, 64])
            tmp = mm.sb("tmp", [P, 256])
            bias = mm.sb("bias", [P, 256])

            def work(link, dve):
                a = acc[:, 0:NW * R].rearrange("p (w r) -> p w r", r=R)
                link(dve.tensor_copy(degree[:, :], a[:, :, R - 1]))
                for h in range(4):
                    z = a[:, :, h * 65 + 64:h * 65 + 65]
                    link(dve.reciprocal(z, z))
                    link(dve.tensor_tensor(y3[:, :, h * 64:(h + 1) * 64], a[:, :, h * 65:h * 65 + 64], wide(z, 64), ALU.mult))
                link(dve.tensor_tensor(y3, y3, bc(bias[:, :].rearrange("p (w n) -> p w n", w=1), [P, NW, 256]), ALU.add))
                link(dve.tensor_scalar(y3, y3, 0.0, None, ALU.max))
                keep_valid(link, dve, c, y3)
                fold(link, dve, W, 0, avec[:, 0, :], 1, 64, 64, tmp)
                fold(link, dve, W, 0, avec[:, 1, :], 1, 64, 65, tmp)

            on_vector(nc, c, "a2w", [
                (W[:, :, 0:64], by_chunk(a_w2)), (bias[:, :], spread_row(a_b1, 256)),
                (avec[:, 0, :], spread_row(a_as2, 64)), (avec[:, 1, :], spread_row(a_ad2, 64)),
            ], work)

            def drain_v2(dve, ps, w, tile):
                dve.tensor_copy(at(acc, w, 65, 0, 64), ps[:, 0:64])
                return dve.tensor_copy(nodes[:, bass.ds(w, 1), 0:2].rearrange("p a n -> p (a n)"), ps[:, 64:66])

            def drain_a2(act, ps, w, tile):
                return act.activation(tile[:, 0:66], ps[:, 0:66], ACT.Copy)

            linear(nc, c, "a2l", [(y3, 0, P), (y3, P, P)], [W[:, 0, :], W[:, 1, :]], None, 66, drain_v2, drain_a2, tables[66], 66, "a")
        on_vector(nc, c, "a2s", [], self_loops(1, 64, 65, False))
        edge_pass(nc, c, "a2e", order, tables[66], 66, acc, 65, "gat", H=1, C=64, node=nodes, node_c0=1, biggest=biggest)

        def add_to_x(dve, ps, w, tile):
            return dve.tensor_tensor(at(X, w, D), at(X, w, D), ps[:, 0:D], ALU.add)

        with ExitStack() as st:
            mm = Memory(nc, st, "af")
            W = mm.sb("W", [P, 256])
            brow = mm.sb("brow", [1, 256])
            bias = mm.sb("bias", [P, 64])
            h64 = all_windows(Y, 64)

            def work(link, dve):
                a = acc[:, 0:NW * 65].rearrange("p (w r) -> p w r", r=65)
                link(dve.reciprocal(a[:, :, 64:65], a[:, :, 64:65]))
                link(dve.tensor_tensor(h64, a[:, :, 0:64], wide(a[:, :, 64:65], 64), ALU.mult))
                link(dve.tensor_tensor(h64, h64, bc(bias[:, :].rearrange("p (w n) -> p w n", w=1), [P, NW, 64]), ALU.add))

            on_vector(nc, c, "afw", [(W[0:64, :], a_wf), (brow[:, :], row(a_bf)), (bias[:, :], spread_row(a_b2, 64))], work)
            linear(nc, c, "afl", [(h64, 0, 64)], [W], brow, 256, add_to_x, None)

        with ExitStack() as st:
            mm = Memory(nc, st, "b")
            W = mm.sb("W", [P, 2, 260])
            avec = mm.sb("avec", [P, 4, 128])
            tmp = mm.sb("tmp", [P, 256])
            R = 2 * 129

            def work(link, dve):
                normalize(link, dve, c, x3, y3, small)
                for h in range(2):
                    fold(link, dve, W, 128 * h, avec[:, 2 * h + 1, :], 1, 128, 256 + h, tmp)
                    fold(link, dve, W, 128 * h, avec[:, 2 * h, :], 1, 128, 258 + h, tmp)
                link(dve.memset(acc[:, 0:NW * R], 0.0))
                for h in range(2):
                    z = acc[:, 0:NW * R].rearrange("p (w r) -> p w r", r=R)[:, LAST:NW, h * 129 + 128]
                    link(dve.tensor_scalar(z, c.valid[:, :], -1.0, 1.0, ALU.mult, ALU.add))

            on_vector(nc, c, "bw", [
                (W[:, :, 0:128], by_chunk(b_w1)), (W[:, :, 128:256], by_chunk(b_w2)),
            ] + [(avec[:, 2 * h + k, :], spread_row(a[:, 128 * k:128 * (k + 1)], 128))
                 for h, a in enumerate((b_a1, b_a2)) for k in range(2)], work, small[:, 1, :])

            def drain_vb(dve, ps, w, tile):
                return dve.tensor_copy(nodes[:, bass.ds(w, 1), 0:2].rearrange("p a n -> p (a n)"), ps[:, 258:260])

            def drain_ab(act, ps, w, tile):
                return act.activation(tile[:, 0:258], ps[:, 0:258], ACT.Copy)

            linear(nc, c, "bl", [(x3, 0, P), (x3, P, P)], [W[:, 0, :], W[:, 1, :]], None, 260, drain_vb, drain_ab, tables[258], 258, "a")
        move_order("src", True)
        edge_pass(nc, c, "be", order, tables[258], 258, acc, R, "neg", H=2, C=128, node=nodes, node_c0=0)

        with ExitStack() as st:
            mm = Memory(nc, st, "t")
            W = mm.sb("W", [P, 2, 768])
            brow = mm.sb("brow", [1, 768])

            def work(link, dve):
                a = acc[:, 0:NW * R].rearrange("p (w r) -> p w r", r=R)
                for h in range(2):
                    z = a[:, :, h * 129 + 128:h * 129 + 129]
                    link(dve.reciprocal(z, z))
                    link(dve.tensor_tensor(y3[:, :, h * 128:(h + 1) * 128], a[:, :, h * 129:h * 129 + 128], wide(z, 128), ALU.mult))
                low = acc[:, 0:NW * D].rearrange("p (w n) -> p w n", n=D)
                link(dve.tensor_scalar(low, y3, 0.0, None, ALU.min))

            on_vector(nc, c, "tw", [
                (W[:, :, 0:256], by_chunk(t_wq)), (W[:, :, 256:512], by_chunk(t_wk)), (W[:, :, 512:768], by_chunk(t_wv)),
                (brow[:, 0:256], row(t_bq)), (brow[:, 256:512], row(t_bk)), (brow[:, 512:768], row(t_bv)),
            ], work)
            s_exp = mm.sem("exp")
            with nc.Block() as block:
                @block.scalar
                def _(act):
                    act.activation(acc[:, 0:NW * D], acc[:, 0:NW * D], ACT.Exp).then_inc(s_exp, 1)

            def work(link, dve):
                low = acc[:, 0:NW * D].rearrange("p (w n) -> p w n", n=D)
                link(dve.scalar_tensor_tensor(y3, y3, 0.0, low, ALU.max, ALU.add))
                link(dve.scalar_tensor_tensor(x3, y3, -1.0, x3, ALU.add, ALU.add))
                normalize(link, dve, c, x3, y3, small)
                link(dve.memset(acc[:, :], 0.0))
                link(dve.memset(biggest[:, :, :], -BIG))

            on_vector(nc, c, "tx", [], work, small[:, 1, :])

            parts = both.bitcast(BF16)[:, 0:3 * NW * D].rearrange("p (w n) -> p w n", n=D)
            query = mm.sb("query", [P, 2, D])
            s_split = mm.sem("split")
            s_away = mm.sem("away")
            with nc.Block() as block:
                @block.sync
                def _(sp):
                    sp.dma_start(x_kept, X).then_inc(s_away, 16)
                    sp.wait_ge(s_away, 16)

            def drain_vt(dve, ps, w, tile):
                done = w * 4 if isinstance(w, int) else dve.snap(w * 4)
                q, r = query[:, 0, :], query[:, 1, :]
                high, middle, low = (parts[:, bass.ds(w * 3 + k, 1), :].rearrange("p a n -> p (a n)") for k in range(3))
                dve.tensor_scalar(q, ps[:, 0:256], 32.0 ** -0.5, None, ALU.mult).then_inc(s_split, 1)
                dve.wait_ge(s_split, done + 1)
                dve.tensor_scalar(high, q, 1.0, None, ALU.mult).then_inc(s_split, 1)
                dve.wait_ge(s_split, done + 2)
                dve.tensor_tensor(r, q, high, ALU.subtract).then_inc(s_split, 1)
                dve.wait_ge(s_split, done + 3)
                dve.tensor_scalar(middle, r, 1.0, None, ALU.mult).then_inc(s_split, 1)
                dve.wait_ge(s_split, done + 4)
                return dve.tensor_tensor(low, r, middle, ALU.subtract)

            def drain_at(act, ps, w, tile):
                return act.activation(tile[:, 0:512], ps[:, 256:768], ACT.Copy)

            linear(nc, c, "tl", [(x3, 0, P), (x3, P, P)], [W[:, 0, :], W[:, 1, :]], brow, 768, drain_vt, drain_at, tables[512], 512, "a")
        R = 8 * 33
        parts = both.bitcast(BF16)[:, 0:3 * NW * D].rearrange("p (w n) -> p w n", n=D)
        edge_pass(nc, c, "te", order, tables[512], 512, acc, R, "dot", H=8, C=32, node=parts, value_c0=256, biggest=biggest, slots=4)

        with ExitStack() as st:
            mm = Memory(nc, st, "to")
            W = mm.sb("W", [P, 2, 256])
            brow = mm.sb("brow", [1, 256])

            def work(link, dve):
                a = acc[:, 0:NW * R].rearrange("p (w r) -> p w r", r=R)
                for h in range(8):
                    z = a[:, :, h * 33 + 32:h * 33 + 33]
                    link(dve.tensor_scalar(z, z, 1e-37, None, ALU.max))
                    link(dve.reciprocal(z, z))
                    link(dve.tensor_tensor(y3[:, :, h * 32:(h + 1) * 32], a[:, :, h * 33:h * 33 + 32], wide(z, 32), ALU.mult))

            on_vector(nc, c, "tow", [(W[:, :, :], by_chunk(t_wo)), (brow[:, :], row(t_bo)), (X, x_kept)], work)
            linear(nc, c, "tol", [(y3, 0, P), (y3, P, P)], [W[:, 0, :], W[:, 1, :]], brow, 256, add_to_x, None)

        move_order("dst", True)

        f1, f2 = Y[:, 0:NW * 128], Y[:, NW * 128:NW * 192]
        f1w = f1.rearrange("p (w n) -> p w n", n=128)
        f2w = f2.rearrange("p (w n) -> p w n", n=64)

        def dinv(n):
            return bc(small[:, 1, :].rearrange("p (w n) -> p w n", n=1), [P, NW, n])

        def convolve(tag, sources, weights, n):
            def drain_v(dve, ps, w, tile):
                dve.tensor_tensor(tile[:, 0:n], ps[:, 0:n], bc(small[:, 1, bass.ds(w, 1)], [P, n]), ALU.mult)
                return dve.tensor_tensor(at(acc, w, n), ps[:, 0:n], bc(small[:, 1, bass.ds(w, 1)], [P, n]), ALU.mult)

            linear(nc, c, tag + "l", sources, weights, None, n, drain_v, None, tables[n], n, "v")
            edge_pass(nc, c, tag + "e", order, tables[n], n, acc, n, "sum")

        def batch_norm(tag, n, to, b, gamma, beta):
            with ExitStack() as st:
                mm = Memory(nc, st, tag)
                vecs = mm.sb("vecs", [P, 3, n])
                part = mm.sb("part", [P, n])
                mean = mm.sb("mean", [P, n])
                scale = mm.sb("scale", [P, n])
                ps = mm.ps("ps", [P, 2, 512])
                s_loaded, s_step, s_part, s_sum, s_ask, s_root = (mm.sem(x) for x in ("loaded", "step", "part", "sum", "ask", "root"))
                a = acc[:, 0:NW * n].rearrange("p (w n) -> p w n", n=n)
                down = acc[:, 0:NW * n].rearrange("p (w n) -> p n w", n=n)
                sq = acc[:, NW * n:2 * NW * n].rearrange("p (w n) -> p w n", n=n)

                def rows(v):
                    return bc(v.rearrange("p (w n) -> p w n", w=1), [P, NW, n])

                with nc.Block() as block:
                    @block.sync
                    def _(sp):
                        for k, v in enumerate((b, gamma, beta)):
                            sp.dma_start(vecs[:, k, :], spread_row(v, n)).then_inc(s_loaded, 16)

                    @block.gpsimd
                    def _(pool):
                        pool.wait_ge(s_ask, 1)
                        inverse_root(pool, c.minus_half[:, :], scale[:, :]).then_inc(s_root, 1)

                    @block.tensor
                    def _(pe):
                        for k in range(2):
                            pe.wait_ge(s_part, k + 1)
                            pe.matmul(ps[:, k, 0:n], c.ones[:, :], part[:, :], start=True, stop=True).then_inc(s_sum, 1)

                    @block.vector
                    def _(dve):
                        link = Link(dve, s_step)
                        dve.wait_ge(s_loaded, 48)
                        link(dve.tensor_tensor(a, a, dinv(n), ALU.mult))
                        link(dve.tensor_tensor(a, a, rows(vecs[:, 0, :]), ALU.add))
                        keep_valid(link, dve, c, a)
                        dve.tensor_reduce(part[:, :], down, AX.X, ALU.add).then_inc(s_part, 1)
                        dve.wait_ge(s_sum, 1)
                        link(dve.tensor_scalar(mean[:, :], ps[:, 0, 0:n], 1.0 / N, None, ALU.mult))
                        link(dve.tensor_tensor(a, a, rows(mean[:, :]), ALU.subtract))
                        keep_valid(link, dve, c, a)
                        link(dve.tensor_tensor(to, a, a, ALU.mult))
                        dve.tensor_reduce(part[:, :], to.rearrange("p w n -> p n w"), AX.X, ALU.add).then_inc(s_part, 1)
                        dve.wait_ge(s_sum, 2)
                        dve.tensor_scalar(scale[:, :], ps[:, 1, 0:n], 1.0 / N, EPS, ALU.mult, ALU.add).then_inc(s_ask, 1)
                        dve.wait_ge(s_root, 1)
                        link(dve.tensor_tensor(scale[:, :], scale[:, :], vecs[:, 1, :], ALU.mult))
                        link(dve.tensor_tensor(a, a, rows(scale[:, :]), ALU.mult))
                        link(dve.tensor_tensor(a, a, rows(vecs[:, 2, :]), ALU.add))
                        link(dve.tensor_scalar(to, a, 0.0, None, ALU.max))

        with ExitStack() as st:
            mm = Memory(nc, st, "g1")
            W = mm.sb("W", [P, 2, 128])

            def work(link, dve):
                normalize(link, dve, c, x3, y3, small)

            def degrees(link, dve):
                link.asked(dve.tensor_copy(small[:, 1, :], degree[:, :]))

            on_vector(nc, c, "g1w", [(W[:, :, :], by_chunk(g_w1))], work, small[:, 1, :])
            on_vector(nc, c, "g1d", [], degrees, small[:, 1, :])
            convolve("g1", [(x3, 0, P), (x3, P, P)], [W[:, 0, :], W[:, 1, :]], 128)
            batch_norm("n1", 128, f1w, g_b1, g_g1, g_be1)
        with ExitStack() as st:
            mm = Memory(nc, st, "g2")
            W = mm.sb("W", [P, 64])
            on_vector(nc, c, "g2w", [(W[:, :], g_w2)], lambda link, dve: None)
            convolve("g2", [(f1w, 0, P)], [W], 64)
            batch_norm("n2", 64, f2w, g_b2, g_g2, g_be2)
        with ExitStack() as st:
            mm = Memory(nc, st, "gf")
            W = mm.sb("W", [P, 4, 256])
            brow = mm.sb("brow", [1, 256])
            on_vector(nc, c, "gfw", [(W[:, 0:3, :], by_chunk(g_wfc[0:384, :])), (W[0:64, 3, :], g_wfc[384:448, :]),
                                  (brow[:, :], row(g_bfc))], lambda link, dve: None)

            def drain_vf(dve, ps, w, tile):
                return dve.scalar_tensor_tensor(at(X, w, D), ps[:, 0:D], 0.0, at(X, w, D), ALU.max, ALU.add)

            linear(nc, c, "gfl", [(x3, 0, P), (x3, P, P), (f1w, 0, P), (f2w, 0, 64)], [W[:, k, :] for k in range(4)], brow, 256, drain_vf, None)
            on_vector(nc, c, "last", [], lambda link, dve: normalize(link, dve, c, x3, y3, small), small[:, 1, :])
        s_out = m.sem("out")
        with nc.Block() as block:
            @block.sync
            def _(sp):
                sp.dma_start(out[0:LAST * P, :].rearrange("(w p) n -> p w n", p=P), x3[:, 0:LAST, :]).then_inc(s_out, 16)
                sp.dma_start(out[LAST * P:N, :], X[0:VALID, LAST * D:(LAST + 1) * D]).then_inc(s_out, 16)
                sp.wait_ge(s_out, 32)


_INS = ["x", "src", "dst", "L0_gnn_W1", "L0_gnn_att_src1", "L0_gnn_att_dst1", "L0_gnn_b1", "L0_gnn_W2",
        "L0_gnn_att_src2", "L0_gnn_att_dst2", "L0_gnn_b2", "L0_gnn_Wf", "L0_gnn_bf", "L1_gnn_W1", "L1_gnn_a1",
        "L1_gnn_W2", "L1_gnn_a2", "L2_gnn_Wq", "L2_gnn_bq", "L2_gnn_Wk", "L2_gnn_bk", "L2_gnn_Wv", "L2_gnn_bv",
        "L2_gnn_Wo", "L2_gnn_bo", "L3_gnn_W1", "L3_gnn_b1", "L3_gnn_g1", "L3_gnn_be1", "L3_gnn_W2", "L3_gnn_b2",
        "L3_gnn_g2", "L3_gnn_be2", "L3_gnn_Wfc", "L3_gnn_bfc"]


def kernel(**inputs):
    import numpy as np
    import concourse.bacc as bacc
    from concourse.bass_utils import run_bass_kernel_spmd

    nc = bacc.Bacc("TRN2", target_bir_lowering=False, num_devices=1)
    arrays, args = {}, []
    for name in _INS:
        a = np.ascontiguousarray(inputs[name])
        arrays[f"in_{name}"] = a
        args.append(nc.dram_tensor(f"in_{name}", a.shape, mybir.dt.from_np(a.dtype), kind="ExternalInput").ap())
    out = nc.dram_tensor("out", (N, D), F32, kind="ExternalOutput").ap()
    gnn_kernel(nc, *args, out)
    r = run_bass_kernel_spmd(nc, [arrays], core_ids=[0])
    return r.results[0]["out"]
```

```python
import concourse.bass as bass
from concourse import mybir
from concourse.alu_op_type import AluOpType as ALU
from contextlib import ExitStack

F32 = mybir.dt.float32
BF16 = mybir.dt.bfloat16
I32 = mybir.dt.int32
ACT = mybir.ActivationFunctionType
AX = mybir.AxisListType

P = 128
N = 6250
E = 100000
D = 256
WIN = -(-N // P)
NW = WIN + 1
NPAD = NW * P
PAD_ROW = NPAD - 1
GE = 2 * P
UN = 8
LEAD = 6
NG = -(-((E + WIN * (GE - 1)) // GE) // UN) * UN
NSLOT = 2 * NG
WT = NG + LEAD + UN
EP, EC = 125, 800
SB = 8
TURNS = EC // (2 * SB)
BIG = 65536.0
CLIP = 30000.0
EPS = 1e-5
LAST = WIN - 1
VALID = N - LAST * P


class Group:

    def __init__(self, i, k, windows=None):
        self.i, self.k = i, k
        self.window = None if windows is None else windows[k + LEAD]

    def plus(self, n):
        return self.i * UN + (self.k + n)

    def slot(self, n):
        return self.k % n

    def turn(self, n):
        return self.i * (UN // n) + self.k // n

    def exists(self):
        return not isinstance(self.i, int) or 0 <= self.i * UN + self.k < NG


def wait(eng, sem, count):
    if isinstance(count, int) and count <= 0:
        return
    eng.wait_ge(sem, count)


class Link:

    def __init__(self, eng, sem):
        self.eng, self.sem, self.n = eng, sem, 0

    def __call__(self, ins):
        self.n += 1
        ins.then_inc(self.sem, 1)
        self.eng.wait_ge(self.sem, self.n)


def apart(eng, sem, count, passed):
    wait(eng, sem, count)
    eng.sem_inc(passed, 1)


def bc(ap, shape):
    return ap.to_broadcast(shape)


class Memory:

    def __init__(self, nc, stack, stage):
        self.nc, self.stack, self.stage = nc, stack, stage
        self.sems = []
        stack.callback(self.clear)

    def clear(self):
        if self.sems:
            self.nc.clear_and_free_semaphores(self.sems)
            self.nc.all_engine_barrier()

    def sb(self, name, shape, dt=F32):
        return self.stack.enter_context(self.nc.sbuf_tensor(f"{self.stage}_{name}", shape, dt))

    def ps(self, name, shape, dt=F32):
        return self.stack.enter_context(self.nc.psum_tensor(f"{self.stage}_{name}", shape, dt))

    def sem(self, name):
        sem = self.nc.alloc_semaphore(f"{self.stage}_{name}")
        self.sems.append(sem)
        return sem



def constants(nc, m, c):
    c.ident = m.sb("ident", [P, P])
    c.ident16 = m.sb("ident16", [P, P], BF16)
    c.lane = m.sb("lane", [P, P])
    c.lanei = m.sb("lanei", [P, P], I32)
    c.tri = m.sb("tri", [P, P])
    c.ones = m.sb("ones", [P, P])
    c.zero = m.sb("zero", [P, 1])
    c.minus_half = m.sb("minus_half", [P, 1])
    c.valid = m.sb("valid", [P, 2])
    s_made = m.sem("made")
    with nc.Block() as block:
        @block.gpsimd
        def _(pool):
            link = Link(pool, s_made)
            link(pool.memset(c.ident[:, :], 0.0))
            link(pool.affine_select(out=c.ident[:, :], in_=c.ident[:, :], compare_op=ALU.not_equal, fill=1.0,
                                    base=0, pattern=[[-1, P]], channel_multiplier=1))
            link(pool.tensor_copy(c.ident16[:, :], c.ident[:, :]))
            link(pool.memset(c.ones[:, :], 1.0))
            link(pool.memset(c.zero[:, :], 0.0))
            link(pool.memset(c.minus_half[:, :], -0.5))
            link(pool.affine_select(out=c.tri[:, :], in_=c.ones[:, :], compare_op=ALU.is_gt, fill=0.0,
                                    base=0, pattern=[[1, P]], channel_multiplier=-1))
            link(pool.iota(c.lanei[:, :], pattern=[[1, P]], base=0, channel_multiplier=0))
            link(pool.tensor_copy(c.lane[:, :], c.lanei[:, :]))
            link(pool.memset(c.valid[:, :], 0.0))
            link(pool.affine_select(out=c.valid[:, 0:1], in_=c.ones[:, 0:1], compare_op=ALU.is_gt, fill=0.0,
                                    base=VALID, pattern=[[0, 1]], channel_multiplier=-1))



class Region:

    def __init__(self, tensor):
        self.views, self.used = {F32: tensor, I32: tensor.bitcast(I32)}, 0

    def take(self, partitions, *shape, dt=F32):
        n = 1
        for k in shape:
            n *= k
        flat = self.views[dt][0:partitions, self.used:self.used + n]
        self.used += n
        if len(shape) == 1:
            return flat
        return flat.rearrange("p (a b) -> p a b", b=shape[1])


class Ranking:

    def __init__(self, region):
        self.key = region.take(EP, EC, dt=I32)
        self.other = region.take(EP, EC, dt=I32)
        self.winf = region.take(EP, EC)
        self.hit = [region.take(EP, EC) for _ in range(2)]
        self.run = [region.take(EP, EC) for _ in range(2)]
        self.rank = region.take(EP, EC)
        self.total = region.take(P, WIN)
        self.offset = region.take(P, WIN)
        self.groups = region.take(P, WIN)
        self.groupsi = region.take(P, WIN, dt=I32)
        self.ends = region.take(P, WIN)
        self.number = region.take(P, NG)


class Posted:

    def __init__(self, region, records):
        self.post = region.take(EP, EC * 3, dt=I32).rearrange("p (e r) -> p e r", r=3)
        self.windowf = region.take(P, NG)
        self.records = records


def rank_edges(nc, c, m, r, posted, numberi, s):
    post, windowf = posted.post, posted.windowf
    ps = s.ps
    hit, run = r.hit, r.run

    def on_tensor(pe):
        pe.wait_ge(s.total, 1)
        pe.matmul(ps[0:EP, 0, 0:WIN], c.tri[0:EP, 0:EP], r.total[0:EP, :], start=True, stop=True)
        pe.matmul(ps[:, 1, 0:WIN], c.ones[0:EP, :], r.total[0:EP, :], start=True, stop=True).then_inc(s.sums, 1)

    def on_vector_engine(dve):
        link = Link(dve, s.step)
        dve.wait_ge(s.loaded, 32)
        link(dve.tensor_single_scalar(post[:, :, 0], r.key, 7, ALU.arith_shift_right))
        link(dve.tensor_copy(r.winf, post[:, :, 0]))
        link(dve.memset(r.rank, 0.0))
        def tally(w, n, base):
            for b in range(n):
                dve.tensor_scalar(hit[b], r.winf, c.lane[0:EP, bass.ds(w + b, 1)], None, ALU.is_equal).then_inc(s.loop, 1)
            for b in range(n):
                dve.wait_ge(s.loop, base + (1 + b))
                dve.tensor_tensor_scan(run[b], hit[b], bc(c.zero[0:EP, :], [EP, EC]), 0.0, ALU.add, ALU.add).then_inc(s.loop, 1)
            for b in range(n):
                dve.wait_ge(s.loop, base + (n + 1 + b))
                dve.tensor_copy(r.total[0:EP, bass.ds(w + b, 1)], run[b][:, EC - 1:EC]).then_inc(s.loop, 1)
                dve.tensor_tensor(hit[b], hit[b], run[b], ALU.mult).then_inc(s.loop, 1)
            for b in range(n):
                dve.wait_ge(s.loop, base + (2 * n + 2 if b == 0 else 4 * n + b))
                dve.tensor_tensor(r.rank, r.rank, hit[b], ALU.add).then_inc(s.loop, 1)
            dve.wait_ge(s.loop, base + 5 * n)

        with dve.Fori(0, WIN // 2) as i:
            tally(i * 2, 2, i * 10)
        for w in range(WIN // 2 * 2, WIN):
            tally(w, 1, WIN // 2 * 10)
        dve.memset(windowf, 0.0).then_inc(s.total, 1)
        dve.wait_ge(s.sums, 1)
        link(dve.tensor_scalar(r.groups, ps[:, 1, 0:WIN], float(GE - 1), None, ALU.add))
        link(dve.tensor_copy(r.groupsi, r.groups))
        link(dve.tensor_single_scalar(r.groupsi, r.groupsi, GE.bit_length() - 1, ALU.arith_shift_right))
        link(dve.tensor_copy(r.groups, r.groupsi))
        link(dve.tensor_tensor_scan(r.ends, r.groups, bc(c.zero[:, :], [P, WIN]), 0.0, ALU.add, ALU.add))
        link(dve.tensor_tensor(r.offset, r.ends, r.groups, ALU.subtract))
        link(dve.tensor_scalar(r.offset, r.offset, float(GE), -1.0, ALU.mult, ALU.add))
        link(dve.tensor_tensor(r.offset[0:EP, :], r.offset[0:EP, :], ps[0:EP, 0, 0:WIN], ALU.add))
        def lift(w, n, base):
            for b in range(n):
                dve.tensor_scalar(hit[b], r.winf, c.lane[0:EP, bass.ds(w + b, 1)], r.offset[0:EP, bass.ds(w + b, 1)],
                                  ALU.is_equal, ALU.mult).then_inc(s.base, 1)
            for b in range(n):
                dve.wait_ge(s.base, base + (n if b == 0 else n + b))
                dve.tensor_tensor(r.rank, r.rank, hit[b], ALU.add).then_inc(s.base, 1)
            dve.wait_ge(s.base, base + 2 * n)

        with dve.Fori(0, WIN // 2) as i:
            lift(i * 2, 2, i * 4)
        for w in range(WIN // 2 * 2, WIN):
            lift(w, 1, WIN // 2 * 4)
        link(dve.tensor_copy(post[:, :, 1], r.rank))
        link(dve.tensor_single_scalar(post[:, :, 2], post[:, :, 1], 7, ALU.arith_shift_right))
        link(dve.tensor_copy(run[0], post[:, :, 2]))
        link(dve.scalar_tensor_tensor(hit[0], run[0], -float(P), r.rank, ALU.mult, ALU.add))
        link(dve.scalar_tensor_tensor(hit[0], hit[0], float(NSLOT), run[0], ALU.mult, ALU.add))
        link(dve.tensor_copy(post[:, :, 0], hit[0]))
        link(dve.tensor_copy(post[:, :, 1], r.other))
        link(dve.tensor_copy(post[:, :, 2], r.key))

    def windows(dve, done):
        link = Link(dve, done)
        link(dve.tensor_copy(r.number, numberi))
        for w in range(WIN):
            link(dve.scalar_tensor_tensor(windowf, r.number, r.ends[:, w:w + 1], windowf, ALU.is_ge, ALU.add))

    return on_tensor, on_vector_engine, windows


class RankSemaphores:
    def __init__(self, m):
        self.ps = m.ps("sums", [P, 2, 256])
        self.loaded = m.sem("loaded")
        self.step = m.sem("step")
        self.loop = m.sem("loop")
        self.total = m.sem("total")
        self.sums = m.sem("sums")
        self.base = m.sem("base")
        self.window = m.sem("window")


class Scatter:

    def __init__(self, m, posted):
        self.posted = posted
        self.staged = m.sb("staged", [EP, 2, SB, 3], I32)
        self.s_staged = m.sem("staged")
        self.s_scattered = [m.sem(f"scattered{h}") for h in range(2)]
        self.s_passed = m.sem("scatter_passed")

    def stage(self, pool, i, h):
        if not isinstance(i, int) or i > 0:
            apart(pool, self.s_scattered[h], i * (16 * SB), self.s_passed)
        pool.tensor_copy(self.staged[:, h, :, :], self.posted.post[:, bass.ds(i * (2 * SB) + h * SB, SB), :]).then_inc(self.s_staged, 1)
        apart(pool, self.s_staged, i * 2 + (h + 1), self.s_passed)

    def send(self, pool, h, j):
        pool.indirect_dma_start(
            out=self.posted.records.rearrange("p s r -> (p s) r"),
            out_offset=bass.IndirectOffsetOnAxis(ap=self.staged[:, h, j, 0:1], axis=0),
            in_=self.staged[:, h, j, 1:3], in_offset=None).then_inc(self.s_scattered[h], 16)

    def finish(self, eng):
        for h in range(2):
            eng.wait_ge(self.s_scattered[h], 16 * SB * TURNS)


def edge_tables(dve, s_step, back, windowf, row, place, window, keyed=None):
    link = Link(dve, s_step)
    link(dve.memset(window, WIN))
    link(dve.tensor_copy(window[:, LEAD:LEAD + NG], windowf))
    if keyed is not None:
        link(dve.tensor_scalar(keyed, back[:, :, 1], 0.0, float(PAD_ROW + 1), ALU.is_lt, ALU.mult))
        link(dve.tensor_tensor(keyed, keyed, back[:, :, 1], ALU.add))
    link(dve.memset(row[:, NSLOT:], PAD_ROW))
    link(dve.tensor_copy(row[:, 0:NSLOT], back[:, :, 0]))
    link(dve.tensor_copy(place, back[:, :, 1]))
    link(dve.scalar_tensor_tensor(
        place.rearrange("p (g j) -> p g j", j=2), bc(windowf.rearrange("p (g j) -> p g j", j=1), [P, NG, 2]),
        -float(P), place.rearrange("p (g j) -> p g j", j=2), ALU.mult, ALU.add))


def load_edges(sp, s, r, key_d, other_d):
    sp.dma_start(r.key, key_d.rearrange("(p c) -> p c", p=EP)).then_inc(s.loaded, 16)
    sp.dma_start(r.other, other_d.rearrange("(p c) -> p c", p=EP)).then_inc(s.loaded, 16)


def sort_edges(nc, c, src, dst, by_dst, by_src, region, order, kept, blank, loads):
    r = Ranking(region)
    back = region.take(P, NSLOT * 2, dt=I32).rearrange("p (s r) -> p s r", r=2)
    numberi = region.take(P, NG, dt=I32)
    with ExitStack() as stack:
        m = Memory(nc, stack, "by_dst")
        s = RankSemaphores(m)
        s_empty, s_filled = m.sem("empty"), m.sem("filled")
        on_tensor, on_vector_engine, windows = rank_edges(nc, c, m, r, by_dst, numberi, s)
        with nc.Block() as block:
            @block.sync
            def _(sp):
                load_edges(sp, s, r, dst, src)
                sp.wait_ge(s_empty, 4)
                for records in (by_dst.records, by_src.records):
                    sp.dma_start(records, back).then_inc(s_filled, 16)
                sp.wait_ge(s_filled, 32)

            @block.gpsimd
            def _(pool):
                pool.memset(blank, 0.0).then_inc(s_empty, 1)
                pool.memset(back[:, :, 0:1], PAD_ROW).then_inc(s_empty, 1)
                pool.memset(back[:, :, 1:2], -1).then_inc(s_empty, 1)
                pool.iota(numberi, pattern=[[1, NG]], base=0, channel_multiplier=0).then_inc(s_empty, 1)

            @block.tensor
            def _(pe):
                on_tensor(pe)

            @block.vector
            def _(dve):
                on_vector_engine(dve)

    with ExitStack() as stack:
        m = Memory(nc, stack, "by_src")
        s = RankSemaphores(m)
        scatter = Scatter(m, by_dst)
        s_early, s_number, s_ends, s_back, s_table, s_kept = (m.sem(x) for x in ("early", "number", "ends", "back", "table", "kept"))
        on_tensor, on_vector_engine, windows = rank_edges(nc, c, m, r, by_src, numberi, s)
        _, _, windows_by_dst = rank_edges(nc, c, m, r, by_dst, numberi, s)
        with nc.Block() as block:
            @block.sync
            def _(sp):
                load_edges(sp, s, r, src, dst)
                for to, frm in loads:
                    sp.dma_start(to, frm).then_inc(s_early, 16)
                sp.wait_ge(s_early, 16 * len(loads))
                scatter.finish(sp)
                sp.dma_start(back, by_dst.records).then_inc(s_back, 16)
                sp.wait_ge(s_table, 6)
                for d, t in zip(kept, (order.row, order.place, order.window)):
                    sp.dma_start(d, t[:, :]).then_inc(s_kept, 16)
                sp.wait_ge(s_kept, 48)

            @block.gpsimd
            def _(pool):
                for h in range(2):
                    scatter.stage(pool, 0, h)
                    for j in range(SB):
                        scatter.send(pool, h, j)
                with pool.Fori(1, TURNS) as i:
                    for h in range(2):
                        scatter.stage(pool, i, h)
                        for j in range(SB):
                            scatter.send(pool, h, j)

            @block.tensor
            def _(pe):
                on_tensor(pe)

            @block.vector
            def _(dve):
                windows_by_dst(dve, s_number)
                on_vector_engine(dve)
                windows(dve, s_ends)
                dve.wait_ge(s_back, 16)
                edge_tables(dve, s_table, back, by_dst.windowf, order.row[:, :], order.place[:, :], order.window[:, :])



def linear(nc, c, stage, sources, weights, bias, width, drain_v, drain_a, tables=(), table_by=""):
    with ExitStack() as stack:
        m = Memory(nc, stack, stage)
        K = len(sources)
        turned = m.sb("turned", [P, 2, K, P])
        fetched = m.sb("fetched", [P, 2, K, P])
        tile = m.sb("tile", [P, 2, max([c0 + n for _, c0, n in tables] + [1])])
        ps_t = [m.ps(f"ps_t{b}", [P, 512]) for b in range(2)]
        banks = -(-width // 512)
        ps_o = [m.ps(f"ps_o{b}", [P, banks * 512]) for b in range(2)]
        s_fetched, s_t, s_turned, s_product, s_v, s_a, s_passed = (m.sem(x) for x in ("fetched", "t", "turned", "product", "v", "a", "passed"))
        s_stored = [m.sem(f"stored{b}") for b in range(2)]
        cuts = [(a, min(a + 512, width)) for a in range(0, width, 512)]

        with nc.Block() as block:
            @block.tensor
            def _(pe):
                def turn(w, b):
                    wait(pe, s_turned, w - 1)
                    apart(pe, s_fetched, w + 1, s_passed)
                    for k, (x, c0, n) in enumerate(sources):
                        last = pe.transpose(ps_t[b][0:n, k * P:(k + 1) * P], fetched[:, b, k, 0:n], c.ident[:, :])
                    last.then_inc(s_t, 1)

                def product(w, b):
                    pe.wait_ge(s_turned, w + 1)
                    if drain_v is not None:
                        wait(pe, s_v, w - 1)
                    if drain_a is not None:
                        wait(pe, s_a, w - 1)
                    for a0, a1 in cuts:
                        for k, (x, c0, n) in enumerate(sources):
                            last = pe.matmul(ps_o[b][:, a0:a1], turned[0:n, b, k, :], weights[k][0:n, a0:a1],
                                             start=k == 0, stop=k == K - 1 and bias is None)
                        if bias is not None:
                            last = pe.matmul(ps_o[b][:, a0:a1], c.ones[0:1, :], bias[0:1, a0:a1], start=False, stop=True)
                    last.then_inc(s_product, 1)

                turn(0, 0)
                turn(1, 1)
                product(0, 0)
                turn(2, 0)
                product(1, 1)
                with pe.Fori(1, NW // 2 - 1) as i:
                    turn(i * 2 + 1, 1)
                    product(i * 2, 0)
                    turn(i * 2 + 2, 0)
                    product(i * 2 + 1, 1)
                turn(NW - 1, 1)
                product(NW - 2, 0)
                product(NW - 1, 1)

            @block.scalar
            def _(act):
                def copy(w, b):
                    act.wait_ge(s_t, w + 1)
                    wait(act, s_product, w - 1)
                    for k, (x, c0, n) in enumerate(sources):
                        last = act.activation(turned[0:n, b, k, :], ps_t[b][0:n, k * P:(k + 1) * P], ACT.Copy)
                    last.then_inc(s_turned, 1)

                def drain(w, b):
                    if drain_a is None:
                        return
                    act.wait_ge(s_product, w + 1)
                    if "a" in table_by:
                        wait(act, s_stored[b], (w // 2) * (16 * len(tables)) if isinstance(w, int) else (w - b) * (8 * len(tables)))
                    drain_a(act, ps_o[b], w, tile[:, b, :]).then_inc(s_a, 1)

                copy(0, 0)
                copy(1, 1)
                drain(0, 0)
                copy(2, 0)
                drain(1, 1)
                with act.Fori(1, NW // 2 - 1) as i:
                    copy(i * 2 + 1, 1)
                    drain(i * 2, 0)
                    copy(i * 2 + 2, 0)
                    drain(i * 2 + 1, 1)
                copy(NW - 1, 1)
                drain(NW - 2, 0)
                drain(NW - 1, 1)

            @block.vector
            def _(dve):
                def drain(w, b):
                    if drain_v is None:
                        return
                    dve.wait_ge(s_a if drain_a is not None else s_product, w + 1)
                    if "v" in table_by:
                        wait(dve, s_stored[b], (w // 2) * (16 * len(tables)) if isinstance(w, int) else (w - b) * (8 * len(tables)))
                    drain_v(dve, ps_o[b], w, tile[:, b, :]).then_inc(s_v, 1)

                def fetch(w, b):
                    wait(dve, s_t, w - 1)
                    for k, (x, c0, n) in enumerate(sources):
                        last = dve.tensor_copy(fetched[:, b, k, 0:n], x[:, bass.ds(w, 1), c0:c0 + n].rearrange("p a n -> p (a n)"))
                    last.then_inc(s_fetched, 1)

                fetch(0, 0)
                fetch(1, 1)
                fetch(2, 0)
                drain(0, 0)
                fetch(3, 1)
                drain(1, 1)
                with dve.Fori(1, NW // 2 - 1) as i:
                    fetch(i * 2 + 2, 0)
                    drain(i * 2, 0)
                    fetch(i * 2 + 3, 1)
                    drain(i * 2 + 1, 1)
                drain(NW - 2, 0)
                drain(NW - 1, 1)

            if tables:
                @block.sync
                def _(sp):
                    def store(w, b):
                        if "v" in table_by:
                            sp.wait_ge(s_v, w + 1)
                        if "a" in table_by:
                            sp.wait_ge(s_a, w + 1)
                        for table, c0, n in tables:
                            rows = table.rearrange("(w p) n -> w p n", p=P)
                            sp.dma_start(rows[bass.ds(w, 1), :, :].rearrange("w p n -> (w p) n"), tile[:, b, c0:c0 + n]).then_inc(s_stored[b], 16)

                    with sp.Fori(0, NW // 2) as i:
                        store(i * 2, 0)
                        store(i * 2 + 1, 1)
                    for b in range(2):
                        sp.wait_ge(s_stored[b], 16 * len(tables) * (NW // 2))



class EdgeSemaphores:

    def __init__(self, m):
        self.keys = m.sem("keys")
        self.index = m.sem("index")
        self.onehot = m.sem("onehot")
        self.transposed = m.sem("transposed")
        self.turned = m.sem("turned")
        self.at_node = m.sem("at_node")
        self.added_up = m.sem("added_up")
        self.product = m.sem("product")
        self.logit = m.sem("logit")
        self.logit16 = m.sem("logit16")
        self.spread = m.sem("spread")
        self.before = m.sem("before")
        self.highest = m.sem("highest")
        self.peak = m.sem("peak")
        self.peak16 = m.sem("peak16")
        self.drop = m.sem("drop")
        self.kept = m.sem("kept")
        self.fade = m.sem("fade")
        self.at_peak = m.sem("at_peak")
        self.argument = m.sem("argument")
        self.weight = m.sem("weight")
        self.summand = m.sem("summand")
        self.summed = m.sem("summed")
        self.faded = m.sem("faded")
        self.added = m.sem("added")
        self.ready = m.sem("ready")
        self.passed = m.sem("passed")
        self.distance = m.sem("distance")
        self.passed_dve = m.sem("passed_dve")


def edge_pass(nc, c, stage, order, table, width, acc, R, kind, H=1, C=0, node=None, value_c0=0, count=False, biggest=None, keys=None, query_table=None, buffer=None, posted=None):
    with ExitStack() as stack:
        m = Memory(nc, stack, stage)
        GS = 8
        guarded = kind in ("gat", "dot")
        weighted = kind != "sum"
        dot = kind == "dot"
        masked = guarded and H > 1
        halves = ((0, H // 2), (H // 2, H)) if masked else ((0, H),)
        HC = H * C
        OS = UN if weighted else 4
        index = m.sb("index", [P, GS, 2], I32)
        if dot:
            key = m.sb("key", [P, NSLOT + 2 * UN], I32)
            key_index = m.sb("key_index", [P, GS, 2], I32)
            rows = buffer[:, 0:GS * 2 * width].rearrange("p (g j n) -> p g j n", j=2, n=width)
            query = buffer[:, GS * 2 * width:GS * 2 * (width + HC)].rearrange("p (g j n) -> p g j n", j=2, n=HC)
        else:
            rows = m.sb("rows", [P, GS, 2, width])
        onehot = m.sb("onehot", [P, OS, 2, P])
        if weighted:
            turned = m.sb("turned", [P, 4, 2, P], BF16)
            logit = m.sb("logit", [P, 4, 2, H])
            summand = m.sb("summand", [P, 2, 2, R])
            product = m.sb("product", [P, 4, 2, HC if dot else H])
            ps_t = m.ps("ps_t", [P, 2, 256])
        if weighted and not dot:
            added_up = m.sb("added_up", [P, 2, H])
            ps_n = m.ps("ps_n", [P, 2, 256])
        if guarded:
            distance = m.sb("distance", [P, 2, P])
            away = m.sb("away", [P, 4, 2, P], BF16)
            logit16 = m.sb("logit16", [P, 2, 2, H], BF16)
            before = m.sb("before", [P, 2, H])
            peak = m.sb("peak", [P, 4, H])
            peak16 = m.sb("peak16", [P, 4, H], BF16)
            highest = m.sb("highest", [P, H])
            drop = m.sb("drop", [P, 2, H])
            fade = m.sb("fade", [P, 4, H])
            argument = m.sb("argument", [P, 2, 2, H])
            ps_m = m.ps("ps_m", [P, max(H, 2), 2, P])
            ps_e = m.ps("ps_e", [P, 2, 256])
        ps_u = m.ps("ps_u", [P, 2, 512])
        s = EdgeSemaphores(m)
        s_rows = [m.sem(f"rows{g}") for g in range(GS)]
        scatter = None if posted is None else Scatter(m, posted)
        per_group = 64 if dot else 32
        freed = s.summand if weighted else s.summed

        def arrived(eng, g):
            eng.wait_ge(s_rows[g.slot(GS)], g.turn(GS) * per_group + per_group)

        def steps(eng, stages, engine_type=None, with_first=None):
            most = max(lag for lag, _ in stages)

            def turn(i, k0=0, k1=UN, extra=None):
                windows = None
                if engine_type is not None:
                    _, windows = nc.values_load_multi_w_load_instructions(
                        order.window[0:1, bass.ds(i * UN, UN + LEAD)], engines=(engine_type,), min_val=0, max_val=NW - 1,
                        skip_runtime_bounds_check_because="a window's number is a count of windows, at most WIN")
                for k in range(k0, k1):
                    for lag, what in stages:
                        g = Group(i, k - lag, windows)
                        if g.exists():
                            what(g)
                    if extra is not None:
                        extra(Group(i, k))

            what, first = with_first if with_first is not None else (None, 1)
            turn(0, extra=what)
            if first > 1:
                with eng.Fori(1, first) as i:
                    turn(i, extra=what)
            with eng.Fori(first, NG // UN) as i:
                turn(i)
            turn(NG // UN, 0, most)

        with nc.Block() as block:
            if dot:
                @block.sync
                def _(sp):
                    sp.dma_start(key[:, 0:NSLOT], keys).then_inc(s.keys, 16)

            if scatter is not None:
                @block.sync
                def _(sp):
                    scatter.finish(sp)

            @block.gpsimd
            def _(pool):
                def gather(g):
                    wait(pool, freed, g.plus(1 - GS))
                    apart(pool, s.index, g.plus(1), s.passed)
                    for j in range(2):
                        if dot:
                            pool.indirect_dma_start(
                                out=query[:, g.slot(GS), j, :], out_offset=None, in_=query_table,
                                in_offset=bass.IndirectOffsetOnAxis(ap=key_index[:, g.slot(GS), j:j + 1], axis=0),
                            ).then_inc(s_rows[g.slot(GS)], 16)
                        pool.indirect_dma_start(
                            out=rows[:, g.slot(GS), j, :], out_offset=None, in_=table,
                            in_offset=bass.IndirectOffsetOnAxis(ap=index[:, g.slot(GS), j:j + 1], axis=0),
                        ).then_inc(s_rows[g.slot(GS)], 16)

                def multiply(g):
                    if not (isinstance(g.i, int) and g.plus(-3) <= 0):
                        apart(pool, s.logit, g.plus(-3), s.passed)
                    apart(pool, s_rows[g.slot(GS)], g.turn(GS) * per_group + per_group, s.passed)
                    pool.tensor_tensor(product[:, g.slot(4), :, :], query[:, g.slot(GS), :, :], rows[:, g.slot(GS), :, 0:HC], ALU.mult).then_inc(s.product, 1)

                def scatter_part(g):
                    h, n = g.k // (UN // 2), 2 * SB // UN
                    if g.k % (UN // 2) == 0:
                        scatter.stage(pool, g.i, h)
                    for j in range(g.k * n - h * SB, (g.k + 1) * n - h * SB):
                        scatter.send(pool, h, j)

                steps(pool, [(0, gather), (3, multiply)] if dot else [(0, gather)],
                      with_first=None if scatter is None else (scatter_part, TURNS))

            @block.tensor
            def _(pe):
                def transpose(g):
                    pe.wait_ge(s.onehot, g.plus(1))
                    wait(pe, s.turned, g.plus(0))
                    for j in range(2):
                        last = pe.transpose(ps_t[:, j, 0:P], onehot[:, g.slot(OS), j, :], c.ident[:, :])
                    last.then_inc(s.transposed, 1)

                def of_node(g):
                    pe.wait_ge(s.turned, g.plus(1))
                    wait(pe, s.added_up, g.plus(0))
                    for j in range(2):
                        last = pe.matmul(ps_n[:, j, 0:3 * H], turned[:, g.slot(4), j, :],
                                         node[:, bass.ds(g.window, 1), 0:3 * H].rearrange("p a n -> p (a n)"), start=True, stop=True)
                    last.then_inc(s.at_node, 1)

                def spread(g, part=0):
                    pe.wait_ge(s.logit16, g.plus(1))
                    if masked:
                        pe.wait_ge(s.turned, g.plus(1))
                        wait(pe, s.highest, g.plus(0) * 2 - 1 + part)
                    else:
                        wait(pe, s.peak, g.plus(0))
                    for h in range(*halves[part]):
                        if masked:
                            pe.matmul(ps_m[:, h, :, :], c.ident16[:, :], away[:, g.slot(4), :, :], start=True, stop=False)
                        for j in range(2):
                            last = pe.matmul(ps_m[:, h, j, :], bc(logit16[:, g.slot(2), j, h:h + 1], [P, P]), c.ident16[:, :],
                                             start=not masked, stop=not masked or j == 1)
                    last.then_inc(s.spread, 1)

                def spread_rest(g):
                    spread(g, 1)

                def of_peak(g):
                    pe.wait_ge(s.peak16, g.plus(1))
                    wait(pe, s.argument, g.plus(0))
                    for j in range(2):
                        last = pe.matmul(ps_e[:, j, 0:H], turned[:, g.slot(4), j, :], peak16[:, g.slot(4), :], start=True, stop=True)
                    last.then_inc(s.at_peak, 1)

                def sum_edges(g):
                    if weighted:
                        pe.wait_ge(s.summand, g.plus(1))
                    else:
                        pe.wait_ge(s.onehot, g.plus(1))
                        arrived(pe, g)
                    wait(pe, s.added, g.plus(-1))
                    for j in range(2):
                        rhs = summand[:, g.slot(2), j, :] if weighted else rows[:, g.slot(GS), j, 0:R]
                        last = pe.matmul(ps_u[:, g.slot(2), 0:R], onehot[:, g.slot(OS), j, :], rhs, start=j == 0, stop=j == 1)
                    last.then_inc(s.summed, 1)

                if dot:
                    steps(pe, [(3, spread), (4, of_peak), (3, spread_rest), (1, transpose), (5, sum_edges)])
                elif masked:
                    steps(pe, [(3, spread), (4, of_peak), (3, spread_rest), (2, of_node), (1, transpose), (5, sum_edges)], mybir.EngineType.PE)
                elif guarded:
                    steps(pe, [(1, transpose), (4, of_peak), (3, spread), (2, of_node), (5, sum_edges)], mybir.EngineType.PE)
                elif weighted:
                    steps(pe, [(1, transpose), (2, of_node), (4, sum_edges)], mybir.EngineType.PE)
                else:
                    steps(pe, [(0, sum_edges)])

            @block.scalar
            def _(act):
                def mark(g):
                    wait(act, s.onehot, g.plus(0))
                    for j in range(2):
                        act.activation(distance[:, j, :], c.lane[:, :], ACT.Abs, scale=-1.0,
                                       bias=order.place[:, bass.ds(g.plus(0) * 2 + j, 1)]).then_inc(s.distance, 1)
                    wait(act, s.summed, g.plus(1 - OS))
                    act.wait_ge(s.distance, g.plus(1) * 2)
                    act.activation(onehot[:, g.slot(OS), :, :], distance[:, :, :], ACT.Relu, scale=-1.0, bias=1.0).then_inc(s.onehot, 1)

                def weight(g):
                    w = summand[:, g.slot(2), :, 0:H * (C + 1)].rearrange("p j (h c) -> p j h c", h=H)[:, :, :, C]
                    wait(act, s.summed, g.plus(-1))
                    if guarded:
                        act.wait_ge(s.argument, g.plus(1))
                        act.activation(w, argument[:, g.slot(2), :, :], ACT.Exp).then_inc(s.weight, 1)
                    else:
                        act.wait_ge(s.logit, g.plus(1))
                        act.activation(w, logit[:, g.slot(4), :, :], ACT.Exp, scale=-1.0).then_inc(s.weight, 1)

                def fading(g):
                    act.wait_ge(s.drop, g.plus(1))
                    wait(act, s.added, g.plus(-3))
                    act.activation(fade[:, g.slot(4), :], drop[:, g.slot(2), :], ACT.Exp).then_inc(s.fade, 1)

                def copy(g):
                    act.wait_ge(s.transposed, g.plus(1))
                    wait(act, s.at_peak if guarded else s.at_node, g.plus(-3))
                    if guarded:
                        wait(act, s.peak, g.plus(-3))
                        act.activation(away[:, g.slot(4), :, :], ps_t[:, :, 0:P], ACT.Copy, scale=BIG, bias=-BIG)
                    act.activation(turned[:, g.slot(4), :, :], ps_t[:, :, 0:P], ACT.Copy).then_inc(s.turned, 1)

                if guarded:
                    steps(act, [(0, mark), (1, copy), (4, fading), (4, weight)])
                elif weighted:
                    steps(act, [(1, copy), (3, weight)])

            @block.vector
            def _(dve):
                def stage_index(g):
                    if dot:
                        dve.tensor_copy(key_index[:, g.slot(GS), :], key[:, bass.ds(g.plus(GS) * 2, 2)])
                    dve.tensor_copy(index[:, g.slot(GS), :], order.row[:, bass.ds(g.plus(GS) * 2, 2)]).then_inc(s.index, 1)

                def mark(g):
                    wait(dve, s.summed, g.plus(1 - OS))
                    dve.tensor_tensor(onehot[:, g.slot(OS), :, :], bc(c.lane[:, :].rearrange("p (j n) -> p j n", j=1), [P, 2, P]),
                                      bc(order.place[:, bass.ds(g.plus(0) * 2, 2)].rearrange("p (j n) -> p j n", n=1), [P, 2, P]),
                                      ALU.is_equal).then_inc(s.onehot, 1)

                def logits(g):
                    arrived(dve, g)
                    stage_index(g)
                    to = logit[:, g.slot(4), :, :]
                    if dot:
                        dve.wait_ge(s.product, g.plus(1))
                        dve.tensor_reduce(to, product[:, g.slot(4), :, :].rearrange("p j (h c) -> p j h c", h=H), AX.X, ALU.add).then_inc(s.logit, 1)
                    else:
                        dve.wait_ge(s.at_node, g.plus(1))
                        dve.tensor_reduce(added_up[:, :, :], ps_n[:, :, 0:3 * H].rearrange("p j (k h) -> p j h k", k=3), AX.X, ALU.add).then_inc(s.added_up, 1)
                        dve.wait_ge(s.added_up, g.plus(1))
                        dve.tensor_tensor(product[:, g.slot(4), :, :], added_up[:, :, :], rows[:, g.slot(GS), :, HC:HC + H], ALU.add).then_inc(s.product, 1)
                        dve.wait_ge(s.product, g.plus(1))
                        dve.scalar_tensor_tensor(to, product[:, g.slot(4), :, :], 0.2, product[:, g.slot(4), :, :], ALU.mult, ALU.max).then_inc(s.logit, 1)
                    if guarded:
                        dve.wait_ge(s.logit, g.plus(1))
                        dve.tensor_scalar(logit16[:, g.slot(2), :, :], to, CLIP, -CLIP, ALU.min, ALU.max).then_inc(s.logit16, 1)

                def maximum(g):
                    now = biggest[:, bass.ds(g.window, 1), 0:H].rearrange("p a h -> p (a h)")
                    wait(dve, s.kept, g.plus(0))
                    dve.tensor_scalar(before[:, g.slot(2), :], now, 1.0, None, ALU.mult).then_inc(s.before, 1)
                    if masked:
                        for part, (h0, h1) in enumerate(halves):
                            dve.wait_ge(s.spread, g.plus(0) * 2 + (part + 1))
                            dve.tensor_reduce(highest[:, h0:h1], ps_m[:, h0:h1, :, :].rearrange("p h j e -> p h (j e)"), AX.X, ALU.max).then_inc(s.highest, 1)
                        dve.wait_ge(s.before, g.plus(1))
                        dve.wait_ge(s.highest, g.plus(1) * 2)
                        last = dve.tensor_tensor(peak[:, g.slot(4), :], highest[:, :], before[:, g.slot(2), :], ALU.max)
                    else:
                        apart(dve, s.before, g.plus(1), s.passed_dve)
                        apart(dve, s.spread, g.plus(1), s.passed_dve)
                        last = dve.tensor_tensor_reduce(out=ps_m[:, 0, :, :], in0=ps_m[:, 0, :, :], in1=away[:, g.slot(4), :, :], scale=1.0,
                                                        scalar=before[:, g.slot(2), 0:1], op0=ALU.add, op1=ALU.max,
                                                        accum_out=peak[:, g.slot(4), 0:1])
                    last.then_inc(s.peak, 1)
                    dve.wait_ge(s.peak, g.plus(1))
                    dve.tensor_scalar(peak16[:, g.slot(4), :], peak[:, g.slot(4), :], 1.0, None, ALU.mult).then_inc(s.peak16, 1)
                    wait(dve, s.fade, g.plus(-1))
                    dve.tensor_tensor(drop[:, g.slot(2), :], before[:, g.slot(2), :], peak[:, g.slot(4), :], ALU.subtract).then_inc(s.drop, 1)
                    dve.tensor_scalar(now, peak[:, g.slot(4), :], 1.0, None, ALU.mult).then_inc(s.kept, 1)

                def subtract(g):
                    dve.wait_ge(s.at_peak, g.plus(1))
                    dve.tensor_tensor(argument[:, g.slot(2), :, :], logit[:, g.slot(4), :, :], ps_e[:, :, 0:H], ALU.subtract).then_inc(s.argument, 1)

                def weigh(g):
                    dve.wait_ge(s.weight, g.plus(1))
                    out = summand[:, g.slot(2), :, 0:H * (C + 1)].rearrange("p j (h c) -> p j h c", h=H)
                    dve.tensor_tensor(out[:, :, :, 0:C],
                                      rows[:, g.slot(GS), :, value_c0:value_c0 + HC].rearrange("p j (h c) -> p j h c", h=H),
                                      bc(out[:, :, :, C:C + 1], [P, 2, H, C]), ALU.mult).then_inc(s.summand, 1)

                def add(g):
                    wait(dve, s.added, g.plus(0))
                    at = g.window * R
                    mine = acc[:, bass.ds(at, R)]
                    if guarded and R == C + 1:
                        dve.wait_ge(s.summed, g.plus(1))
                        apart(dve, s.fade, g.plus(1), s.passed_dve)
                        dve.scalar_tensor_tensor(mine, mine, fade[:, g.slot(4), 0:1], ps_u[:, g.slot(2), 0:R], ALU.mult, ALU.add).then_inc(s.added, 1)
                        return
                    if guarded:
                        dve.wait_ge(s.fade, g.plus(1))
                        part = acc[:, bass.ds(at, H * (C + 1))].rearrange("p (h c) -> p h c", h=H)
                        dve.tensor_tensor(part, part, bc(fade[:, g.slot(4), :].rearrange("p (h c) -> p h c", c=1), [P, H, C + 1]), ALU.mult).then_inc(s.faded, 1)
                        dve.wait_ge(s.faded, g.plus(1))
                    dve.wait_ge(s.summed, g.plus(1))
                    dve.tensor_tensor(mine, mine, ps_u[:, g.slot(2), 0:R], ALU.add).then_inc(s.added, 1)
                    if not weighted:
                        stage_index(g)

                if dot:
                    dve.wait_ge(s.keys, 16)
                    dve.memset(key[:, NSLOT:], PAD_ROW).then_inc(s.ready, 1)
                    for k in range(GS):
                        dve.tensor_copy(key_index[:, k, :], key[:, 2 * k:2 * k + 2])
                for k in range(GS):
                    dve.tensor_copy(index[:, k, :], order.row[:, 2 * k:2 * k + 2]).then_inc(s.index, 1)
                if count:
                    dve.memset(summand[:, :, :, R - 1:R], 1.0).then_inc(s.ready, 1)
                    dve.wait_ge(s.ready, 1)
                if guarded:
                    steps(dve, [(3, logits), (4, maximum), (6, add), (4, subtract), (5, weigh)], mybir.EngineType.DVE)
                elif weighted:
                    steps(dve, [(4, weigh), (0, mark), (3, logits), (5, add)], mybir.EngineType.DVE)
                else:
                    steps(dve, [(0, mark), (2, add)], mybir.EngineType.DVE)



def all_windows(x, n=D):
    return x[:, 0:NW * n].rearrange("p (w n) -> p w n", n=n)


def keep_valid(link, dve, c, x):
    n = x.shape[2]
    link(dve.tensor_tensor(x[:, LAST:NW, :], x[:, LAST:NW, :], bc(c.valid[:, :].rearrange("p (w n) -> p w n", n=1), [P, 2, n]), ALU.mult))


def normalize(link, dve, c, x, scratch, small):
    mean, var = small[:, 0, :], small[:, 1, :]

    def wide(a):
        return bc(a.rearrange("p (w n) -> p w n", n=1), [P, NW, D])

    link(dve.tensor_reduce(mean, x, AX.X, ALU.add))
    link(dve.tensor_scalar(mean, mean, 1.0 / D, None, ALU.mult))
    halves = (slice(0, NW // 2), slice(NW // 2, NW))
    for half in halves:
        part = x[:, half, :]
        link.to_square(dve.tensor_tensor(part, part, bc(mean[:, half].rearrange("p (w n) -> p w n", n=1), [P, NW // 2, D]), ALU.subtract))
    for k, half in enumerate(halves):
        link.squared(k)
        link(dve.tensor_reduce(var[:, half], scratch[:, half, :], AX.X, ALU.add))
    link.asked(dve.tensor_scalar(var, var, 1.0 / D, EPS, ALU.mult, ALU.add))
    link(dve.tensor_tensor(x, x, wide(var), ALU.mult))
    keep_valid(link, dve, c, x)


def inverse_root(pool, minus_half, x):
    return pool.tensor_tensor(x, x, bc(minus_half, [P, x.shape[1]]), ALU.pow)


def on_vector(nc, c, stage, loads, work, root=None, squares=None):
    with ExitStack() as stack:
        m = Memory(nc, stack, stage)
        s_loaded, s_step, s_ask, s_root = (m.sem(x) for x in ("loaded", "step", "ask", "root"))
        s_centred, s_squared = m.sem("centred"), m.sem("squared")
        with nc.Block() as block:
            if squares is not None:
                @block.scalar
                def _(act):
                    to, frm = squares
                    n = NW * D // 2
                    for k in range(2):
                        act.wait_ge(s_centred, k + 1)
                        act.activation(to[:, k * n:(k + 1) * n], frm[:, k * n:(k + 1) * n], ACT.Square).then_inc(s_squared, 1)

            if root is not None:
                @block.gpsimd
                def _(pool):
                    pool.wait_ge(s_ask, 1)
                    inverse_root(pool, c.minus_half[:, :], root).then_inc(s_root, 1)

            @block.sync
            def _(sp):
                for to, frm in loads:
                    sp.dma_start(to, frm).then_inc(s_loaded, 16)

            @block.vector
            def _(dve):
                if loads:
                    dve.wait_ge(s_loaded, 16 * len(loads))
                link = Link(dve, s_step)

                def asked(ins):
                    ins.then_inc(s_ask, 1)
                    dve.wait_ge(s_root, 1)

                link.asked = asked
                link.to_square = lambda ins: ins.then_inc(s_centred, 1)
                link.squared = lambda k: dve.wait_ge(s_squared, k + 1)
                work(link, dve)


def row(v):
    return v.rearrange("(a n) -> a n", a=1)


def spread_row(v, n):
    return row(v).to_broadcast([P, n]) if len(v.shape) == 1 else v.to_broadcast([P, n])


def fold(link, dve, w, c0, a, H, C, to, scratch):
    n = H * C
    for k in range(2):
        link(dve.tensor_tensor(scratch[:, 0:n], w[:, k, c0:c0 + n], a, ALU.mult))
        link(dve.tensor_reduce(w[:, k, to:to + H], scratch[:, 0:n].rearrange("p (h c) -> p h c", h=H), AX.X, ALU.add))


def by_chunk(w):
    return w.rearrange("(k p) n -> p k n", p=P)


class Keep:
    pass


def gnn_kernel(nc, x, src, dst,
               a_w1, a_as1, a_ad1, a_b1, a_w2, a_as2, a_ad2, a_b2, a_wf, a_bf,
               b_w1, b_a1, b_w2, b_a2,
               t_wq, t_bq, t_wk, t_bk, t_wv, t_bv, t_wo, t_bo,
               g_w1, g_b1, g_g1, g_be1, g_w2, g_b2, g_g2, g_be2, g_wfc, g_bfc, out):
    records = [nc.dram_tensor(f"records_{n}", [P, NSLOT, 2], I32, kind="Internal").ap() for n in ("dst", "src")]
    tables = {n: nc.dram_tensor(f"table_{n}", [NPAD, n], F32, kind="Internal").ap() for n in (264, 66, 258, 256, 512, 128, 64)}

    with ExitStack() as stack:
        m = Memory(nc, stack, "all")
        c = Keep()
        constants(nc, m, c)
        order = Keep()
        order.row = m.sb("row", [P, NSLOT + 2 * UN], I32)
        order.place = m.sb("place", [P, NSLOT])
        order.window = m.sb("window", [P, WT], I32)
        kept = {n: (nc.dram_tensor(f"kept_row_{n}", [P, NSLOT + 2 * UN], I32, kind="Internal").ap(),
                    nc.dram_tensor(f"kept_place_{n}", [P, NSLOT], F32, kind="Internal").ap(),
                    nc.dram_tensor(f"kept_window_{n}", [P, WT], I32, kind="Internal").ap()) for n in ("dst", "src")}

        def move_order(name, load):
            s_moved = m.sem(f"moved_{name}_{load}")
            with nc.Block() as block:
                @block.sync
                def _(sp):
                    for d, t in zip(kept[name], (order.row, order.place, order.window)):
                        to, frm = (t[:, :], d) if load else (d, t[:, :])
                        sp.dma_start(to, frm).then_inc(s_moved, 16)
                    sp.wait_ge(s_moved, 48)

        acc = m.sb("acc", [P, NW * 264])
        X = m.sb("X", [P, NW * D])
        Y = m.sb("Y", [P, NW * D])
        nodes = m.sb("nodes", [P, NW, 8])
        biggest = m.sb("biggest", [P, NW, 8])
        rounded = m.sb("rounded", [P, NW, 4], BF16)
        fresh = m.sb("fresh", [P, NW, 8])
        node_parts = m.sb("node_parts", [P, NW, 3 * 4], BF16)
        small = m.sb("small", [P, 2, NW])
        degree = m.sb("degree", [P, NW])
        x3, y3 = all_windows(X), all_windows(Y)

        keys = nc.dram_tensor("keys", [P, NSLOT], I32, kind="Internal").ap()
        in_y = Region(Y)
        by_dst, by_src = Posted(in_y, records[0]), Posted(in_y, records[1])
        sort_edges(nc, c, src, dst, by_dst, by_src, Region(acc), order, kept["dst"], x3[:, LAST:NW, :], [
            (x3[:, 0:LAST, :], x[0:LAST * P, :].rearrange("(w p) n -> p w n", p=P)),
            (X[0:VALID, LAST * D:(LAST + 1) * D], x[LAST * P:N, :])])

        def wide(a, *shape):
            return bc(a, [P, NW, *shape])

        def at(t, w, n, c0=0, c1=None):
            return t[:, bass.ds(w * n + c0, (n if c1 is None else c1) - c0)]

        with ExitStack() as st:
            mm = Memory(nc, st, "a1")
            W = mm.sb("W", [P, 2, 264])
            avec = mm.sb("avec", [P, 2, 256])
            tmp = mm.sb("tmp", [P, 256])

            def work(link, dve):
                fold(link, dve, W, 0, avec[:, 0, :], 4, 64, 256, tmp)
                fold(link, dve, W, 0, avec[:, 1, :], 4, 64, 260, tmp)

            on_vector(nc, c, "a1w", [
                (W[:, :, 0:256], by_chunk(a_w1)),
                (avec[:, 0, :], spread_row(a_as1.rearrange("h c -> (h c)"), 256)),
                (avec[:, 1, :], spread_row(a_ad1.rearrange("h c -> (h c)"), 256)),
            ], work)
            R = 4 * 65 + 1

            def drain_v(dve, ps, w, tile):
                dve.tensor_copy(at(acc, w, R, 0, 260).rearrange("p (h c) -> p h c", h=4)[:, :, 0:64], ps[:, 0:256].rearrange("p (h c) -> p h c", h=4))
                return dve.tensor_copy(nodes[:, bass.ds(w, 1), :].rearrange("p a n -> p (a n)"), ps[:, 256:264])

            def drain_a(act, ps, w, tile):
                return act.activation(tile[:, 0:264], ps[:, 0:264], ACT.Copy)

            linear(nc, c, "a1l", [(x3, 0, P), (x3, P, P)], [W[:, 0, :], W[:, 1, :]], None, 264, drain_v, drain_a, [(tables[264], 0, 264)], "a")

        def split_nodes(link, dve, c0, H):
            rest = nodes[:, :, c0:c0 + H]
            for k in range(3):
                part = node_parts[:, :, k * H:(k + 1) * H]
                link(dve.tensor_scalar(part, rest, 1.0, None, ALU.mult))
                if k < 2:
                    link(dve.tensor_tensor(rest, rest, part, ALU.subtract))

        def self_loops(tag, H, C, R, ones):
            with ExitStack() as st:
                mm = Memory(nc, st, tag)
                own, excess = fresh[:, :, 0:H], fresh[:, :, 4:4 + H]
                s_step, s_excess, s_weights = mm.sem("step"), mm.sem("excess"), mm.sem("weights")
                a = acc[:, 0:NW * R].rearrange("p (w r) -> p w r", r=R)
                with nc.Block() as block:
                    @block.scalar
                    def _(act):
                        act.wait_ge(s_excess, 1)
                        act.activation(excess, excess, ACT.Exp).then_inc(s_weights, 1)

                    @block.vector
                    def _(dve):
                        link = Link(dve, s_step)
                        link(dve.tensor_tensor(own, nodes[:, :, 0:H], nodes[:, :, H:2 * H], ALU.add))
                        link(dve.scalar_tensor_tensor(own, own, 0.2, own, ALU.mult, ALU.max))
                        link(dve.tensor_scalar(rounded[:, :, 0:H], own, 1.0, None, ALU.mult))
                        link(dve.tensor_scalar(biggest[:, :, 0:H], rounded[:, :, 0:H], 1.0, None, ALU.mult))
                        dve.tensor_tensor(excess, own, biggest[:, :, 0:H], ALU.subtract).then_inc(s_excess, 1)
                        split_nodes(link, dve, H, H)
                        link(dve.memset(a[:, :, 0:H * (C + 1)].rearrange("p w (h c) -> p w h c", h=H)[:, :, :, C], 1.0))
                        if ones:
                            link(dve.memset(a[:, :, R - 1:R], 1.0))
                        dve.wait_ge(s_weights, 1)
                        for h in range(H):
                            part = a[:, :, h * (C + 1):(h + 1) * (C + 1)]
                            link(dve.tensor_tensor(part, part, wide(excess[:, :, h:h + 1], C + 1), ALU.mult))

        self_loops("a1s", 4, 64, R, True)
        edge_pass(nc, c, "a1e", order, tables[264], 264, acc, R, "gat", H=4, C=64, node=node_parts, count=True, biggest=biggest, posted=by_src)

        with ExitStack() as st:
            mm = Memory(nc, st, "src_tables")
            s_back, s_step, s_kept = mm.sem("back"), mm.sem("step"), mm.sem("kept")
            back = in_y.take(P, NSLOT * 2, dt=I32).rearrange("p (s r) -> p s r", r=2)
            made = (in_y.take(P, NSLOT + 2 * UN, dt=I32), in_y.take(P, NSLOT), in_y.take(P, WT, dt=I32), in_y.take(P, NSLOT, dt=I32))
            with nc.Block() as block:
                @block.sync
                def _(sp):
                    sp.dma_start(back, by_src.records).then_inc(s_back, 16)
                    sp.wait_ge(s_step, 8)
                    for d, t in zip(kept["src"] + (keys,), made):
                        sp.dma_start(d, t).then_inc(s_kept, 16)
                    sp.wait_ge(s_kept, 64)

                @block.vector
                def _(dve):
                    dve.wait_ge(s_back, 16)
                    edge_tables(dve, s_step, back, by_src.windowf, *made)

        with ExitStack() as st:
            mm = Memory(nc, st, "a2")
            W = mm.sb("W", [P, 2, 66])
            avec = mm.sb("avec", [P, 2, 64])
            tmp = mm.sb("tmp", [P, 256])
            bias = mm.sb("bias", [P, 256])

            def work(link, dve):
                a = acc[:, 0:NW * R].rearrange("p (w r) -> p w r", r=R)
                link(dve.tensor_copy(degree[:, :], a[:, :, R - 1]))
                for h in range(4):
                    z = a[:, :, h * 65 + 64:h * 65 + 65]
                    link(dve.reciprocal(z, z))
                    link(dve.tensor_tensor(y3[:, :, h * 64:(h + 1) * 64], a[:, :, h * 65:h * 65 + 64], wide(z, 64), ALU.mult))
                link(dve.tensor_tensor(y3, y3, bc(bias[:, :].rearrange("p (w n) -> p w n", w=1), [P, NW, 256]), ALU.add))
                link(dve.tensor_scalar(y3, y3, 0.0, None, ALU.max))
                keep_valid(link, dve, c, y3)
                fold(link, dve, W, 0, avec[:, 0, :], 1, 64, 64, tmp)
                fold(link, dve, W, 0, avec[:, 1, :], 1, 64, 65, tmp)

            on_vector(nc, c, "a2w", [
                (W[:, :, 0:64], by_chunk(a_w2)), (bias[:, :], spread_row(a_b1, 256)),
                (avec[:, 0, :], spread_row(a_as2, 64)), (avec[:, 1, :], spread_row(a_ad2, 64)),
            ], work)

            def drain_v2(dve, ps, w, tile):
                dve.tensor_copy(at(acc, w, 65, 0, 64), ps[:, 0:64])
                return dve.tensor_copy(nodes[:, bass.ds(w, 1), 0:2].rearrange("p a n -> p (a n)"), ps[:, 64:66])

            def drain_a2(act, ps, w, tile):
                return act.activation(tile[:, 0:66], ps[:, 0:66], ACT.Copy)

            linear(nc, c, "a2l", [(y3, 0, P), (y3, P, P)], [W[:, 0, :], W[:, 1, :]], None, 66, drain_v2, drain_a2, [(tables[66], 0, 66)], "a")
        self_loops("a2s", 1, 64, 65, False)
        edge_pass(nc, c, "a2e", order, tables[66], 66, acc, 65, "gat", H=1, C=64, node=node_parts, biggest=biggest)

        def add_to_x(dve, ps, w, tile):
            return dve.tensor_tensor(at(X, w, D), at(X, w, D), ps[:, 0:D], ALU.add)

        with ExitStack() as st:
            mm = Memory(nc, st, "af")
            W = mm.sb("W", [P, 256])
            brow = mm.sb("brow", [1, 256])
            bias = mm.sb("bias", [P, 64])
            h64 = all_windows(Y, 64)

            def work(link, dve):
                a = acc[:, 0:NW * 65].rearrange("p (w r) -> p w r", r=65)
                link(dve.reciprocal(a[:, :, 64:65], a[:, :, 64:65]))
                link(dve.tensor_tensor(h64, a[:, :, 0:64], wide(a[:, :, 64:65], 64), ALU.mult))
                link(dve.tensor_tensor(h64, h64, bc(bias[:, :].rearrange("p (w n) -> p w n", w=1), [P, NW, 64]), ALU.add))

            on_vector(nc, c, "afw", [(W[0:64, :], a_wf), (brow[:, :], row(a_bf)), (bias[:, :], spread_row(a_b2, 64))], work)
            linear(nc, c, "afl", [(h64, 0, 64)], [W], brow, 256, add_to_x, None)

        with ExitStack() as st:
            mm = Memory(nc, st, "b")
            W = mm.sb("W", [P, 2, 260])
            avec = mm.sb("avec", [P, 4, 128])
            tmp = mm.sb("tmp", [P, 256])
            R = 2 * 129

            def work(link, dve):
                normalize(link, dve, c, x3, y3, small)
                for h in range(2):
                    fold(link, dve, W, 128 * h, avec[:, 2 * h + 1, :], 1, 128, 256 + h, tmp)
                    fold(link, dve, W, 128 * h, avec[:, 2 * h, :], 1, 128, 258 + h, tmp)
                link(dve.memset(acc[:, 0:NW * R], 0.0))
                for h in range(2):
                    z = acc[:, 0:NW * R].rearrange("p (w r) -> p w r", r=R)[:, LAST:NW, h * 129 + 128]
                    link(dve.tensor_scalar(z, c.valid[:, :], -1.0, 1.0, ALU.mult, ALU.add))

            on_vector(nc, c, "bw", [
                (W[:, :, 0:128], by_chunk(b_w1)), (W[:, :, 128:256], by_chunk(b_w2)),
            ] + [(avec[:, 2 * h + k, :], spread_row(a[:, 128 * k:128 * (k + 1)], 128))
                 for h, a in enumerate((b_a1, b_a2)) for k in range(2)], work, small[:, 1, :], (Y, X))

            def drain_vb(dve, ps, w, tile):
                return dve.tensor_copy(nodes[:, bass.ds(w, 1), 0:2].rearrange("p a n -> p (a n)"), ps[:, 258:260])

            def drain_ab(act, ps, w, tile):
                return act.activation(tile[:, 0:258], ps[:, 0:258], ACT.Copy)

            linear(nc, c, "bl", [(x3, 0, P), (x3, P, P)], [W[:, 0, :], W[:, 1, :]], None, 260, drain_vb, drain_ab, [(tables[258], 0, 258)], "a")
        on_vector(nc, c, "bs", [], lambda link, dve: split_nodes(link, dve, 0, 2))
        move_order("src", True)
        edge_pass(nc, c, "be", order, tables[258], 258, acc, R, "neg", H=2, C=128, node=node_parts)

        with ExitStack() as st:
            mm = Memory(nc, st, "t")
            W = mm.sb("W", [P, 2, 768])
            bias = mm.sb("bias", [P, 768])

            def work(link, dve):
                a = acc[:, 0:NW * R].rearrange("p (w r) -> p w r", r=R)
                for h in range(2):
                    z = a[:, :, h * 129 + 128:h * 129 + 129]
                    link(dve.reciprocal(z, z))
                    link(dve.tensor_tensor(y3[:, :, h * 128:(h + 1) * 128], a[:, :, h * 129:h * 129 + 128], wide(z, 128), ALU.mult))
                low = acc[:, 0:NW * D].rearrange("p (w n) -> p w n", n=D)
                link(dve.tensor_scalar(low, y3, 0.0, None, ALU.min))
                link(dve.tensor_scalar(bias[:, 0:256], bias[:, 0:256], 32.0 ** -0.5, None, ALU.mult))

            on_vector(nc, c, "tw", [
                (W[:, :, 0:256], by_chunk(t_wq)), (W[:, :, 256:512], by_chunk(t_wk)), (W[:, :, 512:768], by_chunk(t_wv)),
                (bias[:, 0:256], spread_row(t_bq, 256)), (bias[:, 256:512], spread_row(t_bk, 256)), (bias[:, 512:768], spread_row(t_bv, 256)),
            ], work)
            s_exp = mm.sem("exp")
            with nc.Block() as block:
                @block.scalar
                def _(act):
                    act.activation(acc[:, 0:NW * D], acc[:, 0:NW * D], ACT.Exp).then_inc(s_exp, 1)

            def work(link, dve):
                low = acc[:, 0:NW * D].rearrange("p (w n) -> p w n", n=D)
                link(dve.scalar_tensor_tensor(y3, y3, 0.0, low, ALU.max, ALU.add))
                link(dve.scalar_tensor_tensor(x3, y3, -1.0, x3, ALU.add, ALU.add))
                normalize(link, dve, c, x3, y3, small)
                link(dve.memset(acc[:, :], 0.0))
                link(dve.memset(biggest[:, :, :], -BIG))

            on_vector(nc, c, "tx", [], work, small[:, 1, :], (Y, X))

            def drain_vt(dve, ps, w, tile):
                dve.scalar_tensor_tensor(tile[:, 0:256], ps[:, 0:256], 32.0 ** -0.5, bias[:, 0:256], ALU.mult, ALU.add)
                return dve.tensor_tensor(tile[:, 256:768], ps[:, 256:768], bias[:, 256:768], ALU.add)

            linear(nc, c, "tl", [(x3, 0, P), (x3, P, P)], [W[:, 0, :], W[:, 1, :]], None, 768, drain_vt, None,
                   [(tables[256], 0, 256), (tables[512], 256, 512)], "v")
            s_zero = mm.sem("zero")
            with nc.Block() as block:
                @block.sync
                def _(sp):
                    sp.dma_start(tables[256][PAD_ROW:PAD_ROW + 1, :], acc[0:1, 0:256]).then_inc(s_zero, 16)
                    sp.wait_ge(s_zero, 16)
        R = 8 * 33
        edge_pass(nc, c, "te", order, tables[512], 512, acc, R, "dot", H=8, C=32, value_c0=256, biggest=biggest,
                  keys=keys, query_table=tables[256], buffer=Y)

        with ExitStack() as st:
            mm = Memory(nc, st, "to")
            W = mm.sb("W", [P, 2, 256])
            brow = mm.sb("brow", [1, 256])

            def work(link, dve):
                a = acc[:, 0:NW * R].rearrange("p (w r) -> p w r", r=R)
                for h in range(8):
                    z = a[:, :, h * 33 + 32:h * 33 + 33]
                    link(dve.tensor_scalar(z, z, 1e-37, None, ALU.max))
                    link(dve.reciprocal(z, z))
                    link(dve.tensor_tensor(y3[:, :, h * 32:(h + 1) * 32], a[:, :, h * 33:h * 33 + 32], wide(z, 32), ALU.mult))

            on_vector(nc, c, "tow", [(W[:, :, :], by_chunk(t_wo)), (brow[:, :], row(t_bo))], work)
            linear(nc, c, "tol", [(y3, 0, P), (y3, P, P)], [W[:, 0, :], W[:, 1, :]], brow, 256, add_to_x, None)

        move_order("dst", True)

        f1, f2 = Y[:, 0:NW * 128], Y[:, NW * 128:NW * 192]
        f1w = f1.rearrange("p (w n) -> p w n", n=128)
        f2w = f2.rearrange("p (w n) -> p w n", n=64)

        def dinv(n):
            return bc(small[:, 1, :].rearrange("p (w n) -> p w n", n=1), [P, NW, n])

        def convolve(tag, sources, weights, n):
            def drain_v(dve, ps, w, tile):
                dve.tensor_tensor(tile[:, 0:n], ps[:, 0:n], bc(small[:, 1, bass.ds(w, 1)], [P, n]), ALU.mult)
                return dve.tensor_tensor(at(acc, w, n), ps[:, 0:n], bc(small[:, 1, bass.ds(w, 1)], [P, n]), ALU.mult)

            linear(nc, c, tag + "l", sources, weights, None, n, drain_v, None, [(tables[n], 0, n)], "v")
            edge_pass(nc, c, tag + "e", order, tables[n], n, acc, n, "sum")

        def batch_norm(tag, n, to, b, gamma, beta):
            with ExitStack() as st:
                mm = Memory(nc, st, tag)
                vecs = mm.sb("vecs", [P, 3, n])
                part = mm.sb("part", [P, n])
                mean = mm.sb("mean", [P, n])
                scale = mm.sb("scale", [P, n])
                ps = mm.ps("ps", [P, 2, 512])
                s_loaded, s_step, s_part, s_sum, s_ask, s_root = (mm.sem(x) for x in ("loaded", "step", "part", "sum", "ask", "root"))
                a = acc[:, 0:NW * n].rearrange("p (w n) -> p w n", n=n)
                down = acc[:, 0:NW * n].rearrange("p (w n) -> p n w", n=n)
                sq = acc[:, NW * n:2 * NW * n].rearrange("p (w n) -> p w n", n=n)

                def rows(v):
                    return bc(v.rearrange("p (w n) -> p w n", w=1), [P, NW, n])

                with nc.Block() as block:
                    @block.sync
                    def _(sp):
                        for k, v in enumerate((b, gamma, beta)):
                            sp.dma_start(vecs[:, k, :], spread_row(v, n)).then_inc(s_loaded, 16)

                    @block.gpsimd
                    def _(pool):
                        pool.wait_ge(s_ask, 1)
                        inverse_root(pool, c.minus_half[:, :], scale[:, :]).then_inc(s_root, 1)

                    @block.tensor
                    def _(pe):
                        for k in range(2):
                            pe.wait_ge(s_part, k + 1)
                            pe.matmul(ps[:, k, 0:n], c.ones[:, :], part[:, :], start=True, stop=True).then_inc(s_sum, 1)

                    @block.vector
                    def _(dve):
                        link = Link(dve, s_step)
                        dve.wait_ge(s_loaded, 48)
                        link(dve.tensor_tensor(a, a, dinv(n), ALU.mult))
                        link(dve.tensor_tensor(a, a, rows(vecs[:, 0, :]), ALU.add))
                        keep_valid(link, dve, c, a)
                        dve.tensor_reduce(part[:, :], down, AX.X, ALU.add).then_inc(s_part, 1)
                        dve.wait_ge(s_sum, 1)
                        link(dve.tensor_scalar(mean[:, :], ps[:, 0, 0:n], 1.0 / N, None, ALU.mult))
                        link(dve.tensor_tensor(a, a, rows(mean[:, :]), ALU.subtract))
                        keep_valid(link, dve, c, a)
                        link(dve.tensor_tensor(to, a, a, ALU.mult))
                        dve.tensor_reduce(part[:, :], to.rearrange("p w n -> p n w"), AX.X, ALU.add).then_inc(s_part, 1)
                        dve.wait_ge(s_sum, 2)
                        dve.tensor_scalar(scale[:, :], ps[:, 1, 0:n], 1.0 / N, EPS, ALU.mult, ALU.add).then_inc(s_ask, 1)
                        dve.wait_ge(s_root, 1)
                        link(dve.tensor_tensor(scale[:, :], scale[:, :], vecs[:, 1, :], ALU.mult))
                        link(dve.tensor_tensor(a, a, rows(scale[:, :]), ALU.mult))
                        link(dve.tensor_tensor(a, a, rows(vecs[:, 2, :]), ALU.add))
                        link(dve.tensor_scalar(to, a, 0.0, None, ALU.max))

        with ExitStack() as st:
            mm = Memory(nc, st, "g1")
            W = mm.sb("W", [P, 2, 128])

            def work(link, dve):
                normalize(link, dve, c, x3, y3, small)

            def degrees(link, dve):
                link.asked(dve.tensor_copy(small[:, 1, :], degree[:, :]))

            on_vector(nc, c, "g1w", [(W[:, :, :], by_chunk(g_w1))], work, small[:, 1, :], (Y, X))
            on_vector(nc, c, "g1d", [], degrees, small[:, 1, :])
            convolve("g1", [(x3, 0, P), (x3, P, P)], [W[:, 0, :], W[:, 1, :]], 128)
            batch_norm("n1", 128, f1w, g_b1, g_g1, g_be1)
        with ExitStack() as st:
            mm = Memory(nc, st, "g2")
            W = mm.sb("W", [P, 64])
            on_vector(nc, c, "g2w", [(W[:, :], g_w2)], lambda link, dve: None)
            convolve("g2", [(f1w, 0, P)], [W], 64)
            batch_norm("n2", 64, f2w, g_b2, g_g2, g_be2)
        with ExitStack() as st:
            mm = Memory(nc, st, "gf")
            W = mm.sb("W", [P, 4, 256])
            brow = mm.sb("brow", [1, 256])
            on_vector(nc, c, "gfw", [(W[:, 0:3, :], by_chunk(g_wfc[0:384, :])), (W[0:64, 3, :], g_wfc[384:448, :]),
                                  (brow[:, :], row(g_bfc))], lambda link, dve: None)

            def drain_vf(dve, ps, w, tile):
                return dve.scalar_tensor_tensor(at(X, w, D), ps[:, 0:D], 0.0, at(X, w, D), ALU.max, ALU.add)

            linear(nc, c, "gfl", [(x3, 0, P), (x3, P, P), (f1w, 0, P), (f2w, 0, 64)], [W[:, k, :] for k in range(4)], brow, 256, drain_vf, None)
            on_vector(nc, c, "last", [], lambda link, dve: normalize(link, dve, c, x3, y3, small), small[:, 1, :], (Y, X))
        s_out = m.sem("out")
        with nc.Block() as block:
            @block.sync
            def _(sp):
                sp.dma_start(out[0:LAST * P, :].rearrange("(w p) n -> p w n", p=P), x3[:, 0:LAST, :]).then_inc(s_out, 16)
                sp.dma_start(out[LAST * P:N, :], X[0:VALID, LAST * D:(LAST + 1) * D]).then_inc(s_out, 16)
                sp.wait_ge(s_out, 32)


_INS = ["x", "src", "dst", "L0_gnn_W1", "L0_gnn_att_src1", "L0_gnn_att_dst1", "L0_gnn_b1", "L0_gnn_W2",
        "L0_gnn_att_src2", "L0_gnn_att_dst2", "L0_gnn_b2", "L0_gnn_Wf", "L0_gnn_bf", "L1_gnn_W1", "L1_gnn_a1",
        "L1_gnn_W2", "L1_gnn_a2", "L2_gnn_Wq", "L2_gnn_bq", "L2_gnn_Wk", "L2_gnn_bk", "L2_gnn_Wv", "L2_gnn_bv",
        "L2_gnn_Wo", "L2_gnn_bo", "L3_gnn_W1", "L3_gnn_b1", "L3_gnn_g1", "L3_gnn_be1", "L3_gnn_W2", "L3_gnn_b2",
        "L3_gnn_g2", "L3_gnn_be2", "L3_gnn_Wfc", "L3_gnn_bfc"]


def kernel(**inputs):
    import numpy as np
    import concourse.bacc as bacc
    from concourse.bass_utils import run_bass_kernel_spmd

    nc = bacc.Bacc("TRN2", target_bir_lowering=False, num_devices=1)
    arrays, args = {}, []
    for name in _INS:
        a = np.ascontiguousarray(inputs[name])
        arrays[f"in_{name}"] = a
        args.append(nc.dram_tensor(f"in_{name}", a.shape, mybir.dt.from_np(a.dtype), kind="ExternalInput").ap())
    out = nc.dram_tensor("out", (N, D), F32, kind="ExternalOutput").ap()
    gnn_kernel(nc, *args, out)
    r = run_bass_kernel_spmd(nc, [arrays], core_ids=[0])
    return r.results[0]["out"]
```
